# Optimizing a Trainium2 kernel written in Bass

```python
import numpy as np
import jax
import jax.numpy as jnp

def _softmax(x, axis=-1):
    return jax.nn.softmax(x, axis=axis)

def _gelu(x):
    return jax.nn.gelu(x, approximate=True)

def _silu(x):
    return jax.nn.silu(x)

def _sigmoid(x):
    return jax.nn.sigmoid(x)

def _layernorm(x, axis=-1, eps=1e-05):
    m = jnp.mean(x, axis=axis, keepdims=True)
    v = jnp.var(x, axis=axis, keepdims=True)
    return (x - m) / jnp.sqrt(v + eps)

def _scatter_add(tgt, idx, src, axis=0):
    return tgt.at[idx].add(src)

def _segment_sum(src, seg, n):
    return jax.ops.segment_sum(src, seg, n)
kernel_name = 'mk_vit_tower_d2_tok_img768_r4_529119'

def setup_inputs(seed: int=0):
    np.random.seed(seed)
    _w = jnp.asarray

    def _rec_inputs():
        import jax
        import jax.numpy as jnp
        _rk = jax.random.key(seed)
        x = -0.000596345 + 1.00056 * jax.random.normal(jax.random.fold_in(_rk, 1), (4, 3, 64, 64), jnp.float32)
        return x
    x = _rec_inputs()

    def _L0_tok_setup():
        import jax, jax.numpy as jnp
        import numpy as np
        B = 16
        IMG = 64
        CH = 3
        EMBED = 64
        GP = 16
        PRE = [1, 2, 4]
        N_LEVELS = 3
        FUSED = EMBED * N_LEVELS

        def hilbert_flat_indices(n):
            t = np.arange(n * n, dtype=np.int64)
            x = np.zeros(n * n, dtype=np.int64)
            y = np.zeros(n * n, dtype=np.int64)
            s = 1
            while s < n:
                rx = 1 & t // 2
                ry = 1 & (t ^ rx)
                swap = ry == 0
                flip = swap & (rx == 1)
                x = np.where(flip, s - 1 - x, x)
                y = np.where(flip, s - 1 - y, y)
                x2 = np.where(swap, y, x)
                y2 = np.where(swap, x, y)
                x, y = (x2, y2)
                x = x + s * rx
                y = y + s * ry
                t = t // 4
                s *= 2
            return y * n + x

        def _level(x, idx, W, b, p, gp):
            Bsz, C, H, _ = x.shape
            h = H // p
            t = x.reshape(Bsz, C, h, p, h, p).transpose(0, 2, 4, 3, 5, 1).reshape(Bsz, h * h, p * p * C)
            t = t[:, idx]
            t = t.reshape(Bsz, h * h // gp, gp * p * p * C)
            return t @ W.T + b

        def _interp_linear(x, n_out):
            L = x.shape[1]
            pos = (jnp.arange(n_out, dtype=jnp.float32) + 0.5) * (L / n_out) - 0.5
            pos = jnp.clip(pos, 0.0, L - 1)
            i0 = jnp.floor(pos).astype(jnp.int32)
            i1 = jnp.minimum(i0 + 1, L - 1)
            w = (pos - i0).astype(x.dtype)
            return x[:, i0] * (1.0 - w)[None, :, None] + x[:, i1] * w[None, :, None]
        key = jax.random.key(seed)
        ks = jax.random.split(key, 9)
        inp = {'x': jax.random.normal(ks[0], (B, CH, IMG, IMG), jnp.float32)}
        for i, p in enumerate(PRE):
            din = CH * p * p * GP
            inp[f'W{i}'] = jax.random.normal(ks[1 + 2 * i], (EMBED, din), jnp.float32) * din ** (-0.5)
            inp[f'b{i}'] = jax.random.normal(ks[2 + 2 * i], (EMBED,), jnp.float32) * 0.02
        inp['Wf'] = jax.random.normal(ks[7], (FUSED, FUSED), jnp.float32) * FUSED ** (-0.5)
        inp['bf'] = jax.random.normal(ks[8], (FUSED,), jnp.float32) * 0.02
        for i, p in enumerate(PRE):
            inp[f'idx{i}'] = jnp.asarray(hilbert_flat_indices(IMG // p), jnp.int32)
        return inp
    _L0_tok_all = _L0_tok_setup()
    _L0_tok_in = {k: v for k, v in _L0_tok_all.items() if k in ('W0', 'b0', 'W1', 'b1', 'W2', 'b2', 'Wf', 'bf', 'idx0', 'idx1', 'idx2')}
    del _L0_tok_all

    def _L0_attn_setup():
        import jax, jax.numpy as jnp
        import numpy as np
        TAU = 2.0
        BN_EPS = 1e-05
        SG_ALPHA = 2.0

        @jax.custom_vjp
        def spike(u):
            return (u >= 0).astype(u.dtype)

        def _spike_fwd(u):
            return (spike(u), u)

        def _spike_bwd(u, g):
            sg = SG_ALPHA / 2.0 / (1.0 + (jnp.pi / 2.0 * SG_ALPHA * u) ** 2)
            return (g * sg,)
        spike.defvjp(_spike_fwd, _spike_bwd)

        def lif(x, v_th):
            return spike(x / TAU - v_th)

        def bn_eval(x, gamma, beta, mean, var):
            inv = gamma / jnp.sqrt(var + BN_EPS)
            return x * inv + (beta - mean * inv)
        key = jax.random.key(seed)
        ks = jax.random.split(key, 7)
        B, N, D = (2, 512, 192)
        x = jax.random.normal(ks[0], (B, N, D), dtype=jnp.float32)
        W = jax.random.normal(ks[1], (4, D, D), dtype=jnp.float32) * 0.02
        b = jnp.zeros((4, D), dtype=jnp.float32)
        bn_gamma = jax.random.uniform(ks[2], (4, D), dtype=jnp.float32, minval=0.5, maxval=1.5)
        bn_beta = jax.random.normal(ks[3], (4, D), dtype=jnp.float32) * 0.1
        bn_mean = jax.random.normal(ks[4], (4, D), dtype=jnp.float32) * 0.1
        bn_var = jax.random.uniform(ks[5], (4, D), dtype=jnp.float32, minval=0.5, maxval=1.5)
        return {'x': x, 'W': W, 'b': b, 'bn_gamma': bn_gamma, 'bn_beta': bn_beta, 'bn_mean': bn_mean, 'bn_var': bn_var}
    _L0_attn_all = _L0_attn_setup()
    _L0_attn_in = {k: v for k, v in _L0_attn_all.items() if k in ('W', 'b', 'bn_gamma', 'bn_beta', 'bn_mean', 'bn_var')}
    del _L0_attn_all

    def _L0_ffn_setup():
        import jax, jax.numpy as jnp
        import numpy as np
        B, S, D, F, E = (4, 512, 192, 768, 8)
        key = jax.random.key(seed)
        ks = jax.random.split(key, 5)
        return {'x': jax.random.normal(ks[0], (B, S, D), dtype=jnp.float32), 'Ws': jax.random.normal(ks[1], (D, E), dtype=jnp.float32) * 0.02, 'bs': jnp.zeros((E,), dtype=jnp.float32), 'W1': jax.random.normal(ks[2], (E, D, F), dtype=jnp.float32) * 0.02, 'b1': jnp.zeros((E, F), dtype=jnp.float32), 'W2': jax.random.normal(ks[3], (E, F, D), dtype=jnp.float32) * 0.02, 'b2': jnp.zeros((E, D), dtype=jnp.float32)}
    _L0_ffn_all = _L0_ffn_setup()
    _L0_ffn_in = {k: v for k, v in _L0_ffn_all.items() if k in ('Ws', 'bs', 'W1', 'b1', 'W2', 'b2')}
    del _L0_ffn_all

    def _L1_attn_setup():
        import jax, jax.numpy as jnp
        import numpy as np
        B, N, E, H = (2, 512, 192, 12)
        D = E // H
        G = 16
        LN_EPS = 1e-05

        def _layernorm(x, w, b):
            mu = jnp.mean(x, axis=-1, keepdims=True)
            var = jnp.mean(jnp.square(x - mu), axis=-1, keepdims=True)
            return (x - mu) * jax.lax.rsqrt(var + LN_EPS) * w + b
        key = jax.random.key(seed)
        ks = jax.random.split(key, 8)
        s = E ** (-0.5)
        x = jax.random.normal(ks[0], (B, N, E), jnp.float32)
        log_slope = -2.0 ** (-8.0 * (jnp.arange(H, dtype=jnp.float32) + 1.0) / H)
        Wq = jax.random.normal(ks[1], (E, E), jnp.float32) * s
        Wk = jax.random.normal(ks[2], (E, E), jnp.float32) * s
        Wv = jax.random.normal(ks[3], (E, E), jnp.float32) * s
        Wo = jax.random.normal(ks[4], (E, E), jnp.float32) * s
        Wg1 = jax.random.normal(ks[5], (E, G), jnp.float32) * s
        Wg2 = jax.random.normal(ks[6], (G, E), jnp.float32) * G ** (-0.5)
        ln_w = jnp.ones((E,), jnp.float32)
        ln_b = jnp.zeros((E,), jnp.float32)
        return {'x': x, 'log_slope': log_slope, 'Wq': Wq, 'Wk': Wk, 'Wv': Wv, 'Wo': Wo, 'Wg1': Wg1, 'Wg2': Wg2, 'ln_w': ln_w, 'ln_b': ln_b}
    _L1_attn_all = _L1_attn_setup()
    _L1_attn_in = {k: v for k, v in _L1_attn_all.items() if k in ('log_slope', 'Wq', 'Wk', 'Wv', 'Wo', 'Wg1', 'Wg2', 'ln_w', 'ln_b')}
    del _L1_attn_all

    def _L1_ffn_setup():
        import jax, jax.numpy as jnp
        import numpy as np
        DECAY = 0.9
        EPS = 0.01
        TOP_K = 2
        key = jax.random.key(seed)
        k1, k2, k3, k4 = jax.random.split(key, 4)
        B, S, H, I, E = (4, 512, 192, 512, 8)
        return {'hidden_states': jax.random.normal(k1, (B, S, H), jnp.float32), 'router_w': jax.random.normal(k2, (E, H), jnp.float32) * 0.02, 'w1': jax.random.normal(k3, (E, I, H), jnp.float32) * 0.02, 'w2': jax.random.normal(k4, (E, H, I), jnp.float32) * 0.02}
    _L1_ffn_all = _L1_ffn_setup()
    _L1_ffn_in = {k: v for k, v in _L1_ffn_all.items() if k in ('router_w', 'w1', 'w2')}
    del _L1_ffn_all
    return {'x': x, 'L0_tok_W0': _L0_tok_in['W0'], 'L0_tok_b0': _L0_tok_in['b0'], 'L0_tok_W1': _L0_tok_in['W1'], 'L0_tok_b1': _L0_tok_in['b1'], 'L0_tok_W2': _L0_tok_in['W2'], 'L0_tok_b2': _L0_tok_in['b2'], 'L0_tok_Wf': _L0_tok_in['Wf'], 'L0_tok_bf': _L0_tok_in['bf'], 'L0_tok_idx0': _L0_tok_in['idx0'], 'L0_tok_idx1': _L0_tok_in['idx1'], 'L0_tok_idx2': _L0_tok_in['idx2'], 'L0_attn_W': _L0_attn_in['W'], 'L0_attn_b': _L0_attn_in['b'], 'L0_attn_bn_gamma': _L0_attn_in['bn_gamma'], 'L0_attn_bn_beta': _L0_attn_in['bn_beta'], 'L0_attn_bn_mean': _L0_attn_in['bn_mean'], 'L0_attn_bn_var': _L0_attn_in['bn_var'], 'L0_ffn_Ws': _L0_ffn_in['Ws'], 'L0_ffn_bs': _L0_ffn_in['bs'], 'L0_ffn_W1': _L0_ffn_in['W1'], 'L0_ffn_b1': _L0_ffn_in['b1'], 'L0_ffn_W2': _L0_ffn_in['W2'], 'L0_ffn_b2': _L0_ffn_in['b2'], 'L1_attn_log_slope': _L1_attn_in['log_slope'], 'L1_attn_Wq': _L1_attn_in['Wq'], 'L1_attn_Wk': _L1_attn_in['Wk'], 'L1_attn_Wv': _L1_attn_in['Wv'], 'L1_attn_Wo': _L1_attn_in['Wo'], 'L1_attn_Wg1': _L1_attn_in['Wg1'], 'L1_attn_Wg2': _L1_attn_in['Wg2'], 'L1_attn_ln_w': _L1_attn_in['ln_w'], 'L1_attn_ln_b': _L1_attn_in['ln_b'], 'L1_ffn_router_w': _L1_ffn_in['router_w'], 'L1_ffn_w1': _L1_ffn_in['w1'], 'L1_ffn_w2': _L1_ffn_in['w2']}

def reference(x, L0_tok_W0, L0_tok_b0, L0_tok_W1, L0_tok_b1, L0_tok_W2, L0_tok_b2, L0_tok_Wf, L0_tok_bf, L0_tok_idx0, L0_tok_idx1, L0_tok_idx2, L0_attn_W, L0_attn_b, L0_attn_bn_gamma, L0_attn_bn_beta, L0_attn_bn_mean, L0_attn_bn_var, L0_ffn_Ws, L0_ffn_bs, L0_ffn_W1, L0_ffn_b1, L0_ffn_W2, L0_ffn_b2, L1_attn_log_slope, L1_attn_Wq, L1_attn_Wk, L1_attn_Wv, L1_attn_Wo, L1_attn_Wg1, L1_attn_Wg2, L1_attn_ln_w, L1_attn_ln_b, L1_ffn_router_w, L1_ffn_w1, L1_ffn_w2):
    import jax
    import jax.numpy as jnp

    def _L0_tok_ref(x, W0, b0, W1, b1, W2, b2, Wf, bf, idx0, idx1, idx2):
        import jax, jax.numpy as jnp
        import numpy as np
        B = 16
        IMG = 64
        CH = 3
        EMBED = 64
        GP = 16
        PRE = [1, 2, 4]
        N_LEVELS = 3
        FUSED = EMBED * N_LEVELS

        def hilbert_flat_indices(n):
            t = np.arange(n * n, dtype=np.int64)
            x = np.zeros(n * n, dtype=np.int64)
            y = np.zeros(n * n, dtype=np.int64)
            s = 1
            while s < n:
                rx = 1 & t // 2
                ry = 1 & (t ^ rx)
                swap = ry == 0
                flip = swap & (rx == 1)
                x = np.where(flip, s - 1 - x, x)
                y = np.where(flip, s - 1 - y, y)
                x2 = np.where(swap, y, x)
                y2 = np.where(swap, x, y)
                x, y = (x2, y2)
                x = x + s * rx
                y = y + s * ry
                t = t // 4
                s *= 2
            return y * n + x

        def _level(x, idx, W, b, p, gp):
            Bsz, C, H, _ = x.shape
            h = H // p
            t = x.reshape(Bsz, C, h, p, h, p).transpose(0, 2, 4, 3, 5, 1).reshape(Bsz, h * h, p * p * C)
            t = t[:, idx]
            t = t.reshape(Bsz, h * h // gp, gp * p * p * C)
            return t @ W.T + b

        def _interp_linear(x, n_out):
            L = x.shape[1]
            pos = (jnp.arange(n_out, dtype=jnp.float32) + 0.5) * (L / n_out) - 0.5
            pos = jnp.clip(pos, 0.0, L - 1)
            i0 = jnp.floor(pos).astype(jnp.int32)
            i1 = jnp.minimum(i0 + 1, L - 1)
            w = (pos - i0).astype(x.dtype)
            return x[:, i0] * (1.0 - w)[None, :, None] + x[:, i1] * w[None, :, None]
        Ws = [(idx0, W0, b0, PRE[0]), (idx1, W1, b1, PRE[1]), (idx2, W2, b2, PRE[2])]
        outs = [_level(x, idx, W, b, p, GP) for idx, W, b, p in Ws]
        n_tokens = outs[0].shape[1]
        outs = [outs[0]] + [_interp_linear(o, n_tokens) for o in outs[1:]]
        y = jnp.concatenate(outs, axis=-1)
        return y @ Wf.T + bf

    def _L0_attn_ref(x, W, b, bn_gamma, bn_beta, bn_mean, bn_var):
        import jax, jax.numpy as jnp
        import numpy as np
        TAU = 2.0
        BN_EPS = 1e-05
        SG_ALPHA = 2.0

        @jax.custom_vjp
        def spike(u):
            return (u >= 0).astype(u.dtype)

        def _spike_fwd(u):
            return (spike(u), u)

        def _spike_bwd(u, g):
            sg = SG_ALPHA / 2.0 / (1.0 + (jnp.pi / 2.0 * SG_ALPHA * u) ** 2)
            return (g * sg,)
        spike.defvjp(_spike_fwd, _spike_bwd)

        def lif(x, v_th):
            return spike(x / TAU - v_th)

        def bn_eval(x, gamma, beta, mean, var):
            inv = gamma / jnp.sqrt(var + BN_EPS)
            return x * inv + (beta - mean * inv)
        B, N, D = x.shape
        H = 12
        Hd = D // H
        scale = Hd ** (-0.125)

        def branch(inp, i, v_th=1.0):
            y = jnp.einsum('bnd,od->bno', inp, W[i]) + b[i]
            y = bn_eval(y, bn_gamma[i], bn_beta[i], bn_mean[i], bn_var[i])
            return lif(y, v_th)
        q = branch(x, 0)
        k = branch(x, 1)
        v = branch(x, 2)
        q = q.reshape(B, N, H, Hd).transpose(0, 2, 1, 3)
        k = k.reshape(B, N, H, Hd).transpose(0, 2, 1, 3)
        v = v.reshape(B, N, H, Hd).transpose(0, 2, 1, 3)
        attn = jnp.einsum('bhnd,bhmd->bhnm', q, k) * scale
        xa = jnp.einsum('bhnm,bhmd->bhnd', attn, v)
        xa = xa.transpose(0, 2, 1, 3).reshape(B, N, D)
        xa = lif(xa, 0.5)
        xa = branch(xa, 3)
        return xa

    def _L0_ffn_ref(x, Ws, bs, W1, b1, W2, b2):
        import jax, jax.numpy as jnp
        import numpy as np
        B, S, D, F, E = (4, 512, 192, 768, 8)
        b, s, d = x.shape
        xt = x.reshape(-1, d)
        logits = xt @ Ws + bs
        probs = jax.nn.softmax(logits, axis=-1)
        routes = jnp.argmax(probs, axis=-1)
        prob_max = jnp.max(probs, axis=-1)
        h = jax.nn.gelu(jnp.einsum('td,edf->etf', xt, W1) + b1[:, None, :], approximate=False)
        y = jnp.einsum('etf,efd->etd', h, W2) + b2[:, None, :]
        out = jnp.take_along_axis(y, routes[None, :, None], axis=0)[0]
        out = out * prob_max[:, None]
        return out.reshape(b, s, d)

    def _L1_attn_ref(x, log_slope, Wq, Wk, Wv, Wo, Wg1, Wg2, ln_w, ln_b):
        import jax, jax.numpy as jnp
        import numpy as np
        B, N, E, H = (2, 512, 192, 12)
        D = E // H
        G = 16
        LN_EPS = 1e-05

        def _layernorm(x, w, b):
            mu = jnp.mean(x, axis=-1, keepdims=True)
            var = jnp.mean(jnp.square(x - mu), axis=-1, keepdims=True)
            return (x - mu) * jax.lax.rsqrt(var + LN_EPS) * w + b
        b, n, e = x.shape
        h = log_slope.shape[0]
        d = e // h
        silu = jax.nn.silu
        q = silu(x @ Wq).reshape(b, n, h, d).transpose(0, 2, 1, 3)
        k = silu(x @ Wk).reshape(b, n, h, d).transpose(0, 2, 1, 3)
        v = silu(x @ Wv).reshape(b, n, h, d).transpose(0, 2, 1, 3)
        idx = jnp.arange(n, dtype=jnp.float32)
        diff = idx[:, None] - idx[None, :]
        keep = diff >= 0
        decay = jnp.where(keep, jnp.exp(log_slope[:, None, None] * jnp.maximum(diff, 0.0)), 0.0)
        energy = jnp.einsum('bhnd,bhmd->bhnm', q, k) * decay
        out = jnp.einsum('bhnm,bhmd->bhnd', energy, v)
        out = out.transpose(0, 2, 1, 3).reshape(b, n, e)
        gate = jax.nn.sigmoid(x @ Wg1 @ Wg2)
        out = out * gate
        out = out @ Wo
        out = _layernorm(out, ln_w, ln_b)
        return out

    def _L1_ffn_ref(hidden_states, router_w, w1, w2):
        import jax, jax.numpy as jnp
        import numpy as np
        DECAY = 0.9
        EPS = 0.01
        TOP_K = 2
        B, S, H = hidden_states.shape
        E = router_w.shape[0]
        flat = hidden_states.reshape(B * S, H)
        logits = flat @ router_w.T
        probs = jax.nn.softmax(logits, axis=-1)
        topk_probs, topk_idx = jax.lax.top_k(probs, TOP_K)
        importance = jax.lax.stop_gradient(probs).sum(axis=0)
        running = jnp.ones((E,), dtype=flat.dtype)
        blended = running + (1.0 - DECAY) * (importance - running)
        running = blended + EPS
        balance = running[topk_idx]
        balanced = topk_probs / balance
        balanced = balanced / balanced.sum(axis=-1, keepdims=True)
        h = jnp.einsum('th,eih->tei', flat, w1)
        h = jax.nn.silu(h)
        outs = jnp.einsum('tei,ehi->teh', h, w2)
        sel = jnp.take_along_axis(outs, topk_idx[:, :, None], axis=1)
        combined = (sel * balanced[..., None]).sum(axis=1)
        return combined.reshape(B, S, H)
    h = _L0_tok_ref(x, L0_tok_W0, L0_tok_b0, L0_tok_W1, L0_tok_b1, L0_tok_W2, L0_tok_b2, L0_tok_Wf, L0_tok_bf, L0_tok_idx0, L0_tok_idx1, L0_tok_idx2)
    h = h + _L0_attn_ref(_layernorm(h, axis=-1), L0_attn_W, L0_attn_b, L0_attn_bn_gamma, L0_attn_bn_beta, L0_attn_bn_mean, L0_attn_bn_var)
    h = h + _L0_ffn_ref(_layernorm(h, axis=-1), L0_ffn_Ws, L0_ffn_bs, L0_ffn_W1, L0_ffn_b1, L0_ffn_W2, L0_ffn_b2)
    h = h + _L1_attn_ref(_layernorm(h, axis=-1), L1_attn_log_slope, L1_attn_Wq, L1_attn_Wk, L1_attn_Wv, L1_attn_Wo, L1_attn_Wg1, L1_attn_Wg2, L1_attn_ln_w, L1_attn_ln_b)
    h = h + _L1_ffn_ref(_layernorm(h, axis=-1), L1_ffn_router_w, L1_ffn_w1, L1_ffn_w2)
    return h

_drawn_inputs = setup_inputs


def setup_inputs(seed=0):
    import zlib

    import numpy as np

    out = dict(_drawn_inputs(seed))
    spreads = {'L0_attn_b': (0.0, 0.1),
     'L0_ffn_bs': (0.0, 0.437),
     'L0_ffn_b1': (0.0, 0.8),
     'L0_ffn_b2': (0.0, 0.282),
     'L1_attn_ln_w': (1.0, 0.2),
     'L1_attn_ln_b': (0.0, 0.1)}
    factors = {'L0_ffn_W1': 2.951}
    for name, (base, spread) in spreads.items():
        noise = np.random.default_rng([zlib.crc32(name.encode()), seed]).standard_normal(out[name].shape)
        drawn = base * np.exp(spread * noise) if base else spread * noise
        out[name] = jnp.asarray(drawn.astype(out[name].dtype))
    for name, factor in factors.items():
        out[name] = (out[name] * factor).astype(out[name].dtype)
    return out
```

```python
from contextlib import ExitStack

import numpy as np

import concourse.bass as bass
from concourse import mybir

F32 = mybir.dt.float32
BF16 = mybir.dt.bfloat16
I32 = mybir.dt.int32
ALU = mybir.AluOpType
ACT = mybir.ActivationFunctionType
AX = mybir.AxisListType.X

P = 128
IMAGES = 4
IMG = 64
CH = 3
GP = 16
EMBED = 64
D = 192
DH = 96
TOKENS = 256
T = IMAGES * TOKENS // P
HALF = T // 2
HEADS = 12
HD = D // HEADS
HPAD = 32
HG = 3
E = 8
F0 = 768
F1 = 512
LN_EPS = 1e-5
L1 = TOKENS // 4
L2 = TOKENS // 16
NT0 = T + E - 1
NT1 = 2 * T + E - 1
ROWS = T * P
PAIRS = [u for t in range(HALF) for u in (t, t + HALF)]

C_ID = 0
C_TRI = C_ID + P
C_DIFF = C_TRI + P
C_KEEP = C_DIFF + P
C_IOTA = C_KEEP + P
C_A = C_IOTA + P
C_BD = C_A + TOKENS
C_BDP = C_BD + DH
C_E8 = C_BDP + 64
C_TRI8 = C_E8 + E
C_J = C_TRI8 + E * E
C_J128 = C_J + NT1
C_TOK = C_J128 + NT1 * (E - 1)
C_ROW = C_TOK + 2 * T
C_DK = C_ROW + NT1
C_DQ = C_DK + 1
C_END = C_DQ + 1


def constants():
    c = np.zeros((P, C_END), np.float32)
    p = np.arange(P)
    c[:, C_ID:C_ID + P] = np.eye(P)
    c[:, C_TRI:C_TRI + P] = p[:, None] < p[None, :]
    c[:, C_DIFF:C_DIFF + P] = np.maximum(p[None, :] - p[:, None], 0)
    c[:, C_KEEP:C_KEEP + P] = p[None, :] >= p[:, None]
    c[:, C_IOTA:C_IOTA + P] = p[None, :]
    for at, n in ((0, L1), (L1, L2)):
        pos = np.clip((np.arange(TOKENS, dtype=np.float32) + 0.5) * (n / TOKENS) - 0.5, 0.0, n - 1)
        i0 = np.floor(pos).astype(np.int64)
        i1 = np.minimum(i0 + 1, n - 1)
        w = (pos - i0).astype(np.float32)
        np.add.at(c, (at + i0, C_A + np.arange(TOKENS)), 1.0 - w)
        np.add.at(c, (at + i1, C_A + np.arange(TOKENS)), w)
    c[L1 + L2, C_A:C_A + TOKENS] = 1.0
    q = np.arange(DH)
    c[:DH, C_BD:C_BD + DH] = q[:, None] // HD == q[None, :] // HD
    c[:, C_BDP:C_BDP + 64] = p[:, None] // HPAD == np.arange(64)[None, :] // HD
    c[:, C_E8:C_E8 + E] = np.arange(E) - E
    c[:, C_TRI8:C_TRI8 + E * E] = np.tril(np.ones((E, E))).reshape(1, -1)
    c[:, C_J:C_J + NT1] = np.arange(NT1)
    c[:, C_J128:C_J128 + NT1 * (E - 1)] = np.repeat(np.arange(NT1) * P, E - 1)
    t = np.arange(T)
    row = (t % HALF) * TOKENS + (t // HALF) * P
    for k in range(2):
        c[:, C_TOK + k * T:C_TOK + (k + 1) * T] = k * ROWS + row[None, :] + p[:, None]
    c[:, C_ROW:C_ROW + NT1] = 2 * ROWS + np.arange(NT1) * P + p[:, None]
    c[:, C_DK] = P - 1 - p
    c[:, C_DQ] = p + 1
    return c


class Count:

    def __init__(self, engine, sem):
        self.engine, self.sem, self.n = engine, sem, 0

    def did(self, instruction):
        instruction.then_inc(self.sem, 1)
        self.n += 1
        return self.n

    def settle(self):
        self.engine.wait_ge(self.sem, self.n)


def spread(ap, axis, shape):
    return ap.unsqueeze(axis).to_broadcast(shape)


def build(nc, a, out):
    ctx = ExitStack()
    with ctx:
        def sb(name, shape, dt=F32):
            return ctx.enter_context(nc.sbuf_tensor(name, shape, dt))

        def sem(name):
            return ctx.enter_context(nc.semaphore(name))

        def dram(name, shape):
            return nc.dram_tensor(name, shape, F32, kind="Internal").ap()

        xn_rows = [dram(f"xn_rows{k}", (ROWS, D)) for k in range(2)]
        y_rows = [dram(f"y_rows{k}", (2 * ROWS + NT1 * P, D)) for k in range(2)]

        cst = sb("cst", [P, C_END])
        ones = sb("ones", [P, P])
        ones16 = sb("ones16", [P, P], BF16)
        ident16 = sb("ident16", [P, P], BF16)
        tri16 = sb("tri16", [P, P], BF16)
        H = sb("H", [P, T, D])
        xn = sb("xn", [P, T, D])
        xT = sb("xT", [DH, T, 2, P])
        stats = sb("stats", [P, T, 6])
        mv = sb("mv", [P, T, 2])
        var_eps = sb("var_eps", [P, T])
        rstd = sb("rstd", [P, T])
        mhalf = sb("mhalf", [P, T])

        w1_space = sb("w1_space", [P, 2 * E * F0])
        w1a = w1_space[0:DH + 1, :].rearrange("p (c e f) -> p c e f", c=2, e=E)
        w2a = sb("w2a", [P, E, F0 // P, D])
        b2a = sb("b2a", [P, E * D])
        R1 = 2 * E * F1
        region = sb("region", [P, R1 + E * (F1 // P) * D])
        w1b = region[0:DH, 0:R1].rearrange("p (c e f) -> p c e f", c=2, e=E)
        w2b = region[:, R1:].rearrange("p (e f d) -> p e f d", e=E, f=F1 // P)
        taken = {"space": 0, "region": 0, "late": 0}

        def place(where, buffer, rows, n):
            lo = taken[where]
            taken[where] += n
            assert taken[where] <= buffer.shape[1], where
            return buffer[0:rows, lo:lo + n]

        def first(rows, n):
            return place("space", w1_space, rows, n)

        def early(rows, n):
            return place("region", region, rows, n)

        idx0 = sb("idx0", [P, 2 * GP], I32)
        idx1 = sb("idx1", [P, 8], I32)
        idx2 = sb("idx2", [P, 2], I32)
        g0 = first(P, 2 * GP * 12)
        g1 = first(P, 8 * 48)
        g2 = first(P, 2 * 192)
        t0 = first(48, 2 * 512)
        t1 = first(DH, 512)
        t2 = first(DH, 512)
        w0t = first(48, EMBED)
        w1t = first(DH, 2 * EMBED)
        w2t = first(DH, 8 * EMBED)
        tb = first(EMBED, 3)
        wft = first(EMBED, 3 * D)
        y0t = first(EMBED, 2 * 512)
        y12t = first(EMBED, IMAGES * (L1 + L2))
        zz = first(L1 + L2 + 1, IMAGES * D)
        bn = first(P, 5 * 4 * D)
        inv = early(P, 4 * D)
        thr = early(P, 4 * D)
        bn_t = first(P, 4 * D)
        wqkv = early(DH, 2 * 3 * D)
        w3 = first(DH, 2 * D)
        w3r = first(DH, 2 * D)
        w3s = early(DH, 3 * D).bitcast(BF16).rearrange("p (s c n) -> p s c n", s=3, c=2)
        spk = early(P, T * 3 * D // 2).bitcast(BF16).rearrange("p (t n) -> p t n", t=T)
        qT16 = early(DH, T * P).bitcast(BF16).rearrange("p (t c n) -> p t c n", t=T, c=2)
        kv16 = early(DH, 2 * DH).bitcast(BF16).rearrange("p (u c n) -> p u c n", u=2, c=2)
        s16 = early(DH, 2 * 2 * P).bitcast(BF16).rearrange("p (u h c n) -> p u h c n", u=2, h=2, c=2)
        fire = early(P, 2 * D)

        ws = sb("ws", [DH, 2, E])
        bsr = sb("bsr", [P, E])
        wr = sb("wr", [DH, 2, E])
        lg = sb("lg", [P, T, E])
        pr = sb("pr", [P, T, E])
        rt = sb("rt", [P, T, E])
        tops = [sb(f"top{k}", [P, T, E]) for k in range(2)]
        oh16 = sb("oh16", [P, T * E], BF16)
        ohs = sb("ohs", [P, T, E])
        sm = sb("sm", [P, 16, T])
        cnt = sb("cnt", [P, 4, E])
        cnti = sb("cnti", [P, E], I32)
        cum = sb("cum", [P, E, E])
        sloti = sb("sloti", [P, 3, 2 * T], I32)
        slot = sb("slot", [P, 3, 2 * T])
        jmap = sb("jmap", [P, NT1, E - 1])
        texp = sb("texp", [P, NT1])
        texpi = [sb(f"texpi{k}", [P, NT1], I32) for k in range(2)]
        AB = sb("AB", [P, 2 * T, 2, NT1])
        ohr = sb("ohr", [P, 2, P])
        dmp = sb("dmp", [P, 3, NT1])
        gid = [sb(f"gid{k}", [P, NT1], I32) for k in range(2)]
        did = [sb(f"did{k}", [P, NT1], I32) for k in range(2)]
        pmax = sb("pmax", [P, 3, T])

        xg = sb("xg", [P, 2, D])
        xgT = sb("xgT", [DH + 1, 2, 2, P])
        hs = sb("hs", [P, 2, F0])
        hT = sb("hT", [P, 2, F0 // P, P])
        ys = sb("ys", [P, 2, D])

        wqk2 = sb("wqk2", [DH, 2, 3 * D + 16])
        wg2 = sb("wg2", [16, D])
        wo = sb("wo", [DH, 2, D])
        lnw = sb("lnw", [P, 2, D])
        ls = sb("ls", [P, HEADS])
        dkq = sb("dkq", [P, 2, HEADS])
        qk = w2a[:, :, :, :].rearrange("p e f d -> p (e f d)")

        def over2(n):
            return place("late", qk, P, n)

        qkp = over2(2 * 2 * HEADS * HPAD).rearrange("p (u a h j) -> p u a h j", u=2, a=2, h=HEADS)
        dec = over2(HEADS * P).rearrange("p (h n) -> p h n", h=HEADS)
        kd = over2(HEADS * HPAD).rearrange("p (h j) -> p h j", h=HEADS)
        v2 = over2(2 * (D + 16)).rearrange("p (u n) -> p u n", u=2)
        qkT = over2(2 * 6 * P).rearrange("p (u g n) -> p u g n", u=2, g=6)
        g1T = over2(2 * P).rearrange("p (u n) -> p u n", u=2)
        pt = over2(HEADS * P).rearrange("p (i g n) -> p i g n", i=4, g=HG)
        kvs = over2(HALF * D).rearrange("p (b g n) -> p b g n", b=HALF, g=HG)
        cross = over2(D)
        gate = hs[:, :, 0:D]
        og = hs[:, :, D:2 * D]
        oT = hT[:, :, 0:2, :]

        ps = ctx.enter_context(nc.psum_tensor("ps", [P, 8, 512], F32))

        def bank(i, rows=P, n=512, lo=0):
            return ps[0:rows, i, lo:lo + n]

        ident = cst[:, C_ID:C_ID + P]

        cst_in = sem("cst_in")
        tokw_in = sem("tokw_in")
        idx_in = sem("idx_in")
        g2_in = sem("g2_in")
        g1_in = sem("g1_in")
        g0_in = [sem(f"g0_in{n}") for n in range(2)]
        bn_in = sem("bn_in")
        aw_in = sem("aw_in")
        rw_in = sem("rw_in")
        lw_in = sem("lw_in")
        wa_in = sem("wa_in")
        wb_in = sem("wb_in")
        consts_ready = sem("consts_ready")
        mhalf_ready = sem("mhalf_ready")
        dve_done = sem("dve_done")
        act_done = sem("act_done")
        pe_t = sem("tok_transposed")
        dve_t = sem("tok_copied")
        pe_y = sem("tok_level_done")
        dve_y = sem("tok_level_copied")
        pe_z = sem("z_done")
        dve_z = sem("z_copied")
        pe_h = sem("h_done")
        dve_h = sem("h_copied")
        var_ready = sem("var_ready")
        rstd_ready = sem("rstd_ready")
        xn_ready = sem("xn_ready")
        pe_xt = sem("xt_done")
        xt_ready = sem("xt_ready")
        bnw_ready = sem("bnw_ready")
        bn_root = sem("bn_root")
        bn_var = sem("bn_var")
        qkv_done = sem("qkv_done")
        spk_ready = sem("spk_ready")
        qtr_done = sem("qtr_done")
        qT_ready = sem("qT_ready")
        kv_done = sem("kv_done")
        kv_ready = sem("kv_ready")
        xa_done = sem("xa_done")
        s_ready = sem("s_ready")
        y3_done = sem("y3_done")
        fire_done = sem("fire_done")
        logit_done = sem("logit_done")
        shift_ready = sem("shift_ready")
        exp_ready = sem("exp_ready")
        oh_ready = sem("oh_ready")
        rank_done = sem("rank_done")
        imp_ready = sem("imp_ready")
        imp_done = sem("imp_done")
        ohr_ready = sem("ohr_ready")
        inv_done = sem("inv_done")
        map_ready = sem("map_ready")
        xrow_out = sem("xrow_out")
        dec_ready = sem("dec_ready")
        dk_ready = sem("dk_ready")
        proj_done = sem("proj_done")
        silu_ready = sem("silu_ready")
        g1_ready = sem("g1_ready")
        tr2_done = sem("tr2_done")
        tr2_ready = sem("tr2_ready")
        gate_done = sem("gate_done")
        gate_ready = sem("gate_ready")
        kd_ready = sem("kd_ready")
        kvs_done = sem("kvs_done")
        kvs_ready = sem("kvs_ready")
        sc_done = sem("scores_done")
        pt_ready = sem("pt_ready")
        pv_done = sem("pv_done")
        og_ready = sem("og_ready")
        ot_done = sem("ot_done")
        oT_ready = sem("oT_ready")
        wo_done = sem("wo_done")
        attn_out = sem("attn_out")
        final = sem("final")
        stored = sem("stored")
        gates_init = sem("gates_init")
        ffn = []
        for k in range(2):
            ffn.append({n: sem(f"m{k}_{n}") for n in (
                "rows0", "rows1", "xt", "xgT", "up", "act", "htr", "hT", "down", "y",
                "put0", "put1", "back")})

        block = ctx.enter_context(nc.Block())

        back0 = xn[:, :, :].unsqueeze(1)
        back1 = qk[:, 0:2 * T * D].rearrange("p (k t d) -> p k t d", k=2, t=T)

        @block.sync
        def _(sp):
            sp.dma_start(idx2[:], a["idx2"]).then_inc(idx_in, 16)
            sp.dma_start(idx1[:], a["idx1"]).then_inc(idx_in, 16)
            sp.dma_start(idx0[:], a["idx0"]).then_inc(idx_in, 16)
            sp.dma_start(cst[:], a["cst"]).then_inc(cst_in, 16)
            sp.dma_start(w0t, a["w0t"]).then_inc(tokw_in, 16)
            sp.dma_start(w1t, a["w1t"]).then_inc(tokw_in, 16)
            sp.dma_start(w2t, a["w2t"]).then_inc(tokw_in, 16)
            sp.dma_start(tb, a["tb"]).then_inc(tokw_in, 16)
            sp.dma_start(wft, a["wft"]).then_inc(tokw_in, 16)
            sp.dma_start(zz[L1 + L2:L1 + L2 + 1, :].rearrange("p (b n) -> p b n", b=IMAGES),
                         spread(a["bf"], 1, [1, IMAGES, D])).then_inc(tokw_in, 16)
            for i in range(5):
                sp.dma_start(bn[:, i * 4 * D:(i + 1) * 4 * D],
                             a["bn"][i, :].partition_broadcast(P)).then_inc(bn_in, 16)
            sp.dma_start(wqkv.rearrange("p (c n) -> p c n", c=2), a["wqkv"]).then_inc(aw_in, 16)
            sp.dma_start(w3.rearrange("p (c n) -> p c n", c=2), a["w3"]).then_inc(aw_in, 16)
            sp.dma_start(ws[:], a["ws"]).then_inc(rw_in, 16)
            sp.dma_start(wr[:], a["wr"]).then_inc(rw_in, 16)
            sp.dma_start(bsr[:], a["bs"].partition_broadcast(P)).then_inc(rw_in, 16)
            for e in range(E):
                sp.dma_start(w2a[:, e, :, :], a["w2a"][:, e, :, :]).then_inc(wa_in, 16)
            sp.wait_ge(dve_h, T // 2)
            sp.wait_ge(bnw_ready, 3)
            for e in range(E):
                sp.dma_start(w1a[0:DH, :, e, :], a["w1a"][:, :, e, :]).then_inc(wa_in, 16)
            sp.dma_start(w1a[DH:DH + 1, 0, :, :], a["b1a"]).then_inc(wa_in, 16)
            sp.dma_start(b2a[:], a["b2a"].partition_broadcast(P)).then_inc(wa_in, 16)
            sp.dma_start(wqk2[:], a["wqk2"]).then_inc(lw_in, 16)
            sp.dma_start(wg2[:], a["wg2"]).then_inc(lw_in, 16)
            sp.dma_start(wo[:], a["wo"]).then_inc(lw_in, 16)
            sp.dma_start(lnw[:, 0, :], a["lnw"].partition_broadcast(P)).then_inc(lw_in, 16)
            sp.dma_start(lnw[:, 1, :], a["lnb"].partition_broadcast(P)).then_inc(lw_in, 16)
            sp.dma_start(ls[:], a["ls"].partition_broadcast(P)).then_inc(lw_in, 16)

            def rows_of(dram_rows, t):
                lo = (t % HALF) * TOKENS + (t // HALF) * P
                return dram_rows[lo:lo + P, :]

            for k, ln in ((0, 1), (1, 3)):
                m = ffn[k]
                for i, t in enumerate((PAIRS, range(T))[k]):
                    sp.wait_ge(xn_ready, (T * ln) + i + 1)
                    sp.dma_start(rows_of(xn_rows[k], t), xn[:, t, :]).then_inc(xrow_out, 16)
                if k == 0:
                    sp.wait_ge(fire_done, T)
                    for e in range(E):
                        sp.dma_start(w1b[:, :, e, :], a["w1b"][:, :, e, :]).then_inc(wb_in, 16)
                        sp.dma_start(w2b[:, e, :, :], a["w2b"][:, e, :, :]).then_inc(wb_in, 16)
                n = (NT0, NT1)[k]
                sp.wait_ge(m["put0"], 16 * ((n + 1) // 2))
                sp.wait_ge(m["put1"], 16 * (n // 2))
                dst = (back0, back1)[k]
                for j in range(k + 1):
                    for t in range(T):
                        sp.dma_start(dst[:, j, t, :],
                                     y_rows[k][j * ROWS + (t % HALF) * TOKENS + (t // HALF) * P:][0:P, :]
                                     ).then_inc(m["back"], 16)
            for t in range(T):
                sp.wait_ge(final, t + 1)
                sp.dma_start(rows_of(out, t), H[:, t, :]).then_inc(stored, 16)
            sp.wait_ge(stored, 16 * T)

        @block.gpsimd
        def _(pool):
            nc.gpsimd.memset(mhalf[:], -0.5).then_inc(mhalf_ready, 1)
            pool.wait_ge(idx_in, 48)
            for q in range(2):
                pool.indirect_dma_start(out=g2[:, q * 192:(q + 1) * 192], out_offset=None, in_=a["x2"],
                                        in_offset=bass.IndirectOffsetOnAxis(idx2[:, q:q + 1], 0)
                                        ).then_inc(g2_in, 16)
            for q in range(8):
                pool.indirect_dma_start(out=g1[:, q * 48:(q + 1) * 48], out_offset=None, in_=a["x1"],
                                        in_offset=bass.IndirectOffsetOnAxis(idx1[:, q:q + 1], 0)
                                        ).then_inc(g1_in, 16)
            for q in range(2 * GP):
                pool.indirect_dma_start(out=g0[:, q * 12:(q + 1) * 12], out_offset=None, in_=a["x0"],
                                        in_offset=bass.IndirectOffsetOnAxis(idx0[:, q:q + 1], 0)
                                        ).then_inc(g0_in[q // GP], 16)
            pool.wait_ge(mhalf_ready, 1)

            def root(first, n, at):
                pool.wait_ge(var_ready, at)
                nc.gpsimd.tensor_tensor(rstd[:, first:first + n], var_eps[:, first:first + n],
                                        mhalf[:, first:first + n], ALU.pow).then_inc(rstd_ready, 1)

            def mlp(k):
                m = ffn[k]
                n = (NT0, NT1)[k]
                pool.wait_ge(xrow_out, 16 * T * (k + 1))
                pool.wait_ge(map_ready, k + 1)
                for s in range(n + 3):
                    if s < n:
                        if s >= 2:
                            pool.wait_ge(m["xt"], s - 1)
                        pool.indirect_dma_start(out=xg[:, s % 2, :], out_offset=None, in_=xn_rows[k],
                                                in_offset=bass.IndirectOffsetOnAxis(gid[k][:, s:s + 1], 0)
                                                ).then_inc(m[f"rows{s % 2}"], 16)
                    if s >= 3:
                        j = s - 3
                        pool.wait_ge(m["y"], j + 1)
                        pool.indirect_dma_start(out=y_rows[k],
                                                out_offset=bass.IndirectOffsetOnAxis(did[k][:, j:j + 1], 0),
                                                in_=ys[:, j % 2, :], in_offset=None
                                                ).then_inc(m[f"put{j % 2}"], 16)

            root(0, HALF, 1)
            root(HALF, HALF, 2)
            for t in range(HALF):
                for u in (t, t + HALF):
                    root(u, 1, 2 + 2 * t + (1 if u == t else 2))
            mlp(0)
            for t in range(T):
                root(t, 1, 2 + T + t + 1)
            for t in range(T):
                root(t, 1, 2 + 2 * T + 2 * t + 1)
                root(t, 1, 2 + 2 * T + 2 * t + 2)
            mlp(1)

        @block.tensor
        def _(pe):
            def mm(o, l, r, start=True, stop=True):
                return nc.tensor.matmul(o, l, r, start=start, stop=stop)

            def tr(o, i, idn):
                return nc.tensor.transpose(o, i, idn)

            pe.wait_ge(cst_in, 16)
            pe.wait_ge(g2_in, 32)
            for b in range(IMAGES):
                last = tr(bank(3, DH, P, b * P), g2.rearrange("p (f b) -> p b f", b=IMAGES)[:, b], ident)
            last.then_inc(pe_t, 1)
            pe.wait_ge(g1_in, 16 * 8)
            for b in range(IMAGES):
                last = tr(bank(2, DH, P, b * P), g1.rearrange("p (f b) -> p b f", b=IMAGES)[:, b], ident)
            last.then_inc(pe_t, 1)
            pe.wait_ge(tokw_in, 96)
            pe.wait_ge(dve_t, 1)
            for j in range(8):
                last = mm(bank(6, EMBED, IMAGES * L2, IMAGES * L1), w2t[:, j * EMBED:(j + 1) * EMBED],
                          t2.rearrange("p (b j n) -> p j b n", b=IMAGES, j=8)[:, j], j == 0, j == 7)
            pe.wait_ge(dve_t, 2)
            for j in range(2):
                last = mm(bank(6, EMBED, IMAGES * L1), w1t[:, j * EMBED:(j + 1) * EMBED],
                          t1.rearrange("p (b j n) -> p j b n", b=IMAGES, j=2)[:, j], j == 0, j == 1)
            last.then_inc(pe_y, 1)
            pe.wait_ge(dve_y, 2)
            for b in range(IMAGES):
                bk = (7, 2, 3, 6)[b]
                mm(bank(bk, L1, D), y12t[:, b * L1:(b + 1) * L1], wft[:, D:2 * D])
                mm(bank(bk, L2, D, D), y12t[:, IMAGES * L1 + b * L2:IMAGES * L1 + (b + 1) * L2],
                   wft[:, 2 * D:3 * D]).then_inc(pe_z, 1)
            for n in range(2):
                pe.wait_ge(g0_in[n], 16 * GP)
                for b in range(IMAGES):
                    last = tr(bank(n, 48, P, b * P),
                              g0.rearrange("p (n f b) -> p n b f", n=2, b=IMAGES)[:, n, b], ident)
                last.then_inc(pe_t, 1)
                pe.wait_ge(dve_t, 3 + n)
                mm(bank(4 + n, EMBED), w0t, t0[:, n * 512:(n + 1) * 512]).then_inc(pe_y, 1)
                pe.wait_ge(dve_y, 3 + n)
                pe.wait_ge(dve_z, 2 * IMAGES)
                for b in range(IMAGES):
                    o = bank(((4, 7), (5, 2))[n][b // 2], P, D, (b % 2) * D)
                    mm(o, y0t[:, n * 512 + b * P:n * 512 + (b + 1) * P], wft[:, 0:D], True, False)
                    last = mm(o, cst[0:L1 + L2 + 1, C_A + n * P:C_A + (n + 1) * P], zz[:, b * D:(b + 1) * D],
                              False, True)
                    if b % 2 == 1:
                        last.then_inc(pe_h, 1)

            def xtr(t, n, base):
                pe.wait_ge(xn_ready, base + 1)
                if n >= 2:
                    pe.wait_ge(xt_ready, n - 1)
                tr(bank(n % 2, DH, P), xn[:, t, 0:DH], ident)
                tr(bank(n % 2, DH, P, P), xn[:, t, DH:D], ident).then_inc(pe_xt, 1)

            pe.wait_ge(consts_ready, 4)
            pe.wait_ge(bnw_ready, 3)

            def qkv(t):
                pe.wait_ge(xt_ready, t + 1)
                if t >= 2:
                    pe.wait_ge(spk_ready, t - 1)
                for h in range(2):
                    for c in range(2):
                        last = mm(bank(2 + 2 * (t % 2) + h, P, 288), xT[:, t, c, :],
                                  wqkv[:, c * 3 * D + h * 288:c * 3 * D + (h + 1) * 288], c == 0, c == 1)
                last.then_inc(qkv_done, 1)

            b6 = ps[:, 6, :].bitcast(BF16)

            def qtr(t):
                pe.wait_ge(spk_ready, t + 1)
                if t >= 1:
                    pe.wait_ge(qT_ready, t)
                for c in range(2):
                    last = tr(b6[0:DH, c * P:(c + 1) * P], spk[:, t, c * DH:(c + 1) * DH], ident16[:])
                last.then_inc(qtr_done, 1)

            pe.wait_ge(dve_h, T // 2)
            xtr(0, 0, 0)
            for t in range(T):
                if t + 1 < T:
                    xtr(t + 1, t + 1, t + 1)
                qkv(t)
                if t >= 1:
                    qtr(t - 1)
            qtr(T - 1)
            for b in range(HALF):
                if b >= 1:
                    pe.wait_ge(kv_ready, b)
                for c in range(2):
                    for t in (b, b + HALF):
                        last = mm(bank(7, DH, DH, c * DH), spk[:, t, D + c * DH:D + (c + 1) * DH],
                                  spk[:, t, 2 * D + c * DH:2 * D + (c + 1) * DH], t == b, t != b)
                last.then_inc(kv_done, 1)
                pe.wait_ge(qT_ready, T)
                pe.wait_ge(kv_ready, b + 1)
                if b >= 1:
                    pe.wait_ge(s_ready, b)
                for h in range(2):
                    for c in range(2):
                        last = mm(bank(2, DH, P, (h * 2 + c) * P), kv16[:, b % 2, c, :], qT16[:, b + h * HALF, c, :])
                last.then_inc(xa_done, 1)
                pe.wait_ge(s_ready, b + 1)
                for h in range(2):
                    n = 2 * b + h
                    if n >= 2:
                        pe.wait_ge(fire_done, n - 1)
                    i = 0
                    for part in range(3):
                        for c in range(2):
                            last = mm(bank(4 + n % 2, P, D), s16[:, b % 2, h, c, :], w3s[:, part, c, :], i == 0, i == 5)
                            i += 1
                    last.then_inc(y3_done, 1)

            def route(k, n0, base, order, w):
                for i, t in enumerate(order):
                    xtr(t, n0 + i, base + i)
                    pe.wait_ge(xt_ready, n0 + i + 1)
                    for c in range(2):
                        last = mm(bank(2, P, E, t * E), xT[:, t, c, :], w[:, c, :], c == 0, c == 1)
                last.then_inc(logit_done, 1)
                if k == 1:
                    pe.wait_ge(imp_ready, 1)
                    mm(bank(5, P, E), ones[:], rt[:, 0, :]).then_inc(imp_done, 1)
                pe.wait_ge(oh_ready, k + 1)
                for s in range(T):
                    last = mm(bank(3, P, (T - s) * E, s * E), tri16[:] if s == 0 else ones16[:],
                              oh16[:, 0:(T - s) * E], s == 0, s == T - 1)
                for t in range(T):
                    last = mm(bank(4, P, E), ones16[:], oh16[:, t * E:(t + 1) * E], t == 0, t == T - 1)
                last.then_inc(rank_done, 1)
                n = T * (k + 1)
                nt = (NT0, NT1)[k]
                done = T * k
                for i in range(n):
                    pe.wait_ge(ohr_ready, done + i + 1)
                    mm(bank(6, P, 2 * nt), ohr[:, i % 2, :], AB[:, i, :, 0:nt], i == 0, i == n - 1
                       ).then_inc(inv_done, 1)

            def mlp(k):
                m = ffn[k]
                n, F = ((NT0, F0), (NT1, F1))[k]
                w1, w2, rows = ((w1a, w2a, DH + 1), (w1b, w2b, DH))[k]
                C = F // P
                NH = (2, 1)[k]
                W = F // NH

                def expert(s):
                    return pe.value_load(texpi[k][0:1, bass.ds(s, 1)], min_val=0, max_val=E - 1)

                def xt(s, b, half):
                    pe.wait_ge(m[f"rows{b}"], (half + 1) * 16)
                    for c in range(2):
                        last = tr(bank(0, DH, P, c * P), xg[:, b, c * DH:(c + 1) * DH], ident)
                    last.then_inc(m["xt"], 1)

                def up(s, b, prior):
                    pe.wait_ge(m["xgT"], s + 1)
                    if prior:
                        pe.wait_ge(m["act"], s - 1)
                    e = expert(s)
                    for h in range(NH):
                        for c in range(2):
                            r = rows if c == 0 else DH
                            flat = w1[0:r, c, :, :].rearrange("p e f -> p (e f)")
                            last = mm(bank(2 + 2 * b + h, P, W), xgT[0:r, b, c, :],
                                      flat[:, bass.ds(e * F + h * W, W)], c == 0, c == 1)
                    last.then_inc(m["up"], 1)

                def htr(s, b, prior):
                    pe.wait_ge(m["act"], s + 1)
                    if prior:
                        pe.wait_ge(m["hT"], s)
                    for c in range(C):
                        last = tr(bank(6 + c // 4, P, P, (c % 4) * P), hs[:, b, c * P:(c + 1) * P], ident)
                    last.then_inc(m["htr"], 1)

                def down(s, b, prior):
                    pe.wait_ge(m["hT"], s + 1)
                    if prior:
                        pe.wait_ge(m["y"], s)
                    e = expert(s)
                    flat = w2[:, :, :, :].rearrange("p e f d -> p (e f d)")
                    for c in range(C):
                        last = mm(bank(1, P, D), hT[:, b, c, :], flat[:, bass.ds(e * (C * D) + c * D, D)],
                                  c == 0, c == C - 1)
                    last.then_inc(m["down"], 1)

                pe.wait_ge(map_ready, k + 1)
                pe.wait_ge((wa_in, wb_in)[k], (16 * (2 * E + 2), 16 * 2 * E)[k])
                xt(0, 0, 0)
                up(0, 0, False)
                xt(1, 1, 0)
                up(1, 1, False)
                xt(2, 0, 1)
                htr(0, 0, False)
                up(2, 0, True)
                xt(3, 1, 1)
                htr(1, 1, True)
                down(0, 0, False)
                up(3, 1, True)
                xt(4, 0, 2)
                htr(2, 0, True)
                down(1, 1, True)
                with pe.Fori(0, (n - 5) // 2) as i:
                    for b in range(2):
                        s = 2 * i + (4 + b)
                        up(s, b, True)
                        xt(s + 1, 1 - b, i + (2 + b))
                        htr(s - 1, 1 - b, True)
                        down(s - 2, b, True)
                up(n - 1, 0, True)
                htr(n - 2, 1, True)
                down(n - 3, 0, True)
                htr(n - 1, 0, True)
                down(n - 2, 1, True)
                down(n - 1, 0, True)

            pe.wait_ge(rw_in, 48)
            route(0, T, T, PAIRS, ws)
            mlp(0)

            pe.wait_ge(lw_in, 96)
            N2 = T * 2

            def inputs(t):
                pe.wait_ge(xn_ready, N2 + t + 1)
                if t >= 2:
                    pe.wait_ge(attn_out, t - 1)
                tr(bank(0, DH, P), xn[:, t, 0:DH], ident)
                tr(bank(0, DH, P, P), xn[:, t, DH:D], ident).then_inc(pe_xt, 1)

            def proj(t):
                pe.wait_ge(xt_ready, N2 + t + 1)
                if t >= 1:
                    pe.wait_ge(gate_ready, t)
                    pe.wait_ge(kvs_ready, min(t, HALF))
                for bk, lo, hi in ((2, 0, 2 * D), (3, 2 * D, 3 * D + 16)):
                    for c in range(2):
                        last = mm(bank(bk, P, hi - lo), xT[:, t, c, :], wqk2[:, c, lo:hi], c == 0, c == 1)
                last.then_inc(proj_done, 1)

            def tr2(t):
                u = t % 2
                pe.wait_ge(silu_ready, 2 * (t + 1))
                pe.wait_ge(g1_ready, t + 1)
                for g in range(HG):
                    tr(bank(2, P, P, g * P), qkp[:, u, 0, 4 * g:4 * g + 4, :], ident)
                tr(bank(2, 16, P, 3 * P), v2[:, u, D:D + 16], ident)
                for g in range(HG):
                    last = tr(bank(3, P, P, g * P), qkp[:, u, 1, 4 * g:4 * g + 4, :], ident)
                last.then_inc(tr2_done, 1)

            def gate_and_state(t):
                u = t % 2
                pe.wait_ge(tr2_ready, t + 1)
                mm(bank(3, P, D), g1T[0:16, u, :], wg2[:]).then_inc(gate_done, 1)
                if t < HALF:
                    pe.wait_ge(kd_ready, t + 1)
                    for g in range(HG):
                        last = mm(bank(2, P, 64, g * 64), kd[:, 4 * g:4 * g + 4, :], v2[:, u, g * 64:(g + 1) * 64])
                    last.then_inc(kvs_done, 1)

            def attend(t):
                u = t % 2
                for i in range(4):
                    if t >= 1:
                        pe.wait_ge(pt_ready, 4 * (t - 1) + i + 1)
                    rows = slice(i * HPAD, i * HPAD + HD)
                    for g in range(HG):
                        last = mm(bank(4 + i, P, P, g * P), qkT[rows, u, 3 + g, :], qkT[rows, u, g, :])
                    last.then_inc(sc_done, 1)
                if t >= 1:
                    pe.wait_ge(og_ready, t)
                if t >= HALF:
                    pe.wait_ge(kvs_ready, t - HALF + 1)
                    for g in range(HG):
                        mm(bank(1, P, 64, 256 + g * 64), qkT[:, u, g, :], kvs[:, t - HALF, g, :])
                for i in range(4):
                    pe.wait_ge(pt_ready, 4 * t + i + 1)
                    for g in range(HG):
                        h = 4 * g + i
                        last = mm(bank(1, P, HD, h * HD), pt[:, i, g, :], v2[:, u, h * HD:(h + 1) * HD])
                last.then_inc(pv_done, 1)

            def project(t):
                u = t % 2
                pe.wait_ge(og_ready, t + 1)
                pe.wait_ge(xt_ready, N2 + min(t + 2, T))
                for c in range(2):
                    last = tr(bank(0, DH, P, c * P), og[:, u, c * DH:(c + 1) * DH], ident)
                last.then_inc(ot_done, 1)
                pe.wait_ge(oT_ready, t + 1)
                for c in range(2):
                    last = mm(bank(0, P, D, 256), oT[0:DH, u, c, :], wo[:, c, :], c == 0, c == 1)
                last.then_inc(wo_done, 1)

            pe.wait_ge(gates_init, 1)
            for t in range(T):
                inputs(t)
                proj(t)
                if t >= 1:
                    project(t - 1)
                tr2(t)
                gate_and_state(t)
                attend(t)
            project(T - 1)
            pe.wait_ge(attn_out, T)
            route(1, 3 * T, 3 * T, list(range(T)), wr)
            mlp(1)

        @block.scalar
        def _(act):
            act.wait_ge(bn_var, 1)
            act.activation(inv, bn_t, ACT.Sqrt).then_inc(bn_root, 1)

            def softmax_exp(k):
                act.wait_ge(shift_ready, k + 1)
                act.activation(pr[:], lg[:], ACT.Exp).then_inc(exp_ready, 1)

            def mlp(k, fn):
                m = ffn[k]
                n, F, NH = ((NT0, F0, 2), (NT1, F1, 1))[k]
                W = F // NH

                def one(s, b, prior):
                    act.wait_ge(m["up"], s + 1)
                    if prior:
                        act.wait_ge(m["htr"], s - 1)
                    act.activation(hs[:, b, 0:F].rearrange("p (h n) -> p h n", h=NH),
                                   ps[:, 2 + 2 * b:2 + 2 * b + NH, 0:W], fn).then_inc(m["act"], 1)

                one(0, 0, False)
                one(1, 1, False)
                with act.Fori(0, (n - 3) // 2) as i:
                    for b in range(2):
                        one(2 * i + (2 + b), b, True)
                one(n - 1, 0, True)

            softmax_exp(0)
            mlp(0, ACT.Gelu)
            act.wait_ge(gates_init, 1)
            done = Count(act, act_done)
            act.wait_ge(lw_in, 96)
            act.wait_ge(cst_in, 16)
            for h in range(HEADS):
                done.did(act.activation(dec[:, (h % 4) * HG + h // 4, :], cst[:, C_DIFF:C_DIFF + P], ACT.Exp, scale=ls[:, h:h + 1]))
            done.did(act.activation(dkq[:, 0, :], ls[:], ACT.Exp, scale=cst[:, C_DK:C_DK + 1]))
            done.did(act.activation(dkq[:, 1, :], ls[:], ACT.Exp, scale=cst[:, C_DQ:C_DQ + 1]))
            for t in range(T):
                u = t % 2
                act.wait_ge(proj_done, t + 1)
                if t >= 2:
                    act.wait_ge(tr2_done, t - 1)
                    act.wait_ge(pv_done, t - 1)
                act.activation(qkp[:, u, :, :, 0:HD], ps[:, 2, 0:2 * D].rearrange("p (a h j) -> p a h j", a=2, h=HEADS),
                               ACT.Silu).then_inc(silu_ready, 1)
                act.activation(v2[:, u, 0:D], ps[:, 3, 0:D], ACT.Silu).then_inc(silu_ready, 1)
                act.activation(v2[:, u, D:D + 16], ps[:, 3, D:D + 16], ACT.Copy).then_inc(g1_ready, 1)
                act.wait_ge(gate_done, t + 1)
                if t >= 2:
                    act.wait_ge(og_ready, t - 1)
                act.activation(gate[:, u, :], ps[:, 3, 0:D], ACT.Tanh, scale=0.5).then_inc(gate_ready, 1)
            softmax_exp(1)
            mlp(1, ACT.Silu)

        @block.vector
        def _(dve):
            v = nc.vector
            own = Count(dve, dve_done)
            did_, settle = own.did, own.settle

            dve.wait_ge(cst_in, 16)
            v.tensor_copy(ident16[:], ident).then_inc(consts_ready, 1)
            v.tensor_copy(tri16[:], cst[:, C_TRI:C_TRI + P]).then_inc(consts_ready, 1)
            v.memset(ones[:], 1.0).then_inc(consts_ready, 1)
            v.memset(ones16[:], 1.0).then_inc(consts_ready, 1)
            did_(v.memset(xgT[DH:DH + 1, :, 0, :], 1.0))
            dve.wait_ge(bn_in, 80)
            W4 = 4 * D
            gamma, beta, mean, var, bias = (bn[:, i * W4:(i + 1) * W4] for i in range(5))
            did_(v.tensor_scalar(bn_t, var, LN_EPS, None, ALU.add))
            settle()
            v.tensor_copy(thr, bn_t).then_inc(bn_var, 1)
            dve.wait_ge(bn_root, 1)
            did_(v.reciprocal(inv, inv))
            settle()
            did_(v.tensor_tensor(bn_t, thr, inv, ALU.mult))
            settle()
            did_(v.tensor_tensor(bn_t, bn_t, inv, ALU.mult))
            settle()
            did_(v.tensor_scalar(bn_t, bn_t, -0.5, 1.5, ALU.mult, ALU.add))
            settle()
            did_(v.tensor_tensor(inv, inv, bn_t, ALU.mult))
            settle()
            did_(v.tensor_tensor(inv, inv, gamma, ALU.mult))
            did_(v.tensor_tensor(thr, mean, bias, ALU.subtract))
            settle()
            did_(v.tensor_tensor(thr, thr, inv, ALU.mult))
            settle()
            did_(v.tensor_tensor(thr, thr, beta, ALU.subtract))
            settle()
            did_(v.tensor_scalar(thr, thr, 2.0, None, ALU.add))
            dve.wait_ge(aw_in, 32)
            for c in range(2):
                part = wqkv[:, c * 3 * D:(c + 1) * 3 * D]
                v.tensor_tensor(part, part, inv[0:DH, 0:3 * D], ALU.mult).then_inc(bnw_ready, 1)
            w3v = w3.rearrange("p (c n) -> p c n", c=2)
            w3rv = w3r.rearrange("p (c n) -> p c n", c=2)
            did_(v.tensor_tensor(w3rv, w3v, spread(inv[0:DH, 3 * D:4 * D], 1, [DH, 2, D]), ALU.mult))
            settle()
            did_(v.tensor_copy(w3s[:, 0], w3rv))
            settle()
            did_(v.tensor_tensor(w3rv, w3rv, w3s[:, 0], ALU.subtract))
            settle()
            did_(v.tensor_copy(w3s[:, 1], w3rv))
            settle()
            did_(v.tensor_tensor(w3rv, w3rv, w3s[:, 1], ALU.subtract))
            settle()
            v.tensor_copy(w3s[:, 2], w3rv).then_inc(bnw_ready, 1)

            dve.wait_ge(pe_t, 1)
            v.tensor_copy(t2, bank(3, DH)).then_inc(dve_t, 1)
            dve.wait_ge(pe_t, 2)
            v.tensor_copy(t1, bank(2, DH)).then_inc(dve_t, 1)
            dve.wait_ge(tokw_in, 96)
            dve.wait_ge(pe_y, 1)
            N1 = IMAGES * L1
            v.tensor_scalar(y12t[:, 0:N1], bank(6, EMBED, N1), tb[:, 1:2], None, ALU.add).then_inc(dve_y, 1)
            v.tensor_scalar(y12t[:, N1:], bank(6, EMBED, IMAGES * L2, N1), tb[:, 2:3], None, ALU.add).then_inc(dve_y, 1)
            for b in range(IMAGES):
                bk = (7, 2, 3, 6)[b]
                dve.wait_ge(pe_z, b + 1)
                v.tensor_copy(zz[0:L1, b * D:(b + 1) * D], bank(bk, L1, D)).then_inc(dve_z, 1)
                v.tensor_copy(zz[L1:L1 + L2, b * D:(b + 1) * D], bank(bk, L2, D, D)).then_inc(dve_z, 1)

            lns = [0]

            def norm_stats(tiles):
                for t in tiles:
                    did_(v.bn_stats(stats[:, t, :], H[:, t, :]))
                settle()
                for t in tiles:
                    did_(v.bn_aggr(mv[:, t, :], stats[:, t, :]))
                settle()
                lo = tiles[0]
                v.tensor_scalar(var_eps[:, lo:lo + len(tiles)], mv[:, lo:lo + len(tiles), 1], LN_EPS, None, ALU.add
                                ).then_inc(var_ready, 1)
                lns[0] += 1

            def normalise(t, at):
                dve.wait_ge(rstd_ready, at)
                v.tensor_scalar(xn[:, t, :], H[:, t, :], mv[:, t, 0:1], rstd[:, t:t + 1], ALU.subtract, ALU.mult
                                ).then_inc(xn_ready, 1)

            def xt_copy(t, n, bk):
                dve.wait_ge(pe_xt, n + 1)
                v.tensor_copy(xT[:, t, :, :], bank(bk, DH, 2 * P).rearrange("p (c n) -> p c n", c=2)
                              ).then_inc(xt_ready, 1)

            for n in range(2):
                dve.wait_ge(pe_t, 3 + n)
                v.tensor_copy(t0[:, n * 512:(n + 1) * 512], bank(n, 48)).then_inc(dve_t, 1)
                dve.wait_ge(pe_y, 2 + n)
                v.tensor_scalar(y0t[:, n * 512:(n + 1) * 512], bank(4 + n, EMBED), tb[:, 0:1], None, ALU.add
                                ).then_inc(dve_y, 1)
                for b in range(2):
                    dve.wait_ge(pe_h, n * 2 + b + 1)
                    v.tensor_copy(H[:, n * HALF + 2 * b:n * HALF + 2 * b + 2, :].rearrange("p t n -> p (t n)"),
                                  bank(((4, 7), (5, 2))[n][b], P, 2 * D)).then_inc(dve_h, 1)
                dve.wait_ge(dve_h, (n + 1) * 2)
                norm_stats(list(range(n * HALF, (n + 1) * HALF)))
                for t in range(n * HALF, (n + 1) * HALF):
                    normalise(t, n + 1)

            xt_copy(0, 0, 0)
            settle()
            for t in range(T):
                if t + 1 < T:
                    xt_copy(t + 1, t + 1, (t + 1) % 2)
                dve.wait_ge(qkv_done, t + 1)
                bk = 2 + 2 * (t % 2)
                v.tensor_tensor(spk[:, t, :].rearrange("p (h n) -> p h n", h=2), ps[:, bk:bk + 2, 0:288],
                                thr[:, 0:3 * D].rearrange("p (h n) -> p h n", h=2), ALU.is_ge).then_inc(spk_ready, 1)
                if t >= 1:
                    dve.wait_ge(qtr_done, t)
                    v.tensor_copy(qT16[:, t - 1], ps[0:DH, 6, :].bitcast(BF16)[:, 0:2 * P].rearrange("p (c n) -> p c n", c=2)
                                  ).then_inc(qT_ready, 1)
            dve.wait_ge(qtr_done, T)
            v.tensor_copy(qT16[:, T - 1], ps[0:DH, 6, :].bitcast(BF16)[:, 0:2 * P].rearrange("p (c n) -> p c n", c=2)
                          ).then_inc(qT_ready, 1)
            for b in range(HALF):
                dve.wait_ge(kv_done, b + 1)
                if b >= 2:
                    dve.wait_ge(xa_done, b - 1)
                v.tensor_tensor(kv16[:, b % 2], bank(7, DH, 2 * DH).rearrange("p (c n) -> p c n", c=2),
                                spread(cst[0:DH, C_BD:C_BD + DH], 1, [DH, 2, DH]), ALU.mult).then_inc(kv_ready, 1)
                dve.wait_ge(xa_done, b + 1)
                if b >= 2:
                    dve.wait_ge(y3_done, 2 * (b - 1))
                v.tensor_scalar(s16[:, b % 2].rearrange("p h c n -> p (h c n)"), bank(2, DH),
                                float(HD) ** -0.125, 1.0, ALU.mult, ALU.is_ge).then_inc(s_ready, 1)
                for h in range(2):
                    n = 2 * b + h
                    t = b + h * HALF
                    dve.wait_ge(y3_done, n + 1)
                    did_(v.tensor_tensor(fire[:, h * D:(h + 1) * D], bank(4 + n % 2, P, D), thr[:, 3 * D:4 * D],
                                         ALU.is_ge))
                    settle()
                    v.tensor_tensor(H[:, t, :], H[:, t, :], fire[:, h * D:(h + 1) * D], ALU.add).then_inc(fire_done, 1)
                    dve.wait_ge(fire_done, n + 1)
                    norm_stats([t])
                    normalise(t, 2 + n + 1)

            def argmax_first(src, oh, best):
                did_(v.tensor_reduce(best, src, AX, ALU.max))
                settle()
                did_(v.tensor_tensor(oh, src, spread(best, 2, [P, T, E]), ALU.is_ge))
                settle()
                did_(v.tensor_tensor(rt[:], oh, spread(cst[:, C_E8:C_E8 + E], 1, [P, T, E]), ALU.mult))
                settle()
                did_(v.tensor_reduce(sm[:, 0, :], rt[:], AX, ALU.min))
                settle()
                did_(v.tensor_tensor(oh, spread(cst[:, C_E8:C_E8 + E], 1, [P, T, E]), spread(sm[:, 0, :], 2, [P, T, E]),
                                     ALU.is_equal))
                settle()

            def route(k, n0, order):
                nt = (NT0, NT1)[k]
                for i, t in enumerate(order):
                    xt_copy(t, n0 + i, (n0 + i) % 2)
                dve.wait_ge(logit_done, k + 1)
                src = bank(2, P, T * E).rearrange("p (t e) -> p t e", t=T)
                if k == 0:
                    dve.wait_ge(rw_in, 48)
                    did_(v.tensor_tensor(lg[:], src, spread(bsr[:], 1, [P, T, E]), ALU.add))
                else:
                    did_(v.tensor_copy(lg[:], src))
                settle()
                did_(v.tensor_reduce(sm[:, 1, :], lg[:], AX, ALU.max))
                settle()
                v.tensor_tensor(lg[:], lg[:], spread(sm[:, 1, :], 2, [P, T, E]), ALU.subtract).then_inc(shift_ready, 1)
                dve.wait_ge(exp_ready, k + 1)
                did_(v.tensor_reduce(sm[:, 2, :], pr[:], AX, ALU.add))
                settle()
                did_(v.reciprocal(sm[:, 3, :], sm[:, 2, :]))
                settle()
                did_(v.tensor_tensor(pr[:], pr[:], spread(sm[:, 3, :], 2, [P, T, E]), ALU.mult))
                settle()
                argmax_first(pr[:], tops[0][:], pmax[:, 0, :])
                if k == 0:
                    v.tensor_copy(oh16[:], tops[0][:].rearrange("p t e -> p (t e)")).then_inc(oh_ready, 1)
                else:
                    did_(v.scalar_tensor_tensor(ohs[:], tops[0][:], -2.0, pr[:], ALU.mult, ALU.add))
                    settle()
                    argmax_first(ohs[:], tops[1][:], sm[:, 4, :])
                    v.tensor_tensor(oh16[:].rearrange("p (t e) -> p t e", t=T), tops[0][:], tops[1][:], ALU.add
                                    ).then_inc(oh_ready, 1)
                    v.tensor_reduce(rt[:, 0, :], pr[:].rearrange("p t e -> p e t"), AX, ALU.add).then_inc(imp_ready, 1)
                    dve.wait_ge(imp_done, 1)
                    did_(v.tensor_scalar(cnt[:, 0, :], bank(5, P, E), 1.0, 1.0 - 0.9, ALU.subtract, ALU.mult))
                    settle()
                    did_(v.tensor_scalar(cnt[:, 0, :], cnt[:, 0, :], 1.0, 0.01, ALU.add, ALU.add))
                    settle()
                    did_(v.reciprocal(cnt[:, 0, :], cnt[:, 0, :]))
                    settle()
                    did_(v.tensor_tensor(ohs[:], pr[:], spread(cnt[:, 0, :], 1, [P, T, E]), ALU.mult))
                    settle()
                    for j in range(2):
                        did_(v.tensor_tensor(rt[:], tops[j][:], ohs[:], ALU.mult))
                        settle()
                        did_(v.tensor_reduce(pmax[:, j, :], rt[:], AX, ALU.add))
                        settle()
                    did_(v.tensor_tensor(pmax[:, 2, :], pmax[:, 0, :], pmax[:, 1, :], ALU.add))
                    settle()
                    did_(v.reciprocal(pmax[:, 2, :], pmax[:, 2, :]))
                    settle()
                    for j in range(2):
                        did_(v.tensor_tensor(pmax[:, j, :], pmax[:, j, :], pmax[:, 2, :], ALU.mult))
                    settle()
                dve.wait_ge(rank_done, k + 1)
                did_(v.tensor_scalar(cnti[:], bank(4, P, E), float(P - 1), None, ALU.add))
                settle()
                did_(v.tensor_scalar(cnti[:], cnti[:], -P, None, ALU.bitwise_and))
                settle()
                did_(v.tensor_copy(cnt[:, 1, :], cnti[:]))
                settle()
                did_(v.tensor_tensor(cum[:], spread(cnt[:, 1, :], 1, [P, E, E]),
                                     cst[:, C_TRI8:C_TRI8 + E * E].rearrange("p (e f) -> p e f", e=E), ALU.mult))
                settle()
                did_(v.tensor_reduce(cnt[:, 2, :], cum[:], AX, ALU.add))
                settle()
                did_(v.tensor_tensor(cnt[:, 3, :], cnt[:, 2, :], cnt[:, 1, :], ALU.subtract))
                did_(v.tensor_tensor(jmap[:, 0:nt, :],
                                     cst[:, C_J128:C_J128 + nt * (E - 1)].rearrange("p (j e) -> p j e", j=nt),
                                     spread(cnt[:, 2, 0:E - 1], 1, [P, nt, E - 1]), ALU.is_ge))
                settle()
                did_(v.tensor_reduce(texp[:, 0:nt], jmap[:, 0:nt, :], AX, ALU.add))
                did_(v.tensor_tensor(lg[:], bank(3, P, T * E).rearrange("p (t e) -> p t e", t=T),
                                     spread(cnt[:, 3, :], 1, [P, T, E]), ALU.add))
                settle()
                did_(v.tensor_copy(texpi[k][:, 0:nt], texp[:, 0:nt]))
                K = k + 1
                for j in range(K):
                    did_(v.tensor_tensor(rt[:], lg[:], tops[j][:], ALU.mult))
                    settle()
                    did_(v.tensor_reduce(slot[:, 0, j * T:(j + 1) * T], rt[:], AX, ALU.add))
                    settle()
                n = K * T
                did_(v.tensor_copy(sloti[:, 0, 0:n], slot[:, 0, 0:n]))
                settle()
                did_(v.tensor_scalar(sloti[:, 1, 0:n], sloti[:, 0, 0:n], P - 1, None, ALU.bitwise_and))
                did_(v.tensor_scalar(sloti[:, 2, 0:n], sloti[:, 0, 0:n], 7, None, ALU.arith_shift_right))
                settle()
                did_(v.tensor_copy(slot[:, 1:3, 0:n], sloti[:, 1:3, 0:n]))
                settle()
                did_(v.tensor_tensor(AB[:, 0:n, 1, 0:nt], spread(cst[:, C_J:C_J + nt], 1, [P, n, nt]),
                                     spread(slot[:, 2, 0:n], 2, [P, n, nt]), ALU.is_equal))
                settle()
                did_(v.tensor_tensor(AB[:, 0:n, 0, 0:nt], AB[:, 0:n, 1, 0:nt],
                                     spread(cst[:, C_TOK:C_TOK + n], 2, [P, n, nt]), ALU.mult))
                settle()
                for i in range(n):
                    if i >= 2 or k == 1:
                        dve.wait_ge(inv_done, T * k + i - 1)
                    v.tensor_scalar(ohr[:, i % 2, :], cst[:, C_IOTA:C_IOTA + P], slot[:, 1, i:i + 1], None, ALU.is_equal
                                    ).then_inc(ohr_ready, 1)
                dve.wait_ge(inv_done, T * k + n)
                did_(v.tensor_copy(dmp[:, 0:2, 0:nt], bank(6, P, 2 * nt).rearrange("p (a j) -> p a j", a=2)))
                settle()
                did_(v.tensor_copy(gid[k][:, 0:nt], dmp[:, 0, 0:nt]))
                did_(v.tensor_scalar(dmp[:, 2, 0:nt], dmp[:, 1, 0:nt], -1.0, 1.0, ALU.mult, ALU.add))
                settle()
                did_(v.tensor_tensor(dmp[:, 2, 0:nt], dmp[:, 2, 0:nt], cst[:, C_ROW:C_ROW + nt], ALU.mult))
                settle()
                did_(v.tensor_tensor(did[k][:, 0:nt], dmp[:, 2, 0:nt], dmp[:, 0, 0:nt], ALU.add))
                settle()
                v.tensor_scalar(gid[k][:, 0:nt], gid[k][:, 0:nt], ROWS - 1, None, ALU.bitwise_and).then_inc(map_ready, 1)

            def mlp(k):
                m = ffn[k]
                n, F = ((NT0, F0), (NT1, F1))[k]
                C = F // P
                dve.wait_ge(map_ready, k + 1)
                if k == 0:
                    dve.wait_ge(wa_in, 16 * (2 * E + 2))

                def xt(s, b, prior):
                    dve.wait_ge(m["xt"], s + 1)
                    if prior:
                        dve.wait_ge(m["up"], s - 1)
                    v.tensor_copy(xgT[0:DH, b, :, :], bank(0, DH, 2 * P).rearrange("p (c n) -> p c n", c=2)
                                  ).then_inc(m["xgT"], 1)

                def ht(s, b, prior):
                    dve.wait_ge(m["htr"], s + 1)
                    if prior:
                        dve.wait_ge(m["down"], s - 1)
                    v.tensor_copy(hT[:, b, 0:C, :].rearrange("p c n -> p (c n)"),
                                  ps[:, 6:8, :].rearrange("p a n -> p (a n)")[:, 0:F]).then_inc(m["hT"], 1)

                def y(s, b, half, prior):
                    dve.wait_ge(m["down"], s + 1)
                    if prior:
                        dve.wait_ge(m[f"put{b}"], half * 16)
                    if k == 0:
                        e = dve.value_load(texpi[k][0:1, bass.ds(s, 1)], min_val=0, max_val=E - 1)
                        v.tensor_tensor(ys[:, b, :], bank(1, P, D), b2a[:, bass.ds(e * D, D)], ALU.add
                                        ).then_inc(m["y"], 1)
                    else:
                        v.tensor_copy(ys[:, b, :], bank(1, P, D)).then_inc(m["y"], 1)

                xt(0, 0, False)
                xt(1, 1, False)
                xt(2, 0, True)
                ht(0, 0, False)
                xt(3, 1, True)
                ht(1, 1, False)
                y(0, 0, 0, False)
                xt(4, 0, True)
                ht(2, 0, True)
                y(1, 1, 0, False)
                with dve.Fori(0, (n - 5) // 2) as i:
                    for b in range(2):
                        s = 2 * i + (4 + b)
                        xt(s + 1, 1 - b, True)
                        ht(s - 1, 1 - b, True)
                        y(s - 2, b, i + 1, True)
                ht(n - 2, 1, True)
                y(n - 3, 0, (n - 3) // 2, True)
                ht(n - 1, 0, True)
                y(n - 2, 1, (n - 3) // 2, True)
                y(n - 1, 0, (n - 1) // 2, True)

            route(0, T, PAIRS)
            mlp(0)

            m = ffn[0]
            v.memset(qkp.rearrange("p u a h j -> p (u a h j)"), 0.0).then_inc(gates_init, 1)
            dve.wait_ge(m["back"], 16 * T)
            for t in range(T):
                did_(v.scalar_tensor_tensor(H[:, t, :], xn[:, t, :], pmax[:, 0, t:t + 1], H[:, t, :], ALU.mult, ALU.add))
                settle()
                norm_stats([t])
                if t >= 1:
                    normalise(t - 1, 2 + T + t)
            normalise(T - 1, 2 + T + T)
            dve.wait_ge(lw_in, 96)
            dve.wait_ge(act_done, HEADS + 2)
            v.tensor_tensor(dec[:], dec[:], spread(cst[:, C_KEEP:C_KEEP + P], 1, [P, HEADS, P]), ALU.mult
                            ).then_inc(dec_ready, 1)
            dve.wait_ge(dec_ready, 1)
            N2 = 2 * T

            def finish(t):
                dve.wait_ge(wo_done, t + 1)
                src = bank(0, P, D, 256)
                did_(v.bn_stats(stats[:, t, :], src))
                settle()
                did_(v.bn_aggr(mv[:, t, :], stats[:, t, :]))
                settle()
                v.tensor_scalar(var_eps[:, t:t + 1], mv[:, t, 1:2], LN_EPS, None, ALU.add).then_inc(var_ready, 1)
                dve.wait_ge(rstd_ready, 2 + 2 * T + 2 * t + 1)
                v.tensor_scalar(cross, src, mv[:, t, 0:1], rstd[:, t:t + 1], ALU.subtract, ALU.mult).then_inc(attn_out, 1)
                dve.wait_ge(attn_out, t + 1)
                did_(v.tensor_tensor(cross, cross, lnw[:, 0, :], ALU.mult))
                settle()
                did_(v.tensor_tensor(cross, cross, lnw[:, 1, :], ALU.add))
                settle()
                did_(v.tensor_tensor(H[:, t, :], H[:, t, :], cross, ALU.add))
                settle()
                norm_stats([t])
                normalise(t, 2 + 2 * T + 2 * t + 2)

            for t in range(T):
                u = t % 2
                xt_copy(t, N2 + t, 0)
                if t >= 1:
                    dve.wait_ge(ot_done, t)
                    v.tensor_copy(oT[0:DH, 1 - u].rearrange("p c n -> p (c n)"), bank(0, DH, 2 * P)).then_inc(oT_ready, 1)
                    finish(t - 1)
                if t < HALF:
                    dve.wait_ge(silu_ready, 2 * t + 2)
                    if t >= 1:
                        dve.wait_ge(kvs_done, t)
                    v.tensor_tensor(kd[:], qkp[:, u, 1], spread(dkq[:, 0, :], 2, [P, HEADS, HPAD]), ALU.mult
                                    ).then_inc(kd_ready, 1)
                dve.wait_ge(tr2_done, t + 1)
                if t >= 2:
                    dve.wait_ge(pv_done, t - 1)
                did_(v.tensor_copy(qkT[:, u, 0:3].rearrange("p g n -> p (g n)"), bank(2, P, 3 * P)))
                did_(v.tensor_copy(g1T[0:16, u, :], bank(2, 16, P, 3 * P)))
                settle()
                v.tensor_copy(qkT[:, u, 3:6].rearrange("p g n -> p (g n)"), bank(3, P, 3 * P)).then_inc(tr2_ready, 1)
                if t < HALF:
                    dve.wait_ge(kvs_done, t + 1)
                    v.tensor_tensor(kvs[:, t], bank(2, P, D).rearrange("p (g n) -> p g n", g=HG),
                                    spread(cst[:, C_BDP:C_BDP + 64], 1, [P, HG, 64]), ALU.mult).then_inc(kvs_ready, 1)
                for i in range(4):
                    dve.wait_ge(sc_done, 4 * t + i + 1)
                    if i == 0 and t >= 1:
                        dve.wait_ge(pv_done, t)
                    v.tensor_tensor(pt[:, i], bank(4 + i, P, HG * P).rearrange("p (g n) -> p g n", g=HG),
                                    dec[:, i * HG:(i + 1) * HG, :], ALU.mult).then_inc(pt_ready, 1)
                dve.wait_ge(pv_done, t + 1)
                o = og[:, u, :]
                if t >= HALF:
                    did_(v.tensor_tensor(cross.rearrange("p (h j) -> p h j", h=HEADS),
                                         bank(1, P, D, 256).rearrange("p (h j) -> p h j", h=HEADS),
                                         spread(dkq[:, 1, :], 2, [P, HEADS, HD]), ALU.mult))
                    settle()
                    did_(v.tensor_tensor(cross, cross, bank(1, P, D), ALU.add))
                else:
                    did_(v.tensor_copy(cross, bank(1, P, D)))
                dve.wait_ge(gate_ready, t + 1)
                did_(v.tensor_scalar(gate[:, u, :], gate[:, u, :], 1.0, 0.5, ALU.add, ALU.mult))
                settle()
                v.tensor_tensor(o, cross, gate[:, u, :], ALU.mult).then_inc(og_ready, 1)
            dve.wait_ge(ot_done, T)
            v.tensor_copy(oT[0:DH, 1].rearrange("p c n -> p (c n)"), bank(0, DH, 2 * P)).then_inc(oT_ready, 1)
            finish(T - 1)

            route(1, 3 * T, list(range(T)))
            mlp(1)
            dve.wait_ge(ffn[1]["back"], 16 * 2 * T)
            for t in range(T):
                did_(v.scalar_tensor_tensor(H[:, t, :], back1[:, 0, t, :], pmax[:, 0, t:t + 1], H[:, t, :],
                                            ALU.mult, ALU.add))
            settle()
            for t in range(T):
                v.scalar_tensor_tensor(H[:, t, :], back1[:, 1, t, :], pmax[:, 1, t:t + 1], H[:, t, :],
                                       ALU.mult, ALU.add).then_inc(final, 1)


def layouts(i):
    x = i["x"]
    c = np.ascontiguousarray

    def pixels(p):
        h = IMG // p
        t = x.reshape(IMAGES, CH, h, p, h, p).transpose(2, 4, 3, 5, 1, 0)
        return c(t.reshape(h * h, IMAGES * p * p * CH))

    def halves(w):
        return c(w.reshape(2, DH, -1).transpose(1, 0, 2))

    r = {"cst": constants(), "x0": pixels(1), "x1": pixels(2), "x2": pixels(4)}
    r["idx0"] = c(i["L0_tok_idx0"].reshape(2, P, GP).transpose(1, 0, 2).reshape(P, 2 * GP))
    r["idx1"] = c(i["L0_tok_idx1"].reshape(L1, 2, 8).transpose(1, 0, 2).reshape(P, 8))
    r["idx2"] = c(i["L0_tok_idx2"].reshape(L2, 8, 2).transpose(1, 0, 2).reshape(P, 2))
    r["w0t"] = c(i["L0_tok_W0"].T)
    r["w1t"] = c(i["L0_tok_W1"].T.reshape(2, DH, EMBED).transpose(1, 0, 2).reshape(DH, -1))
    r["w2t"] = c(i["L0_tok_W2"].T.reshape(8, DH, EMBED).transpose(1, 0, 2).reshape(DH, -1))
    r["tb"] = c(np.stack([i[f"L0_tok_b{k}"] for k in range(3)], 1))
    r["wft"] = c(i["L0_tok_Wf"].T.reshape(3, EMBED, D).transpose(1, 0, 2).reshape(EMBED, -1))
    r["bf"] = c(i["L0_tok_bf"].reshape(1, D))
    r["bn"] = c(np.stack([i[f"L0_attn_{n}"].reshape(-1) for n in ("bn_gamma", "bn_beta", "bn_mean", "bn_var", "b")]))
    w = i["L0_attn_W"]
    r["wqkv"] = halves(w[0:3].transpose(2, 0, 1).reshape(D, 3 * D))
    r["w3"] = halves(w[3].T)
    r["ws"] = halves(i["L0_ffn_Ws"])
    r["bs"] = c(i["L0_ffn_bs"])
    r["wr"] = halves(i["L1_ffn_router_w"].T)
    r["w1a"] = c(i["L0_ffn_W1"].reshape(E, 2, DH, F0).transpose(2, 1, 0, 3))
    r["b1a"] = c(i["L0_ffn_b1"].reshape(1, E, F0))
    r["w2a"] = c(i["L0_ffn_W2"].reshape(E, F0 // P, P, D).transpose(2, 0, 1, 3))
    r["b2a"] = c(i["L0_ffn_b2"].reshape(-1))
    r["w1b"] = c(i["L1_ffn_w1"].transpose(0, 2, 1).reshape(E, 2, DH, F1).transpose(2, 1, 0, 3))
    r["w2b"] = c(i["L1_ffn_w2"].transpose(0, 2, 1).reshape(E, F1 // P, P, D).transpose(2, 0, 1, 3))
    r["wqk2"] = halves(np.concatenate([i[f"L1_attn_{n}"] for n in ("Wq", "Wk", "Wv", "Wg1")], 1))
    r["wg2"] = c(i["L1_attn_Wg2"])
    r["wo"] = halves(i["L1_attn_Wo"])
    r["lnw"] = c(i["L1_attn_ln_w"])
    r["lnb"] = c(i["L1_attn_ln_b"])
    r["ls"] = c(i["L1_attn_log_slope"])
    return r


def kernel(**inputs):
    import concourse.bacc as bacc
    from concourse.bass_utils import run_bass_kernel_spmd

    nc = bacc.Bacc("TRN2", target_bir_lowering=False, num_devices=1)
    arrays = {f"in_{n}": v for n, v in layouts({n: np.asarray(v) for n, v in inputs.items()}).items()}
    aps = {n[3:]: nc.dram_tensor(n, v.shape, mybir.dt.from_np(v.dtype), kind="ExternalInput").ap()
           for n, v in arrays.items()}
    out = nc.dram_tensor("out_rows", (ROWS, D), F32, kind="ExternalOutput").ap()
    build(nc, aps, out)
    r = run_bass_kernel_spmd(nc, [arrays], core_ids=[0])
    return r.results[0]["out_rows"].reshape(IMAGES, TOKENS, D)
```

```python
from contextlib import ExitStack

import numpy as np

import concourse.bass as bass
from concourse import mybir

F32 = mybir.dt.float32
BF16 = mybir.dt.bfloat16
I32 = mybir.dt.int32
ALU = mybir.AluOpType
ACT = mybir.ActivationFunctionType
AX = mybir.AxisListType.X

P = 128
IMAGES = 4
IMG = 64
CH = 3
GP = 16
EMBED = 64
D = 192
DH = 96
TOKENS = 256
T = IMAGES * TOKENS // P
HALF = T // 2
HEADS = 12
HD = D // HEADS
HPAD = 32
HG = 3
E = 8
F0 = 768
F1 = 512
LN_EPS = 1e-5
L1 = TOKENS // 4
L2 = TOKENS // 16
NT0 = T + E - 1
NT1 = 2 * T + E - 1
ROWS = T * P
XB = 4
AHEAD = 6
PAIRS = [u for t in range(HALF) for u in (t, t + HALF)]

C_ID = 0
C_TRI = C_ID + P
C_DIFF = C_TRI + P
C_KEEP = C_DIFF + P
C_IOTA = C_KEEP + P
C_A = C_IOTA + P
C_BD = C_A + TOKENS
C_BDP = C_BD + DH
C_E8 = C_BDP + 64
C_TRI8 = C_E8 + E
C_J = C_TRI8 + E * E
C_J128 = C_J + NT1
C_TOK = C_J128 + NT1 * (E - 1)
C_ROW = C_TOK + 2 * T
C_DK = C_ROW + NT1
C_DQ = C_DK + 1
C_END = C_DQ + 1


def constants():
    c = np.zeros((P, C_END), np.float32)
    p = np.arange(P)
    c[:, C_ID:C_ID + P] = np.eye(P)
    c[:, C_TRI:C_TRI + P] = p[:, None] < p[None, :]
    c[:, C_DIFF:C_DIFF + P] = np.maximum(p[None, :] - p[:, None], 0)
    c[:, C_KEEP:C_KEEP + P] = p[None, :] >= p[:, None]
    c[:, C_IOTA:C_IOTA + P] = p[None, :]
    for at, n in ((0, L1), (L1, L2)):
        pos = np.clip((np.arange(TOKENS, dtype=np.float32) + 0.5) * (n / TOKENS) - 0.5, 0.0, n - 1)
        i0 = np.floor(pos).astype(np.int64)
        i1 = np.minimum(i0 + 1, n - 1)
        w = (pos - i0).astype(np.float32)
        np.add.at(c, (at + i0, C_A + np.arange(TOKENS)), 1.0 - w)
        np.add.at(c, (at + i1, C_A + np.arange(TOKENS)), w)
    c[L1 + L2, C_A:C_A + TOKENS] = 1.0
    q = np.arange(DH)
    c[:DH, C_BD:C_BD + DH] = q[:, None] // HD == q[None, :] // HD
    c[:, C_BDP:C_BDP + 64] = p[:, None] // HPAD == np.arange(64)[None, :] // HD
    c[:, C_E8:C_E8 + E] = np.arange(E) - E
    c[:, C_TRI8:C_TRI8 + E * E] = np.tril(np.ones((E, E))).reshape(1, -1)
    c[:, C_J:C_J + NT1] = np.arange(NT1)
    c[:, C_J128:C_J128 + NT1 * (E - 1)] = np.repeat(np.arange(NT1) * P, E - 1)
    t = np.arange(T)
    row = (t % HALF) * TOKENS + (t // HALF) * P
    for k in range(2):
        c[:, C_TOK + k * T:C_TOK + (k + 1) * T] = k * ROWS + row[None, :] + p[:, None]
    c[:, C_ROW:C_ROW + NT1] = 2 * ROWS + np.arange(NT1) * P + p[:, None]
    c[:, C_DK] = P - 1 - p
    c[:, C_DQ] = p + 1
    return c


class Count:

    def __init__(self, engine, sem):
        self.engine, self.sem, self.n = engine, sem, 0

    def did(self, instruction):
        instruction.then_inc(self.sem, 1)
        self.n += 1
        return self.n

    def settle(self):
        self.engine.wait_ge(self.sem, self.n)


def spread(ap, axis, shape):
    return ap.unsqueeze(axis).to_broadcast(shape)


def build(nc, a, out):
    ctx = ExitStack()
    with ctx:
        def sb(name, shape, dt=F32):
            return ctx.enter_context(nc.sbuf_tensor(name, shape, dt))

        def sem(name):
            return ctx.enter_context(nc.semaphore(name))

        def dram(name, shape):
            return nc.dram_tensor(name, shape, F32, kind="Internal").ap()

        xn_rows = [dram(f"xn_rows{k}", (ROWS, D)) for k in range(2)]
        y_rows = [dram(f"y_rows{k}", (2 * ROWS + NT1 * P, D)) for k in range(2)]

        cst = sb("cst", [P, C_END])
        ones = sb("ones", [P, P])
        ones16 = sb("ones16", [P, P], BF16)
        ident16 = sb("ident16", [P, P], BF16)
        tri16 = sb("tri16", [P, P], BF16)
        H = sb("H", [P, T, D])
        xn = sb("xn", [P, T, D])
        xT = sb("xT", [DH, T, 2, P])
        NORMS = 5
        stats = sb("stats", [P, 2, 6])
        mv = sb("mv", [P, NORMS, T, 2])
        var_eps = sb("var_eps", [P, NORMS, T])
        rstd = sb("rstd", [P, NORMS, T])
        mhalf = sb("mhalf", [P, T])

        w1_space = sb("w1_space", [P, 2 * E * F0])
        w1a = w1_space[0:DH + 1, :].rearrange("p (c e f) -> p c e f", c=2, e=E)
        w2a = sb("w2a", [P, E, F0 // P, D])
        b2a = sb("b2a", [P, E * D])
        R1 = 2 * E * F1
        region = sb("region", [P, R1 + E * (F1 // P) * D])
        w1b = region[0:DH, 0:R1].rearrange("p (c e f) -> p c e f", c=2, e=E)
        w2b = region[:, R1:].rearrange("p (e f d) -> p e f d", e=E, f=F1 // P)
        taken = {"space": 0, "region": 0, "late": 0}

        def place(where, buffer, rows, n):
            lo = taken[where]
            taken[where] += n
            assert taken[where] <= buffer.shape[1], where
            return buffer[0:rows, lo:lo + n]

        def first(rows, n):
            return place("space", w1_space, rows, n)

        def early(rows, n):
            return place("region", region, rows, n)

        idx0 = sb("idx0", [P, 2 * GP], I32)
        idx1 = sb("idx1", [P, 8], I32)
        idx2 = sb("idx2", [P, 2], I32)
        g0 = first(P, 2 * GP * 12)
        g1 = first(P, 8 * 48)
        g2 = first(P, 2 * 192)
        t0 = first(48, 2 * 512)
        t1 = first(DH, 512)
        t2 = first(DH, 512)
        w0t = first(48, EMBED)
        w1t = first(DH, 2 * EMBED)
        w2t = first(DH, 8 * EMBED)
        tb = first(EMBED, 3)
        wft = first(EMBED, 3 * D)
        y0t = first(EMBED, 2 * 512)
        y12t = first(EMBED, IMAGES * (L1 + L2))
        zz = first(L1 + L2 + 1, IMAGES * D)
        bn = first(P, 5 * 4 * D)
        inv = early(P, 4 * D)
        thr = early(P, 4 * D)
        bn_t = first(P, 4 * D)
        wqkv = early(DH, 2 * 3 * D)
        w3 = first(DH, 2 * D)
        w3r = first(DH, 2 * D)
        w3s = early(DH, 3 * D).bitcast(BF16).rearrange("p (s c n) -> p s c n", s=3, c=2)
        spk = early(P, T * 3 * D // 2).bitcast(BF16).rearrange("p (t n) -> p t n", t=T)
        qT16 = early(DH, T * P).bitcast(BF16).rearrange("p (t c n) -> p t c n", t=T, c=2)
        kv16 = early(DH, HALF * DH).bitcast(BF16).rearrange("p (b c n) -> p b c n", b=HALF, c=2)
        s16 = early(DH, 2 * 2 * P).bitcast(BF16).rearrange("p (u h c n) -> p u h c n", u=2, h=2, c=2)
        fire = early(P, 2 * D)

        ws = sb("ws", [DH, 2, E])
        bsr = sb("bsr", [P, E])
        wr = sb("wr", [DH, 2, E])
        lg = sb("lg", [P, T, E])
        pr = sb("pr", [P, T, E])
        rt = sb("rt", [P, T, E])
        tops = [sb(f"top{k}", [P, T, E]) for k in range(2)]
        oh16 = sb("oh16", [P, T * E], BF16)
        ohs = sb("ohs", [P, T, E])
        sm = sb("sm", [P, 16, T])
        cnt = sb("cnt", [P, 4, E])
        cnti = sb("cnti", [P, E], I32)
        cum = sb("cum", [P, E, E])
        sloti = sb("sloti", [P, 3, 2 * T], I32)
        slot = sb("slot", [P, 3, 2 * T])
        texp = sb("texp", [P, NT1])
        texpi = [sb(f"texpi{k}", [P, NT1], I32) for k in range(2)]
        dmp = sb("dmp", [P, 3, NT1])
        gid = [sb(f"gid{k}", [P, NT1], I32) for k in range(2)]
        did = [sb(f"did{k}", [P, NT1], I32) for k in range(2)]
        pmax = sb("pmax", [P, 3, T])

        xg = sb("xg", [P, XB, D])
        xgT = sb("xgT", [DH + 1, 2, 2, P])
        hs = sb("hs", [P, 2, F0])
        hT = sb("hT", [P, 2, F0 // P, P])
        ys = sb("ys", [P, 2, D])
        AB = hs[:, 0, 0:2 * T * 2 * NT1].rearrange("p (i a j) -> p i a j", i=2 * T, a=2)
        jmap = hs[:, 1, 0:NT1 * (E - 1)].rearrange("p (j e) -> p j e", j=NT1)
        ohr = hT[:, 0, 0:2, :]

        wqk2 = sb("wqk2", [DH, 2, 3 * D + 16])
        wg2 = sb("wg2", [16, D])
        wo = sb("wo", [DH, 2, D])
        lnw = sb("lnw", [P, 2, D])
        ls = sb("ls", [P, HEADS])
        dkq = sb("dkq", [P, 2, HEADS])
        qk = w2a[:, :, :, :].rearrange("p e f d -> p (e f d)")

        def over2(n):
            return place("late", qk, P, n)

        qkp = over2(2 * 2 * HEADS * HPAD).rearrange("p (u a h j) -> p u a h j", u=2, a=2, h=HEADS)
        dec = over2(HEADS * P).rearrange("p (h n) -> p h n", h=HEADS)
        kd = over2(HEADS * HPAD).rearrange("p (h j) -> p h j", h=HEADS)
        v2 = over2(2 * (D + 16)).rearrange("p (u n) -> p u n", u=2)
        qkT = over2(2 * 6 * P).rearrange("p (u g n) -> p u g n", u=2, g=6)
        g1T = over2(2 * P).rearrange("p (u n) -> p u n", u=2)
        pt = over2(HEADS * P).rearrange("p (i g n) -> p i g n", i=4, g=HG)
        kvs = over2(HALF * D).rearrange("p (b g n) -> p b g n", b=HALF, g=HG)
        ao = ys
        cross = xg[:, 0, 0:D]
        gate = hs[:, :, 0:D]
        og = hs[:, :, D:2 * D]
        oT = hT[:, :, 0:2, :]

        ps = ctx.enter_context(nc.psum_tensor("ps", [P, 8, 512], F32))

        def bank(i, rows=P, n=512, lo=0):
            return ps[0:rows, i, lo:lo + n]

        ident = cst[:, C_ID:C_ID + P]

        cst_in = sem("cst_in")
        tokw_in = sem("tokw_in")
        idx_in = sem("idx_in")
        g2_in = sem("g2_in")
        g1_in = sem("g1_in")
        g0_in = [sem(f"g0_in{n}") for n in range(2)]
        bn_in = sem("bn_in")
        aw_in = sem("aw_in")
        rw_in = sem("rw_in")
        lw_in = sem("lw_in")
        wa_in = sem("wa_in")
        wb_in = sem("wb_in")
        consts_ready = sem("consts_ready")
        mhalf_ready = sem("mhalf_ready")
        dve_done = sem("dve_done")
        act_done = sem("act_done")
        pe_t = sem("tok_transposed")
        dve_t = sem("tok_copied")
        pe_y = sem("tok_level_done")
        dve_y = sem("tok_level_copied")
        pe_z = sem("z_done")
        dve_z = sem("z_copied")
        pe_h = sem("h_done")
        dve_h = sem("h_copied")
        var_ready = [sem(f"var_ready{k}") for k in range(NORMS)]
        rstd_ready = [sem(f"rstd_ready{k}") for k in range(NORMS)]
        xn_ready = sem("xn_ready")
        xn_last = sem("xn_last")
        pe_xt = sem("xt_done")
        xt_ready = sem("xt_ready")
        bnw_ready = sem("bnw_ready")
        bn_root = sem("bn_root")
        bn_var = sem("bn_var")
        qkv_done = sem("qkv_done")
        spk_ready = sem("spk_ready")
        qtr_done = sem("qtr_done")
        qT_ready = sem("qT_ready")
        kv_done = sem("kv_done")
        kv_ready = sem("kv_ready")
        xa_done = sem("xa_done")
        s_ready = sem("s_ready")
        y3_done = sem("y3_done")
        fired = sem("fired")
        fire_done = sem("fire_done")
        logit_done = sem("logit_done")
        shift_ready = sem("shift_ready")
        exp_ready = sem("exp_ready")
        oh_ready = sem("oh_ready")
        rank_done = sem("rank_done")
        imp_ready = sem("imp_ready")
        imp_done = sem("imp_done")
        ohr_ready = sem("ohr_ready")
        inv_done = sem("inv_done")
        map_ready = sem("map_ready")
        xrow_out = sem("xrow_out")
        dec_ready = sem("dec_ready")
        dk_ready = sem("dk_ready")
        proj_done = sem("proj_done")
        silu_ready = sem("silu_ready")
        g1_ready = sem("g1_ready")
        tr2_done = sem("tr2_done")
        tr2_ready = sem("tr2_ready")
        gate_done = sem("gate_done")
        gate_ready = sem("gate_ready")
        kd_ready = sem("kd_ready")
        kvs_done = sem("kvs_done")
        kvs_ready = sem("kvs_ready")
        sc_done = sem("scores_done")
        pt_ready = sem("pt_ready")
        pv_done = sem("pv_done")
        og_ready = sem("og_ready")
        ot_done = sem("ot_done")
        oT_ready = sem("oT_ready")
        wo_done = sem("wo_done")
        attn_out = sem("attn_out")
        final = sem("final")
        stored = sem("stored")
        gates_init = sem("gates_init")
        ao_ready = sem("ao_ready")
        pool_done = sem("pool_done")
        res_ready = sem("res_ready")
        kT_ready = sem("kT_ready")
        ffn = []
        for k in range(2):
            ffn.append({n: sem(f"m{k}_{n}") for n in (
                "rows0", "rows1", "rows2", "rows3", "xt", "xgT", "up", "act", "htr", "hT", "down", "y",
                "put0", "put1")})
        back = [[sem(f"back{k}_{t}") for t in range(T)] for k in range(2)]

        block = ctx.enter_context(nc.Block())

        back0 = xn[:, :, :].unsqueeze(1)
        back1 = qk[:, 0:2 * T * D].rearrange("p (k t d) -> p k t d", k=2, t=T)

        @block.sync
        def _(sp):
            sp.dma_start(idx2[:], a["idx2"]).then_inc(idx_in, 16)
            sp.dma_start(idx1[:], a["idx1"]).then_inc(idx_in, 16)
            sp.dma_start(idx0[:], a["idx0"]).then_inc(idx_in, 16)
            sp.dma_start(cst[:], a["cst"]).then_inc(cst_in, 16)
            sp.dma_start(w0t, a["w0t"]).then_inc(tokw_in, 16)
            sp.dma_start(w1t, a["w1t"]).then_inc(tokw_in, 16)
            sp.dma_start(w2t, a["w2t"]).then_inc(tokw_in, 16)
            sp.dma_start(tb, a["tb"]).then_inc(tokw_in, 16)
            sp.dma_start(wft, a["wft"]).then_inc(tokw_in, 16)
            sp.dma_start(zz[L1 + L2:L1 + L2 + 1, :].rearrange("p (b n) -> p b n", b=IMAGES),
                         spread(a["bf"], 1, [1, IMAGES, D])).then_inc(tokw_in, 16)
            for i in range(5):
                sp.dma_start(bn[:, i * 4 * D:(i + 1) * 4 * D],
                             a["bn"][i, :].partition_broadcast(P)).then_inc(bn_in, 16)
            sp.dma_start(wqkv.rearrange("p (c n) -> p c n", c=2), a["wqkv"]).then_inc(aw_in, 16)
            sp.dma_start(w3.rearrange("p (c n) -> p c n", c=2), a["w3"]).then_inc(aw_in, 16)
            sp.dma_start(ws[:], a["ws"]).then_inc(rw_in, 16)
            sp.dma_start(wr[:], a["wr"]).then_inc(rw_in, 16)
            sp.dma_start(bsr[:], a["bs"].partition_broadcast(P)).then_inc(rw_in, 16)
            for e in range(E):
                sp.dma_start(w2a[:, e, :, :], a["w2a"][:, e, :, :]).then_inc(wa_in, 16)
            sp.wait_ge(dve_h, T // 2)
            sp.wait_ge(bnw_ready, 3)
            for e in range(E):
                sp.dma_start(w1a[0:DH, :, e, :], a["w1a"][:, :, e, :]).then_inc(wa_in, 16)
            sp.dma_start(w1a[DH:DH + 1, 0, :, :], a["b1a"]).then_inc(wa_in, 16)
            sp.dma_start(b2a[:], a["b2a"].partition_broadcast(P)).then_inc(wa_in, 16)
            sp.dma_start(wqk2[:], a["wqk2"]).then_inc(lw_in, 16)
            sp.dma_start(wg2[:], a["wg2"]).then_inc(lw_in, 16)
            sp.dma_start(wo[:], a["wo"]).then_inc(lw_in, 16)
            sp.dma_start(lnw[:, 0, :], a["lnw"].partition_broadcast(P)).then_inc(lw_in, 16)
            sp.dma_start(lnw[:, 1, :], a["lnb"].partition_broadcast(P)).then_inc(lw_in, 16)
            sp.dma_start(ls[:], a["ls"].partition_broadcast(P)).then_inc(lw_in, 16)

            def rows_of(dram_rows, t):
                lo = (t % HALF) * TOKENS + (t // HALF) * P
                return dram_rows[lo:lo + P, :]

            for k, (ready, before) in enumerate(((xn_ready, T), (xn_last, 0))):
                m = ffn[k]
                for i, t in enumerate((PAIRS, range(T))[k]):
                    sp.wait_ge(ready, before + i + 1)
                    sp.dma_start(rows_of(xn_rows[k], t), xn[:, t, :]).then_inc(xrow_out, 16)
                if k == 0:
                    sp.wait_ge(fire_done, T)
                    for e in range(E):
                        sp.dma_start(w1b[:, :, e, :], a["w1b"][:, :, e, :]).then_inc(wb_in, 16)
                        sp.dma_start(w2b[:, e, :, :], a["w2b"][:, e, :, :]).then_inc(wb_in, 16)
                n = (NT0, NT1)[k]
                sp.wait_ge(m["put0"], 16 * ((n + 1) // 2))
                sp.wait_ge(m["put1"], 16 * (n // 2))
                dst = (back0, back1)[k]
                for t in range(T):
                    for j in range(k + 1):
                        sp.dma_start(dst[:, j, t, :],
                                     y_rows[k][j * ROWS + (t % HALF) * TOKENS + (t // HALF) * P:][0:P, :]
                                     ).then_inc(back[k][t], 16)
            for t in range(T):
                sp.wait_ge(final, t + 1)
                sp.dma_start(rows_of(out, t), H[:, t, :]).then_inc(stored, 16)
            sp.wait_ge(stored, 16 * T)

        @block.gpsimd
        def _(pool):
            nc.gpsimd.memset(mhalf[:], -0.5).then_inc(mhalf_ready, 1)
            pool.wait_ge(idx_in, 48)
            for q in range(2):
                pool.indirect_dma_start(out=g2[:, q * 192:(q + 1) * 192], out_offset=None, in_=a["x2"],
                                        in_offset=bass.IndirectOffsetOnAxis(idx2[:, q:q + 1], 0)
                                        ).then_inc(g2_in, 16)
            for q in range(8):
                pool.indirect_dma_start(out=g1[:, q * 48:(q + 1) * 48], out_offset=None, in_=a["x1"],
                                        in_offset=bass.IndirectOffsetOnAxis(idx1[:, q:q + 1], 0)
                                        ).then_inc(g1_in, 16)
            for q in range(2 * GP):
                pool.indirect_dma_start(out=g0[:, q * 12:(q + 1) * 12], out_offset=None, in_=a["x0"],
                                        in_offset=bass.IndirectOffsetOnAxis(idx0[:, q:q + 1], 0)
                                        ).then_inc(g0_in[q // GP], 16)
            pool.wait_ge(mhalf_ready, 1)

            def root(norm, first, n, at):
                pool.wait_ge(var_ready[norm], at)
                nc.gpsimd.tensor_tensor(rstd[:, norm, first:first + n], var_eps[:, norm, first:first + n],
                                        mhalf[:, first:first + n], ALU.pow).then_inc(rstd_ready[norm], 1)

            def mlp(k):
                m = ffn[k]
                n = (NT0, NT1)[k]
                pool.wait_ge(xrow_out, 16 * T * (k + 1))
                pool.wait_ge(map_ready, k + 1)
                for s in range(n + AHEAD):
                    if s < n:
                        if s >= XB:
                            pool.wait_ge(m["xt"], s - XB + 1)
                        pool.indirect_dma_start(out=xg[:, s % XB, :], out_offset=None, in_=xn_rows[k],
                                                in_offset=bass.IndirectOffsetOnAxis(gid[k][:, s:s + 1], 0)
                                                ).then_inc(m[f"rows{s % XB}"], 16)
                    if s >= AHEAD:
                        j = s - AHEAD
                        pool.wait_ge(m["y"], j + 1)
                        pool.indirect_dma_start(out=y_rows[k],
                                                out_offset=bass.IndirectOffsetOnAxis(did[k][:, j:j + 1], 0),
                                                in_=ys[:, j % 2, :], in_offset=None
                                                ).then_inc(m[f"put{j % 2}"], 16)

            root(0, 0, HALF, 1)
            root(0, HALF, HALF, 2)
            for i, t in enumerate(PAIRS):
                root(1, t, 1, i + 1)
            mlp(0)
            for t in range(3):
                root(2, t, 1, t + 1)
            for t in range(T + 1):
                if t >= 1:
                    root(3, t - 1, 1, t)
                if t + 3 < T:
                    root(2, t + 3, 1, t + 4)
                if t >= 1:
                    o = ao[:, (t - 1) % 2, :]
                    pool.wait_ge(ao_ready, t)
                    nc.gpsimd.tensor_tensor(o, o, lnw[:, 0, :], ALU.mult).then_inc(pool_done, 1)
                    pool.wait_ge(pool_done, 2 * t - 1)
                    nc.gpsimd.tensor_tensor(o, o, lnw[:, 1, :], ALU.add).then_inc(pool_done, 1)
                    pool.wait_ge(pool_done, 2 * t)
                    nc.gpsimd.tensor_tensor(H[:, t - 1, :], H[:, t - 1, :], o, ALU.add).then_inc(res_ready, 1)
                    root(4, t - 1, 1, t)
            mlp(1)

        @block.tensor
        def _(pe):
            def mm(o, l, r, start=True, stop=True):
                return nc.tensor.matmul(o, l, r, start=start, stop=stop)

            def tr(o, i, idn):
                return nc.tensor.transpose(o, i, idn)

            pe.wait_ge(cst_in, 16)
            pe.wait_ge(g2_in, 32)
            for b in range(IMAGES):
                last = tr(bank(3, DH, P, b * P), g2.rearrange("p (f b) -> p b f", b=IMAGES)[:, b], ident)
            last.then_inc(pe_t, 1)
            pe.wait_ge(g1_in, 16 * 8)
            for b in range(IMAGES):
                last = tr(bank(2, DH, P, b * P), g1.rearrange("p (f b) -> p b f", b=IMAGES)[:, b], ident)
            last.then_inc(pe_t, 1)
            pe.wait_ge(tokw_in, 96)
            pe.wait_ge(dve_t, 1)
            for j in range(8):
                last = mm(bank(6, EMBED, IMAGES * L2, IMAGES * L1), w2t[:, j * EMBED:(j + 1) * EMBED],
                          t2.rearrange("p (b j n) -> p j b n", b=IMAGES, j=8)[:, j], j == 0, j == 7)
            pe.wait_ge(dve_t, 2)
            for j in range(2):
                last = mm(bank(6, EMBED, IMAGES * L1), w1t[:, j * EMBED:(j + 1) * EMBED],
                          t1.rearrange("p (b j n) -> p j b n", b=IMAGES, j=2)[:, j], j == 0, j == 1)
            last.then_inc(pe_y, 1)
            pe.wait_ge(dve_y, 2)
            for b in range(IMAGES):
                bk = (7, 2, 3, 6)[b]
                mm(bank(bk, L1, D), y12t[:, b * L1:(b + 1) * L1], wft[:, D:2 * D])
                mm(bank(bk, L2, D, D), y12t[:, IMAGES * L1 + b * L2:IMAGES * L1 + (b + 1) * L2],
                   wft[:, 2 * D:3 * D]).then_inc(pe_z, 1)
            def level0(n):
                pe.wait_ge(g0_in[n], 16 * GP)
                if n == 1:
                    pe.wait_ge(xt_ready, HALF)
                for b in range(IMAGES):
                    last = tr(bank(n, 48, P, b * P),
                              g0.rearrange("p (n f b) -> p n b f", n=2, b=IMAGES)[:, n, b], ident)
                last.then_inc(pe_t, 1)
                pe.wait_ge(dve_t, 3 + n)
                if n == 1:
                    pe.wait_ge(spk_ready, HALF)
                mm(bank(4 + n, EMBED), w0t, t0[:, n * 512:(n + 1) * 512]).then_inc(pe_y, 1)
                pe.wait_ge(dve_y, 3 + n)
                pe.wait_ge(dve_z, 2 * IMAGES)
                for b in range(IMAGES):
                    o = bank(((4, 7), (3, 2))[n][b // 2], P, D, (b % 2) * D)
                    mm(o, y0t[:, n * 512 + b * P:n * 512 + (b + 1) * P], wft[:, 0:D], True, False)
                    last = mm(o, cst[0:L1 + L2 + 1, C_A + n * P:C_A + (n + 1) * P], zz[:, b * D:(b + 1) * D],
                              False, True)
                    if b % 2 == 1:
                        last.then_inc(pe_h, 1)

            def xtr(t, n, at, ready=xn_ready):
                pe.wait_ge(ready, at + 1)
                if n >= 2:
                    pe.wait_ge(xt_ready, n - 1)
                tr(bank(n % 2, DH, P), xn[:, t, 0:DH], ident)
                tr(bank(n % 2, DH, P, P), xn[:, t, DH:D], ident).then_inc(pe_xt, 1)

            def qkv(t):
                pe.wait_ge(xt_ready, t + 1)
                if t >= 2:
                    pe.wait_ge(spk_ready, t - 1)
                for h in range(2):
                    for c in range(2):
                        last = mm(bank(2 + 2 * (t % 2) + h, P, 288), xT[:, t, c, :],
                                  wqkv[:, c * 3 * D + h * 288:c * 3 * D + (h + 1) * 288], c == 0, c == 1)
                last.then_inc(qkv_done, 1)

            b6 = ps[:, 6, :].bitcast(BF16)

            def qtr(t):
                pe.wait_ge(spk_ready, t + 1)
                if t >= 1:
                    pe.wait_ge(qT_ready, t)
                for c in range(2):
                    last = tr(b6[0:DH, c * P:(c + 1) * P], spk[:, t, c * DH:(c + 1) * DH], ident16[:])
                last.then_inc(qtr_done, 1)

            for n in range(2):
                level0(n)
                if n == 0:
                    pe.wait_ge(consts_ready, 4)
                    pe.wait_ge(bnw_ready, 3)
                pe.wait_ge(dve_h, 2 * n + 2)
                lo = n * HALF
                xtr(lo, lo, lo)
                for t in range(lo, lo + HALF):
                    if t + 1 < lo + HALF:
                        xtr(t + 1, t + 1, t + 1)
                    qkv(t)
                    if t > lo:
                        qtr(t - 1)
                qtr(lo + HALF - 1)
            pe.wait_ge(qT_ready, T)
            for b in range(HALF):
                for c in range(2):
                    for t in (b, b + HALF):
                        last = mm(bank(6 + b // 2, DH, DH, ((b % 2) * 2 + c) * DH), spk[:, t, D + c * DH:D + (c + 1) * DH],
                                  spk[:, t, 2 * D + c * DH:2 * D + (c + 1) * DH], t == b, t != b)
                if b % 2 == 1:
                    last.then_inc(kv_done, 1)

            def xa(b):
                pe.wait_ge(kv_ready, b + 1)
                for h in range(2):
                    for c in range(2):
                        last = mm(bank(2 + b, DH, P, (h * 2 + c) * P), kv16[:, b, c, :], qT16[:, b + h * HALF, c, :])
                last.then_inc(xa_done, 1)

            def y3(b):
                pe.wait_ge(s_ready, b + 1)
                for h in range(2):
                    n = 2 * b + h
                    if n >= 2:
                        pe.wait_ge(fired, n - 1)
                    i = 0
                    for part in range(3):
                        for c in range(2):
                            last = mm(bank(6 + n % 2, P, D), s16[:, b % 2, h, c, :], w3s[:, part, c, :], i == 0, i == 5)
                            i += 1
                    last.then_inc(y3_done, 1)

            pe.wait_ge(spk_ready, T)
            xa(0)
            xa(1)
            pe.wait_ge(kv_ready, HALF)
            y3(0)
            xa(2)
            y3(1)
            xa(3)
            y3(2)
            y3(3)

            def route(k, n0, base, order, w, ready):
                for i, t in enumerate(order):
                    xtr(t, n0 + i, base + i, ready)
                    pe.wait_ge(xt_ready, n0 + i + 1)
                    for c in range(2):
                        last = mm(bank(2, P, E, t * E), xT[:, t, c, :], w[:, c, :], c == 0, c == 1)
                last.then_inc(logit_done, 1)
                if k == 1:
                    pe.wait_ge(imp_ready, 1)
                    mm(bank(5, P, E), ones[:], rt[:, 0, :]).then_inc(imp_done, 1)
                pe.wait_ge(oh_ready, k + 1)
                for s in range(T):
                    last = mm(bank(3, P, (T - s) * E, s * E), tri16[:] if s == 0 else ones16[:],
                              oh16[:, 0:(T - s) * E], s == 0, s == T - 1)
                for t in range(T):
                    last = mm(bank(4, P, E), ones16[:], oh16[:, t * E:(t + 1) * E], t == 0, t == T - 1)
                last.then_inc(rank_done, 1)
                n = T * (k + 1)
                nt = (NT0, NT1)[k]
                done = T * k
                for i in range(n):
                    pe.wait_ge(ohr_ready, done + i + 1)
                    mm(bank(6, P, 2 * nt), ohr[:, i % 2, :], AB[:, i, :, 0:nt], i == 0, i == n - 1
                       ).then_inc(inv_done, 1)

            def mlp(k):
                m = ffn[k]
                n, F = ((NT0, F0), (NT1, F1))[k]
                w1, w2, rows = ((w1a, w2a, DH + 1), (w1b, w2b, DH))[k]
                C = F // P
                NH = (2, 1)[k]
                W = F // NH

                def expert(s):
                    return pe.value_load(texpi[k][0:1, bass.ds(s, 1)], min_val=0, max_val=E - 1)

                def xt(s, b, quarter):
                    pe.wait_ge(m[f"rows{b}"], (quarter + 1) * 16)
                    for c in range(2):
                        last = tr(bank(0, DH, P, c * P), xg[:, b, c * DH:(c + 1) * DH], ident)
                    last.then_inc(m["xt"], 1)

                def up(s, b, prior):
                    e = expert(s)
                    pe.wait_ge(m["xgT"], s + 1)
                    if prior:
                        pe.wait_ge(m["act"], s - 1)
                    for h in range(NH):
                        for c in range(2):
                            r = rows if c == 0 else DH
                            flat = w1[0:r, c, :, :].rearrange("p e f -> p (e f)")
                            last = mm(bank(2 + 2 * b + h, P, W), xgT[0:r, b, c, :],
                                      flat[:, bass.ds(e * F + h * W, W)], c == 0, c == 1)
                    last.then_inc(m["up"], 1)

                def htr(s, b, prior):
                    pe.wait_ge(m["act"], s + 1)
                    if prior:
                        pe.wait_ge(m["hT"], s)
                    for c in range(C):
                        last = tr(bank(6 + c // 4, P, P, (c % 4) * P), hs[:, b, c * P:(c + 1) * P], ident)
                    last.then_inc(m["htr"], 1)

                def down(s, b, prior):
                    e = expert(s)
                    pe.wait_ge(m["hT"], s + 1)
                    if prior:
                        pe.wait_ge(m["y"], s)
                    flat = w2[:, :, :, :].rearrange("p e f d -> p (e f d)")
                    for c in range(C):
                        last = mm(bank(1, P, D), hT[:, b, c, :], flat[:, bass.ds(e * (C * D) + c * D, D)],
                                  c == 0, c == C - 1)
                    last.then_inc(m["down"], 1)

                pe.wait_ge(map_ready, k + 1)
                pe.wait_ge((wa_in, wb_in)[k], (16 * (2 * E + 2), 16 * 2 * E)[k])
                xt(0, 0, 0)
                up(0, 0, False)
                xt(1, 1, 0)
                up(1, 1, False)
                xt(2, 2, 0)
                htr(0, 0, False)
                for s in range(2, XB):
                    up(s, s % 2, True)
                    xt(s + 1, (s + 1) % XB, (s + 1) // XB)
                    htr(s - 1, (s - 1) % 2, True)
                    down(s - 2, s % 2, s > 2)
                with pe.Fori(0, (n - XB) // XB) as i:
                    for b in range(XB):
                        s = XB * i + (XB + b)
                        up(s, b % 2, True)
                        xt(s + 1, (b + 1) % XB, i + (1 + (b + 1) // XB))
                        htr(s - 1, (b + 1) % 2, True)
                        down(s - 2, b % 2, True)
                for s in range(n // XB * XB, n + 2):
                    if s < n:
                        up(s, s % 2, True)
                    if s + 1 < n:
                        xt(s + 1, (s + 1) % XB, (s + 1) // XB)
                    if s <= n:
                        htr(s - 1, (s - 1) % 2, True)
                    down(s - 2, s % 2, True)

            pe.wait_ge(rw_in, 48)
            route(0, T, T, PAIRS, ws, xn_ready)
            mlp(0)

            pe.wait_ge(lw_in, 96)
            N2 = T * 2

            def inputs(t):
                pe.wait_ge(xn_ready, N2 + t + 1)
                if t >= 1:
                    pe.wait_ge(xt_ready, N2 + t)
                if t >= 3:
                    pe.wait_ge(attn_out, t - 2)
                tr(bank(0, DH, P), xn[:, t, 0:DH], ident)
                tr(bank(0, DH, P, P), xn[:, t, DH:D], ident).then_inc(pe_xt, 1)

            def proj(t):
                pe.wait_ge(xt_ready, N2 + t + 1)
                if t >= 1:
                    pe.wait_ge(gate_ready, t)
                    pe.wait_ge(kvs_ready, min(t, HALF))
                for bk, lo, hi in ((2, 0, 2 * D), (3, 2 * D, 3 * D + 16)):
                    for c in range(2):
                        last = mm(bank(bk, P, hi - lo), xT[:, t, c, :], wqk2[:, c, lo:hi], c == 0, c == 1)
                last.then_inc(proj_done, 1)

            def tr2(t):
                u = t % 2
                pe.wait_ge(silu_ready, 2 * (t + 1))
                pe.wait_ge(g1_ready, t + 1)
                for g in range(HG):
                    tr(bank(2, P, P, g * P), qkp[:, u, 0, 4 * g:4 * g + 4, :], ident)
                tr(bank(2, 16, P, 3 * P), v2[:, u, D:D + 16], ident)
                for g in range(HG):
                    last = tr(bank(3, P, P, g * P), qkp[:, u, 1, 4 * g:4 * g + 4, :], ident)
                last.then_inc(tr2_done, 1)

            def gate_and_state(t):
                u = t % 2
                pe.wait_ge(tr2_ready, t + 1)
                pe.wait_ge(kT_ready, t + 1)
                mm(bank(3, P, D), g1T[0:16, u, :], wg2[:]).then_inc(gate_done, 1)
                if t < HALF:
                    pe.wait_ge(kd_ready, t + 1)
                    for g in range(HG):
                        last = mm(bank(2, P, 64, g * 64), kd[:, 4 * g:4 * g + 4, :], v2[:, u, g * 64:(g + 1) * 64])
                    last.then_inc(kvs_done, 1)

            def attend(t):
                u = t % 2
                for i in range(4):
                    if t >= 1:
                        pe.wait_ge(pt_ready, 4 * (t - 1) + i + 1)
                    rows = slice(i * HPAD, i * HPAD + HD)
                    for g in range(HG):
                        last = mm(bank(4 + i, P, P, g * P), qkT[rows, u, 3 + g, :], qkT[rows, u, g, :])
                    last.then_inc(sc_done, 1)

            def values(t):
                u = t % 2
                if t >= 1:
                    pe.wait_ge(og_ready, t)
                if t >= HALF:
                    pe.wait_ge(kvs_ready, t - HALF + 1)
                    for g in range(HG):
                        mm(bank(1, P, 64, 256 + g * 64), qkT[:, u, g, :], kvs[:, t - HALF, g, :])
                for i in range(4):
                    pe.wait_ge(pt_ready, 4 * t + i + 1)
                    for g in range(HG):
                        h = 4 * g + i
                        last = mm(bank(1, P, HD, h * HD), pt[:, i, g, :], v2[:, u, h * HD:(h + 1) * HD])
                last.then_inc(pv_done, 1)

            def out_transposed(t):
                pe.wait_ge(og_ready, t + 1)
                pe.wait_ge(xt_ready, N2 + min(t + 3, T))
                if t >= 1:
                    pe.wait_ge(attn_out, t)
                for c in range(2):
                    last = tr(bank(0, DH, P, c * P), og[:, t % 2, c * DH:(c + 1) * DH], ident)
                last.then_inc(ot_done, 1)

            def out_projected(t):
                pe.wait_ge(oT_ready, t + 1)
                for c in range(2):
                    last = mm(bank(0, P, D, 256), oT[0:DH, t % 2, c, :], wo[:, c, :], c == 0, c == 1)
                last.then_inc(wo_done, 1)

            pe.wait_ge(gates_init, 1)
            inputs(0)
            proj(0)
            inputs(1)
            tr2(0)
            gate_and_state(0)
            for t in range(T):
                if t >= 1:
                    out_transposed(t - 1)
                attend(t)
                if t >= 1:
                    out_projected(t - 1)
                if t + 1 < T:
                    proj(t + 1)
                if t + 2 < T:
                    inputs(t + 2)
                values(t)
                if t + 1 < T:
                    tr2(t + 1)
                    gate_and_state(t + 1)
            out_transposed(T - 1)
            out_projected(T - 1)
            pe.wait_ge(attn_out, T)
            route(1, 3 * T, 0, list(range(T)), wr, xn_last)
            mlp(1)

        @block.scalar
        def _(act):
            act.wait_ge(bn_var, 1)
            act.activation(inv, bn_t, ACT.Sqrt).then_inc(bn_root, 1)

            def softmax_exp(k):
                act.wait_ge(shift_ready, k + 1)
                act.activation(pr[:], lg[:], ACT.Exp).then_inc(exp_ready, 1)

            def mlp(k, fn):
                m = ffn[k]
                n, F, NH = ((NT0, F0, 2), (NT1, F1, 1))[k]
                W = F // NH

                def one(s, b, prior):
                    act.wait_ge(m["up"], s + 1)
                    if prior:
                        act.wait_ge(m["htr"], s - 1)
                    act.activation(hs[:, b, 0:F].rearrange("p (h n) -> p h n", h=NH),
                                   ps[:, 2 + 2 * b:2 + 2 * b + NH, 0:W], fn).then_inc(m["act"], 1)

                one(0, 0, False)
                one(1, 1, False)
                with act.Fori(0, (n - 3) // 2) as i:
                    for b in range(2):
                        one(2 * i + (2 + b), b, True)
                one(n - 1, 0, True)

            softmax_exp(0)
            mlp(0, ACT.Gelu)
            act.wait_ge(gates_init, 1)
            done = Count(act, act_done)
            act.wait_ge(lw_in, 96)
            act.wait_ge(cst_in, 16)
            for h in range(HEADS):
                done.did(act.activation(dec[:, (h % 4) * HG + h // 4, :], cst[:, C_DIFF:C_DIFF + P], ACT.Exp, scale=ls[:, h:h + 1]))
            done.did(act.activation(dkq[:, 0, :], ls[:], ACT.Exp, scale=cst[:, C_DK:C_DK + 1]))
            done.did(act.activation(dkq[:, 1, :], ls[:], ACT.Exp, scale=cst[:, C_DQ:C_DQ + 1]))
            for t in range(T):
                u = t % 2
                act.wait_ge(proj_done, t + 1)
                if t >= 2:
                    act.wait_ge(tr2_done, t - 1)
                    act.wait_ge(pv_done, t - 1)
                act.activation(qkp[:, u, :, :, 0:HD], ps[:, 2, 0:2 * D].rearrange("p (a h j) -> p a h j", a=2, h=HEADS),
                               ACT.Silu).then_inc(silu_ready, 1)
                act.activation(v2[:, u, 0:D], ps[:, 3, 0:D], ACT.Silu).then_inc(silu_ready, 1)
                act.activation(v2[:, u, D:D + 16], ps[:, 3, D:D + 16], ACT.Copy).then_inc(g1_ready, 1)
                act.wait_ge(tr2_done, t + 1)
                act.activation(qkT[:, u, 3:6].rearrange("p g n -> p (g n)"), bank(3, P, 3 * P), ACT.Copy
                               ).then_inc(kT_ready, 1)
                act.wait_ge(gate_done, t + 1)
                if t >= 2:
                    act.wait_ge(og_ready, t - 1)
                act.activation(gate[:, u, :], ps[:, 3, 0:D], ACT.Tanh, scale=0.5).then_inc(gate_ready, 1)
            softmax_exp(1)
            mlp(1, ACT.Silu)

        @block.vector
        def _(dve):
            v = nc.vector
            own = Count(dve, dve_done)
            did_, settle = own.did, own.settle

            dve.wait_ge(cst_in, 16)
            v.tensor_copy(ident16[:], ident).then_inc(consts_ready, 1)
            v.tensor_copy(tri16[:], cst[:, C_TRI:C_TRI + P]).then_inc(consts_ready, 1)
            v.memset(ones[:], 1.0).then_inc(consts_ready, 1)
            v.memset(ones16[:], 1.0).then_inc(consts_ready, 1)
            did_(v.memset(xgT[DH:DH + 1, :, 0, :], 1.0))
            dve.wait_ge(bn_in, 80)
            W4 = 4 * D
            gamma, beta, mean, var, bias = (bn[:, i * W4:(i + 1) * W4] for i in range(5))
            did_(v.tensor_scalar(bn_t, var, LN_EPS, None, ALU.add))
            settle()
            v.tensor_copy(thr, bn_t).then_inc(bn_var, 1)
            dve.wait_ge(bn_root, 1)
            did_(v.reciprocal(inv, inv))
            settle()
            did_(v.tensor_tensor(bn_t, thr, inv, ALU.mult))
            settle()
            did_(v.tensor_tensor(bn_t, bn_t, inv, ALU.mult))
            settle()
            did_(v.tensor_scalar(bn_t, bn_t, -0.5, 1.5, ALU.mult, ALU.add))
            settle()
            did_(v.tensor_tensor(inv, inv, bn_t, ALU.mult))
            settle()
            did_(v.tensor_tensor(inv, inv, gamma, ALU.mult))
            did_(v.tensor_tensor(thr, mean, bias, ALU.subtract))
            settle()
            did_(v.tensor_tensor(thr, thr, inv, ALU.mult))
            settle()
            did_(v.tensor_tensor(thr, thr, beta, ALU.subtract))
            settle()
            did_(v.tensor_scalar(thr, thr, 2.0, None, ALU.add))
            dve.wait_ge(aw_in, 32)
            for c in range(2):
                part = wqkv[:, c * 3 * D:(c + 1) * 3 * D]
                v.tensor_tensor(part, part, inv[0:DH, 0:3 * D], ALU.mult).then_inc(bnw_ready, 1)
            w3v = w3.rearrange("p (c n) -> p c n", c=2)
            w3rv = w3r.rearrange("p (c n) -> p c n", c=2)
            did_(v.tensor_tensor(w3rv, w3v, spread(inv[0:DH, 3 * D:4 * D], 1, [DH, 2, D]), ALU.mult))
            settle()
            did_(v.tensor_copy(w3s[:, 0], w3rv))
            settle()
            did_(v.tensor_tensor(w3rv, w3rv, w3s[:, 0], ALU.subtract))
            settle()
            did_(v.tensor_copy(w3s[:, 1], w3rv))
            settle()
            did_(v.tensor_tensor(w3rv, w3rv, w3s[:, 1], ALU.subtract))
            settle()
            v.tensor_copy(w3s[:, 2], w3rv).then_inc(bnw_ready, 1)

            dve.wait_ge(pe_t, 1)
            v.tensor_copy(t2, bank(3, DH)).then_inc(dve_t, 1)
            dve.wait_ge(pe_t, 2)
            v.tensor_copy(t1, bank(2, DH)).then_inc(dve_t, 1)
            dve.wait_ge(tokw_in, 96)
            dve.wait_ge(pe_y, 1)
            N1 = IMAGES * L1
            v.tensor_scalar(y12t[:, 0:N1], bank(6, EMBED, N1), tb[:, 1:2], None, ALU.add).then_inc(dve_y, 1)
            v.tensor_scalar(y12t[:, N1:], bank(6, EMBED, IMAGES * L2, N1), tb[:, 2:3], None, ALU.add).then_inc(dve_y, 1)
            for b in range(IMAGES):
                bk = (7, 2, 3, 6)[b]
                dve.wait_ge(pe_z, b + 1)
                v.tensor_copy(zz[0:L1, b * D:(b + 1) * D], bank(bk, L1, D)).then_inc(dve_z, 1)
                v.tensor_copy(zz[L1:L1 + L2, b * D:(b + 1) * D], bank(bk, L2, D, D)).then_inc(dve_z, 1)

            def norm_stats(norm, src, t):
                did_(v.bn_stats(stats[:, t % 2, :], src))
                settle()
                did_(v.bn_aggr(mv[:, norm, t, :], stats[:, t % 2, :]))

            def norm_var(norm, lo, n=1):
                settle()
                v.tensor_scalar(var_eps[:, norm, lo:lo + n], mv[:, norm, lo:lo + n, 1], LN_EPS, None, ALU.add
                                ).then_inc(var_ready[norm], 1)

            def normalise(norm, t, at, dst=None, src=None, sig=None):
                dve.wait_ge(rstd_ready[norm], at)
                v.tensor_scalar(xn[:, t, :] if dst is None else dst, H[:, t, :] if src is None else src,
                                mv[:, norm, t, 0:1], rstd[:, norm, t:t + 1], ALU.subtract, ALU.mult
                                ).then_inc(xn_ready if sig is None else sig, 1)

            def xt_copy(t, n, bk):
                dve.wait_ge(pe_xt, n + 1)
                v.tensor_copy(xT[:, t, :, :], bank(bk, DH, 2 * P).rearrange("p (c n) -> p c n", c=2)
                              ).then_inc(xt_ready, 1)

            def spikes(t):
                dve.wait_ge(qkv_done, t + 1)
                bk = 2 + 2 * (t % 2)
                v.tensor_tensor(spk[:, t, :].rearrange("p (h n) -> p h n", h=2), ps[:, bk:bk + 2, 0:288],
                                thr[:, 0:3 * D].rearrange("p (h n) -> p h n", h=2), ALU.is_ge).then_inc(spk_ready, 1)

            def qT_copy(t):
                dve.wait_ge(qtr_done, t + 1)
                v.tensor_copy(qT16[:, t], ps[0:DH, 6, :].bitcast(BF16)[:, 0:2 * P].rearrange("p (c n) -> p c n", c=2)
                              ).then_inc(qT_ready, 1)

            for n in range(2):
                dve.wait_ge(pe_t, 3 + n)
                v.tensor_copy(t0[:, n * 512:(n + 1) * 512], bank(n, 48)).then_inc(dve_t, 1)
                dve.wait_ge(pe_y, 2 + n)
                v.tensor_scalar(y0t[:, n * 512:(n + 1) * 512], bank(4 + n, EMBED), tb[:, 0:1], None, ALU.add
                                ).then_inc(dve_y, 1)
                lo = n * HALF
                for b in range(2):
                    dve.wait_ge(pe_h, n * 2 + b + 1)
                    v.tensor_copy(H[:, lo + 2 * b:lo + 2 * b + 2, :].rearrange("p t n -> p (t n)"),
                                  bank(((4, 7), (3, 2))[n][b], P, 2 * D)).then_inc(dve_h, 1)
                    dve.wait_ge(dve_h, n * 2 + b + 1)
                    for t in (lo + 2 * b, lo + 2 * b + 1):
                        norm_stats(0, H[:, t, :], t)
                norm_var(0, lo, HALF)
                for t in range(lo, lo + HALF):
                    normalise(0, t, n + 1)
                xt_copy(lo, lo, 0)
                for t in range(lo, lo + HALF):
                    if t + 1 < lo + HALF:
                        xt_copy(t + 1, t + 1, (t + 1) % 2)
                    spikes(t)
                    if t > lo:
                        qT_copy(t - 1)
                qT_copy(lo + HALF - 1)

            for b in range(HALF):
                dve.wait_ge(kv_done, b // 2 + 1)
                v.tensor_tensor(kv16[:, b], bank(6 + b // 2, DH, 2 * DH, (b % 2) * 2 * DH).rearrange("p (c n) -> p c n", c=2),
                                spread(cst[0:DH, C_BD:C_BD + DH], 1, [DH, 2, DH]), ALU.mult).then_inc(kv_ready, 1)

            def spikes_out(b):
                dve.wait_ge(xa_done, b + 1)
                if b >= 2:
                    dve.wait_ge(y3_done, 2 * (b - 1))
                v.tensor_scalar(s16[:, b % 2].rearrange("p h c n -> p (h c n)"), bank(2 + b, DH),
                                float(HD) ** -0.125, 1.0, ALU.mult, ALU.is_ge).then_inc(s_ready, 1)

            def fire_tile(n):
                t = PAIRS[n]
                f = fire[:, (n % 2) * D:(n % 2 + 1) * D]
                dve.wait_ge(y3_done, n + 1)
                v.tensor_tensor(f, bank(6 + n % 2, P, D), thr[:, 3 * D:4 * D], ALU.is_ge).then_inc(fired, 1)
                dve.wait_ge(fired, n + 1)
                v.tensor_tensor(H[:, t, :], H[:, t, :], f, ALU.add).then_inc(fire_done, 1)
                dve.wait_ge(fire_done, n + 1)
                norm_stats(1, H[:, t, :], t)
                norm_var(1, t)

            spikes_out(0)
            spikes_out(1)
            for n in range(T):
                fire_tile(n)
                if n % 2 == 1 and n // 2 + 2 < HALF:
                    spikes_out(n // 2 + 2)
                if n >= 1:
                    normalise(1, PAIRS[n - 1], n)
            normalise(1, PAIRS[T - 1], T)

            def argmax_first(src, oh, best):
                did_(v.tensor_reduce(best, src, AX, ALU.max))
                settle()
                did_(v.tensor_tensor(oh, src, spread(best, 2, [P, T, E]), ALU.is_ge))
                settle()
                did_(v.tensor_tensor(rt[:], oh, spread(cst[:, C_E8:C_E8 + E], 1, [P, T, E]), ALU.mult))
                settle()
                did_(v.tensor_reduce(sm[:, 0, :], rt[:], AX, ALU.min))
                settle()
                did_(v.tensor_tensor(oh, spread(cst[:, C_E8:C_E8 + E], 1, [P, T, E]), spread(sm[:, 0, :], 2, [P, T, E]),
                                     ALU.is_equal))
                settle()

            def route(k, n0, order):
                nt = (NT0, NT1)[k]
                for i, t in enumerate(order):
                    xt_copy(t, n0 + i, (n0 + i) % 2)
                dve.wait_ge(logit_done, k + 1)
                src = bank(2, P, T * E).rearrange("p (t e) -> p t e", t=T)
                if k == 0:
                    dve.wait_ge(rw_in, 48)
                    did_(v.tensor_tensor(lg[:], src, spread(bsr[:], 1, [P, T, E]), ALU.add))
                else:
                    did_(v.tensor_copy(lg[:], src))
                settle()
                did_(v.tensor_reduce(sm[:, 1, :], lg[:], AX, ALU.max))
                settle()
                v.tensor_tensor(lg[:], lg[:], spread(sm[:, 1, :], 2, [P, T, E]), ALU.subtract).then_inc(shift_ready, 1)
                dve.wait_ge(exp_ready, k + 1)
                did_(v.tensor_reduce(sm[:, 2, :], pr[:], AX, ALU.add))
                settle()
                did_(v.reciprocal(sm[:, 3, :], sm[:, 2, :]))
                settle()
                did_(v.tensor_tensor(pr[:], pr[:], spread(sm[:, 3, :], 2, [P, T, E]), ALU.mult))
                settle()
                argmax_first(pr[:], tops[0][:], pmax[:, 0, :])
                if k == 0:
                    v.tensor_copy(oh16[:], tops[0][:].rearrange("p t e -> p (t e)")).then_inc(oh_ready, 1)
                else:
                    did_(v.scalar_tensor_tensor(ohs[:], tops[0][:], -2.0, pr[:], ALU.mult, ALU.add))
                    settle()
                    argmax_first(ohs[:], tops[1][:], sm[:, 4, :])
                    v.tensor_tensor(oh16[:].rearrange("p (t e) -> p t e", t=T), tops[0][:], tops[1][:], ALU.add
                                    ).then_inc(oh_ready, 1)
                    v.tensor_reduce(rt[:, 0, :], pr[:].rearrange("p t e -> p e t"), AX, ALU.add).then_inc(imp_ready, 1)
                    dve.wait_ge(imp_done, 1)
                    did_(v.tensor_scalar(cnt[:, 0, :], bank(5, P, E), 1.0, 1.0 - 0.9, ALU.subtract, ALU.mult))
                    settle()
                    did_(v.tensor_scalar(cnt[:, 0, :], cnt[:, 0, :], 1.0, 0.01, ALU.add, ALU.add))
                    settle()
                    did_(v.reciprocal(cnt[:, 0, :], cnt[:, 0, :]))
                    settle()
                    did_(v.tensor_tensor(ohs[:], pr[:], spread(cnt[:, 0, :], 1, [P, T, E]), ALU.mult))
                    settle()
                    for j in range(2):
                        did_(v.tensor_tensor(rt[:], tops[j][:], ohs[:], ALU.mult))
                        settle()
                        did_(v.tensor_reduce(pmax[:, j, :], rt[:], AX, ALU.add))
                        settle()
                    did_(v.tensor_tensor(pmax[:, 2, :], pmax[:, 0, :], pmax[:, 1, :], ALU.add))
                    settle()
                    did_(v.reciprocal(pmax[:, 2, :], pmax[:, 2, :]))
                    settle()
                    for j in range(2):
                        did_(v.tensor_tensor(pmax[:, j, :], pmax[:, j, :], pmax[:, 2, :], ALU.mult))
                    settle()
                dve.wait_ge(rank_done, k + 1)
                did_(v.tensor_scalar(cnti[:], bank(4, P, E), float(P - 1), None, ALU.add))
                settle()
                did_(v.tensor_scalar(cnti[:], cnti[:], -P, None, ALU.bitwise_and))
                settle()
                did_(v.tensor_copy(cnt[:, 1, :], cnti[:]))
                settle()
                did_(v.tensor_tensor(cum[:], spread(cnt[:, 1, :], 1, [P, E, E]),
                                     cst[:, C_TRI8:C_TRI8 + E * E].rearrange("p (e f) -> p e f", e=E), ALU.mult))
                settle()
                did_(v.tensor_reduce(cnt[:, 2, :], cum[:], AX, ALU.add))
                settle()
                did_(v.tensor_tensor(cnt[:, 3, :], cnt[:, 2, :], cnt[:, 1, :], ALU.subtract))
                did_(v.tensor_tensor(jmap[:, 0:nt, :],
                                     cst[:, C_J128:C_J128 + nt * (E - 1)].rearrange("p (j e) -> p j e", j=nt),
                                     spread(cnt[:, 2, 0:E - 1], 1, [P, nt, E - 1]), ALU.is_ge))
                settle()
                did_(v.tensor_reduce(texp[:, 0:nt], jmap[:, 0:nt, :], AX, ALU.add))
                did_(v.tensor_tensor(lg[:], bank(3, P, T * E).rearrange("p (t e) -> p t e", t=T),
                                     spread(cnt[:, 3, :], 1, [P, T, E]), ALU.add))
                settle()
                did_(v.tensor_copy(texpi[k][:, 0:nt], texp[:, 0:nt]))
                K = k + 1
                for j in range(K):
                    did_(v.tensor_tensor(rt[:], lg[:], tops[j][:], ALU.mult))
                    settle()
                    did_(v.tensor_reduce(slot[:, 0, j * T:(j + 1) * T], rt[:], AX, ALU.add))
                    settle()
                n = K * T
                did_(v.tensor_copy(sloti[:, 0, 0:n], slot[:, 0, 0:n]))
                settle()
                did_(v.tensor_scalar(sloti[:, 1, 0:n], sloti[:, 0, 0:n], P - 1, None, ALU.bitwise_and))
                did_(v.tensor_scalar(sloti[:, 2, 0:n], sloti[:, 0, 0:n], 7, None, ALU.arith_shift_right))
                settle()
                did_(v.tensor_copy(slot[:, 1:3, 0:n], sloti[:, 1:3, 0:n]))
                settle()
                did_(v.tensor_tensor(AB[:, 0:n, 1, 0:nt], spread(cst[:, C_J:C_J + nt], 1, [P, n, nt]),
                                     spread(slot[:, 2, 0:n], 2, [P, n, nt]), ALU.is_equal))
                settle()
                did_(v.tensor_tensor(AB[:, 0:n, 0, 0:nt], AB[:, 0:n, 1, 0:nt],
                                     spread(cst[:, C_TOK:C_TOK + n], 2, [P, n, nt]), ALU.mult))
                settle()
                for i in range(n):
                    if i >= 2 or k == 1:
                        dve.wait_ge(inv_done, T * k + i - 1)
                    v.tensor_scalar(ohr[:, i % 2, :], cst[:, C_IOTA:C_IOTA + P], slot[:, 1, i:i + 1], None, ALU.is_equal
                                    ).then_inc(ohr_ready, 1)
                dve.wait_ge(inv_done, T * k + n)
                did_(v.tensor_copy(dmp[:, 0:2, 0:nt], bank(6, P, 2 * nt).rearrange("p (a j) -> p a j", a=2)))
                settle()
                did_(v.tensor_copy(gid[k][:, 0:nt], dmp[:, 0, 0:nt]))
                did_(v.tensor_scalar(dmp[:, 2, 0:nt], dmp[:, 1, 0:nt], -1.0, 1.0, ALU.mult, ALU.add))
                settle()
                did_(v.tensor_tensor(dmp[:, 2, 0:nt], dmp[:, 2, 0:nt], cst[:, C_ROW:C_ROW + nt], ALU.mult))
                settle()
                did_(v.tensor_tensor(did[k][:, 0:nt], dmp[:, 2, 0:nt], dmp[:, 0, 0:nt], ALU.add))
                settle()
                v.tensor_scalar(gid[k][:, 0:nt], gid[k][:, 0:nt], ROWS - 1, None, ALU.bitwise_and).then_inc(map_ready, 1)

            def mlp(k):
                m = ffn[k]
                n, F = ((NT0, F0), (NT1, F1))[k]
                C = F // P
                dve.wait_ge(map_ready, k + 1)
                if k == 0:
                    dve.wait_ge(wa_in, 16 * (2 * E + 2))

                def xt(s, b, prior):
                    dve.wait_ge(m["xt"], s + 1)
                    if prior:
                        dve.wait_ge(m["up"], s - 1)
                    v.tensor_copy(xgT[0:DH, b, :, :], bank(0, DH, 2 * P).rearrange("p (c n) -> p c n", c=2)
                                  ).then_inc(m["xgT"], 1)

                def ht(s, b, prior):
                    dve.wait_ge(m["htr"], s + 1)
                    if prior:
                        dve.wait_ge(m["down"], s - 1)
                    v.tensor_copy(hT[:, b, 0:C, :].rearrange("p c n -> p (c n)"),
                                  ps[:, 6:8, :].rearrange("p a n -> p (a n)")[:, 0:F]).then_inc(m["hT"], 1)

                def y(s, b, half, prior):
                    dve.wait_ge(m["down"], s + 1)
                    if prior:
                        dve.wait_ge(m[f"put{b}"], half * 16)
                    if k == 0:
                        e = dve.value_load(texpi[k][0:1, bass.ds(s, 1)], min_val=0, max_val=E - 1)
                        v.tensor_tensor(ys[:, b, :], bank(1, P, D), b2a[:, bass.ds(e * D, D)], ALU.add
                                        ).then_inc(m["y"], 1)
                    else:
                        v.tensor_copy(ys[:, b, :], bank(1, P, D)).then_inc(m["y"], 1)

                xt(0, 0, False)
                xt(1, 1, False)
                xt(2, 0, True)
                ht(0, 0, False)
                for s in range(2, XB):
                    xt(s + 1, (s + 1) % 2, True)
                    ht(s - 1, (s - 1) % 2, s > 2)
                    y(s - 2, s % 2, 0, False)
                with dve.Fori(0, (n - XB) // XB) as i:
                    for b in range(XB):
                        s = XB * i + (XB + b)
                        xt(s + 1, (b + 1) % 2, True)
                        ht(s - 1, (b + 1) % 2, True)
                        y(s - 2, b % 2, 2 * i + (XB + b - 2) // 2, True)
                for s in range(n // XB * XB, n + 2):
                    if s + 1 < n:
                        xt(s + 1, (s + 1) % 2, True)
                    if s <= n:
                        ht(s - 1, (s - 1) % 2, True)
                    y(s - 2, s % 2, (s - 2) // 2, True)

            route(0, T, PAIRS)
            mlp(0)

            v.memset(qkp.rearrange("p u a h j -> p (u a h j)"), 0.0).then_inc(gates_init, 1)

            def input_sum(t):
                dve.wait_ge(back[0][t], 16)
                did_(v.scalar_tensor_tensor(H[:, t, :], xn[:, t, :], pmax[:, 0, t:t + 1], H[:, t, :], ALU.mult, ALU.add))
                settle()
                norm_stats(2, H[:, t, :], t)
                norm_var(2, t)

            N2 = 2 * T

            def keys_decayed(t):
                dve.wait_ge(silu_ready, 2 * t + 2)
                if t >= 1:
                    dve.wait_ge(kvs_done, t)
                v.tensor_tensor(kd[:], qkp[:, t % 2, 1], spread(dkq[:, 0, :], 2, [P, HEADS, HPAD]), ALU.mult
                                ).then_inc(kd_ready, 1)

            def queries_copy(t):
                u = t % 2
                dve.wait_ge(tr2_done, t + 1)
                if t >= 2:
                    dve.wait_ge(pv_done, t - 1)
                did_(v.tensor_copy(g1T[0:16, u, :], bank(2, 16, P, 3 * P)))
                v.tensor_copy(qkT[:, u, 0:3].rearrange("p g n -> p (g n)"), bank(2, P, 3 * P)).then_inc(tr2_ready, 1)

            def state_copy(t):
                dve.wait_ge(kvs_done, t + 1)
                v.tensor_tensor(kvs[:, t], bank(2, P, D).rearrange("p (g n) -> p g n", g=HG),
                                spread(cst[:, C_BDP:C_BDP + 64], 1, [P, HG, 64]), ALU.mult).then_inc(kvs_ready, 1)

            def weigh(t):
                for i in range(4):
                    dve.wait_ge(sc_done, 4 * t + i + 1)
                    if i == 0 and t >= 1:
                        dve.wait_ge(pv_done, t)
                    v.tensor_tensor(pt[:, i], bank(4 + i, P, HG * P).rearrange("p (g n) -> p g n", g=HG),
                                    dec[:, i * HG:(i + 1) * HG, :], ALU.mult).then_inc(pt_ready, 1)

            def gated(t):
                u = t % 2
                dve.wait_ge(gate_ready, t + 1)
                did_(v.tensor_scalar(gate[:, u, :], gate[:, u, :], 1.0, 0.5, ALU.add, ALU.mult))
                dve.wait_ge(pv_done, t + 1)
                if t >= HALF:
                    did_(v.tensor_tensor(cross.rearrange("p (h j) -> p h j", h=HEADS),
                                         bank(1, P, D, 256).rearrange("p (h j) -> p h j", h=HEADS),
                                         spread(dkq[:, 1, :], 2, [P, HEADS, HD]), ALU.mult))
                    settle()
                    did_(v.tensor_tensor(cross, cross, bank(1, P, D), ALU.add))
                    settle()
                    v.tensor_tensor(og[:, u, :], cross, gate[:, u, :], ALU.mult).then_inc(og_ready, 1)
                else:
                    settle()
                    v.tensor_tensor(og[:, u, :], bank(1, P, D), gate[:, u, :], ALU.mult).then_inc(og_ready, 1)

            def out_copy(t):
                dve.wait_ge(ot_done, t + 1)
                v.tensor_copy(oT[0:DH, t % 2].rearrange("p c n -> p (c n)"), bank(0, DH, 2 * P)).then_inc(oT_ready, 1)

            def out_stats(t):
                dve.wait_ge(wo_done, t + 1)
                if t >= 2:
                    dve.wait_ge(res_ready, t - 1)
                v.tensor_copy(ao[:, t % 2, :], bank(0, P, D, 256)).then_inc(attn_out, 1)
                dve.wait_ge(attn_out, t + 1)
                norm_stats(3, ao[:, t % 2, :], t)
                norm_var(3, t)

            def out_norm(t):
                o = ao[:, t % 2, :]
                normalise(3, t, t + 1, o, o, ao_ready)

            def next_stats(t):
                dve.wait_ge(res_ready, t + 1)
                norm_stats(4, H[:, t, :], t)
                norm_var(4, t)

            for t in range(3):
                input_sum(t)
            for t in range(3):
                normalise(2, t, t + 1)
            dve.wait_ge(act_done, HEADS + 2)
            v.tensor_tensor(dec[:], dec[:], spread(cst[:, C_KEEP:C_KEEP + P], 1, [P, HEADS, P]), ALU.mult
                            ).then_inc(dec_ready, 1)
            xt_copy(0, N2, 0)
            xt_copy(1, N2 + 1, 0)
            keys_decayed(0)
            queries_copy(0)
            state_copy(0)
            dve.wait_ge(dec_ready, 1)
            for t in range(T):
                if t >= 1:
                    out_copy(t - 1)
                weigh(t)
                if t >= 1:
                    out_stats(t - 1)
                if t + 3 < T:
                    input_sum(t + 3)
                if t + 2 < T:
                    xt_copy(t + 2, N2 + t + 2, 0)
                if t >= 1:
                    out_norm(t - 1)
                if t + 3 < T:
                    normalise(2, t + 3, t + 4)
                if t + 1 < HALF:
                    keys_decayed(t + 1)
                gated(t)
                if t + 1 < T:
                    queries_copy(t + 1)
                if t >= 1:
                    next_stats(t - 1)
                if t + 1 < HALF:
                    state_copy(t + 1)
                if t >= 1:
                    normalise(4, t - 1, t, sig=xn_last)
            out_copy(T - 1)
            out_stats(T - 1)
            out_norm(T - 1)
            next_stats(T - 1)
            normalise(4, T - 1, T, sig=xn_last)

            route(1, 3 * T, list(range(T)))
            mlp(1)
            for t in range(T):
                dve.wait_ge(back[1][t], 32)
                did_(v.scalar_tensor_tensor(H[:, t, :], back1[:, 0, t, :], pmax[:, 0, t:t + 1], H[:, t, :],
                                            ALU.mult, ALU.add))
            settle()
            for t in range(T):
                v.scalar_tensor_tensor(H[:, t, :], back1[:, 1, t, :], pmax[:, 1, t:t + 1], H[:, t, :],
                                       ALU.mult, ALU.add).then_inc(final, 1)


def layouts(i):
    x = i["x"]
    c = np.ascontiguousarray

    def pixels(p):
        h = IMG // p
        t = x.reshape(IMAGES, CH, h, p, h, p).transpose(2, 4, 3, 5, 1, 0)
        return c(t.reshape(h * h, IMAGES * p * p * CH))

    def halves(w):
        return c(w.reshape(2, DH, -1).transpose(1, 0, 2))

    r = {"cst": constants(), "x0": pixels(1), "x1": pixels(2), "x2": pixels(4)}
    r["idx0"] = c(i["L0_tok_idx0"].reshape(2, P, GP).transpose(1, 0, 2).reshape(P, 2 * GP))
    r["idx1"] = c(i["L0_tok_idx1"].reshape(L1, 2, 8).transpose(1, 0, 2).reshape(P, 8))
    r["idx2"] = c(i["L0_tok_idx2"].reshape(L2, 8, 2).transpose(1, 0, 2).reshape(P, 2))
    r["w0t"] = c(i["L0_tok_W0"].T)
    r["w1t"] = c(i["L0_tok_W1"].T.reshape(2, DH, EMBED).transpose(1, 0, 2).reshape(DH, -1))
    r["w2t"] = c(i["L0_tok_W2"].T.reshape(8, DH, EMBED).transpose(1, 0, 2).reshape(DH, -1))
    r["tb"] = c(np.stack([i[f"L0_tok_b{k}"] for k in range(3)], 1))
    r["wft"] = c(i["L0_tok_Wf"].T.reshape(3, EMBED, D).transpose(1, 0, 2).reshape(EMBED, -1))
    r["bf"] = c(i["L0_tok_bf"].reshape(1, D))
    r["bn"] = c(np.stack([i[f"L0_attn_{n}"].reshape(-1) for n in ("bn_gamma", "bn_beta", "bn_mean", "bn_var", "b")]))
    w = i["L0_attn_W"]
    r["wqkv"] = halves(w[0:3].transpose(2, 0, 1).reshape(D, 3 * D))
    r["w3"] = halves(w[3].T)
    r["ws"] = halves(i["L0_ffn_Ws"])
    r["bs"] = c(i["L0_ffn_bs"])
    r["wr"] = halves(i["L1_ffn_router_w"].T)
    r["w1a"] = c(i["L0_ffn_W1"].reshape(E, 2, DH, F0).transpose(2, 1, 0, 3))
    r["b1a"] = c(i["L0_ffn_b1"].reshape(1, E, F0))
    r["w2a"] = c(i["L0_ffn_W2"].reshape(E, F0 // P, P, D).transpose(2, 0, 1, 3))
    r["b2a"] = c(i["L0_ffn_b2"].reshape(-1))
    r["w1b"] = c(i["L1_ffn_w1"].transpose(0, 2, 1).reshape(E, 2, DH, F1).transpose(2, 1, 0, 3))
    r["w2b"] = c(i["L1_ffn_w2"].transpose(0, 2, 1).reshape(E, F1 // P, P, D).transpose(2, 0, 1, 3))
    r["wqk2"] = halves(np.concatenate([i[f"L1_attn_{n}"] for n in ("Wq", "Wk", "Wv", "Wg1")], 1))
    r["wg2"] = c(i["L1_attn_Wg2"])
    r["wo"] = halves(i["L1_attn_Wo"])
    r["lnw"] = c(i["L1_attn_ln_w"])
    r["lnb"] = c(i["L1_attn_ln_b"])
    r["ls"] = c(i["L1_attn_log_slope"])
    return r


def kernel(**inputs):
    import concourse.bacc as bacc
    from concourse.bass_utils import run_bass_kernel_spmd

    nc = bacc.Bacc("TRN2", target_bir_lowering=False, num_devices=1)
    arrays = {f"in_{n}": v for n, v in layouts({n: np.asarray(v) for n, v in inputs.items()}).items()}
    aps = {n[3:]: nc.dram_tensor(n, v.shape, mybir.dt.from_np(v.dtype), kind="ExternalInput").ap()
           for n, v in arrays.items()}
    out = nc.dram_tensor("out_rows", (ROWS, D), F32, kind="ExternalOutput").ap()
    build(nc, aps, out)
    r = run_bass_kernel_spmd(nc, [arrays], core_ids=[0])
    return r.results[0]["out_rows"].reshape(IMAGES, TOKENS, D)
```

```python
from contextlib import ExitStack

import numpy as np

import concourse.bass as bass
from concourse import mybir

F32 = mybir.dt.float32
BF16 = mybir.dt.bfloat16
I32 = mybir.dt.int32
ALU = mybir.AluOpType
ACT = mybir.ActivationFunctionType
AX = mybir.AxisListType.X

P = 128
IMAGES = 4
IMG = 64
CH = 3
GP = 16
EMBED = 64
D = 192
DH = 96
TOKENS = 256
T = IMAGES * TOKENS // P
HALF = T // 2
HEADS = 12
HD = D // HEADS
HPAD = 32
HG = 3
E = 8
F0 = 768
F1 = 512
LN_EPS = 1e-5
L1 = TOKENS // 4
L2 = TOKENS // 16
NT0 = T + E - 1
NT1 = 2 * T + E - 1
ROWS = T * P
XB = 4
AHEAD = 6
WB = 4
SPACE = 7680
REGION = 7488
PARTS = [(0, (0, 1)), (0, (2, 3)), (1, (0, 1, 2, 3))]
PAIRS = [u for t in range(HALF) for u in (t, t + HALF)]

C_ID = 0
C_TRI = C_ID + P
C_DIFF = C_TRI + P
C_KEEP = C_DIFF + P
C_IOTA = C_KEEP + P
C_A = C_IOTA + P
C_BD = C_A + TOKENS
C_BDP = C_BD + DH
C_E8 = C_BDP + 64
C_TRI8 = C_E8 + E
C_J = C_TRI8 + 2 * E * E
C_J128 = C_J + NT1
C_TOK = C_J128 + NT1 * (E - 1)
C_ROW = C_TOK + 4 * T
C_DK = C_ROW + NT1
C_ZERO = C_DK + 1
C_END = C_ZERO + 1


def constants():
    c = np.zeros((P, C_END), np.float32)
    p = np.arange(P)
    c[:, C_ID:C_ID + P] = np.eye(P)
    c[:, C_TRI:C_TRI + P] = p[:, None] < p[None, :]
    c[:, C_DIFF:C_DIFF + P] = np.maximum(p[None, :] - p[:, None], 0)
    c[:, C_KEEP:C_KEEP + P] = p[None, :] >= p[:, None]
    c[:, C_IOTA:C_IOTA + P] = p[None, :]
    for at, n in ((0, L1), (L1, L2)):
        pos = np.clip((np.arange(TOKENS, dtype=np.float32) + 0.5) * (n / TOKENS) - 0.5, 0.0, n - 1)
        i0 = np.floor(pos).astype(np.int64)
        i1 = np.minimum(i0 + 1, n - 1)
        w = (pos - i0).astype(np.float32)
        np.add.at(c, (at + i0, C_A + np.arange(TOKENS)), 1.0 - w)
        np.add.at(c, (at + i1, C_A + np.arange(TOKENS)), w)
    c[L1 + L2, C_A:C_A + TOKENS] = 1.0
    q = np.arange(DH)
    c[:DH, C_BD:C_BD + DH] = q[:, None] // HD == q[None, :] // HD
    c[:, C_BDP:C_BDP + 64] = p[:, None] // HPAD == np.arange(64)[None, :] // HD
    c[:, C_E8:C_E8 + E] = np.arange(E) - E
    for k in range(2):
        c[:, C_TRI8 + k * E * E:C_TRI8 + (k + 1) * E * E] = np.tril(np.ones((E, E)), -k).reshape(1, -1)
    c[:, C_J:C_J + NT1] = np.arange(NT1) * P
    c[:, C_J128:C_J128 + NT1 * (E - 1)] = np.repeat(np.arange(NT1) * P, E - 1)
    t = np.arange(T)
    row = (t % HALF) * TOKENS + (t // HALF) * P
    for k in range(2):
        c[:, C_TOK + k * T:C_TOK + (k + 1) * T] = (k * ROWS + row[None, :]) // P
        c[:, C_TOK + (2 + k) * T:C_TOK + (3 + k) * T] = p[:, None]
    c[:, C_ROW:C_ROW + NT1] = 2 * ROWS + np.arange(NT1) * P + p[:, None]
    c[:, C_DK] = P - 1 - p
    return c


class Count:

    def __init__(self, engine, sem):
        self.engine, self.sem, self.n = engine, sem, 0

    def did(self, instruction):
        instruction.then_inc(self.sem, 1)
        self.n += 1
        return self.n

    def settle(self):
        self.engine.wait_ge(self.sem, self.n)


def spread(ap, axis, shape):
    return ap.unsqueeze(axis).to_broadcast(shape)


def build(nc, a, out):
    ctx = ExitStack()
    with ctx:
        def sb(name, shape, dt=F32):
            return ctx.enter_context(nc.sbuf_tensor(name, shape, dt))

        def sem(name):
            return ctx.enter_context(nc.semaphore(name))

        def dram(name, shape):
            return nc.dram_tensor(name, shape, F32, kind="Internal").ap()

        xn_rows = [dram(f"xn_rows{k}", (ROWS, D)) for k in range(2)]
        bn_rows = dram("bn_rows", (2, 4 * D))
        y_rows = [dram(f"y_rows{k}", (2 * ROWS + NT1 * P, D)) for k in range(2)]

        cst = sb("cst", [P, C_END])
        ones = sb("ones", [P, P])
        ones16 = sb("ones16", [P, P], BF16)
        ident16 = sb("ident16", [P, P], BF16)
        tri16 = sb("tri16", [P, P], BF16)
        H = sb("H", [P, T, D])
        xn = sb("xn", [P, T, D])
        xT = sb("xT", [DH, T, 2, P])
        NORMS = 5
        stats = sb("stats", [P, 2, 6])
        mv = sb("mv", [P, NORMS, T, 2])
        var_eps = sb("var_eps", [P, NORMS, T])
        rstd = sb("rstd", [P, NORMS, T])
        mhalf = sb("mhalf", [P, T])

        w1_space = sb("w1_space", [P, SPACE])
        w1buf = w1_space[0:DH + 1, 0:WB * 2 * F0].rearrange("p (b n) -> p b n", b=WB)
        w2a = sb("w2a", [P, E, F0 // P, D])
        b2a = sb("b2a", [P, E * D])
        w2b = sb("w2b", [P, E, F1 // P, D])
        region = sb("region", [P, REGION])
        taken = {"space": 0, "region": 0, "late1": 0, "late2": 0, "late3": 0}

        def place(where, buffer, rows, n):
            lo = taken[where]
            taken[where] += n
            assert taken[where] <= buffer.shape[1], where
            return buffer[0:rows, lo:lo + n]

        def first(rows, n):
            return place("space", w1_space, rows, n)

        def early(rows, n):
            return place("region", region, rows, n)

        idx0 = sb("idx0", [P, 2 * GP], I32)
        idx1 = sb("idx1", [P, 8], I32)
        idx2 = sb("idx2", [P, 2], I32)
        g0 = first(P, 2 * GP * 12)
        pg1 = first(P, 8 * 48)
        g2 = first(P, 2 * 192)
        t0 = first(48, 2 * 512)
        t1 = first(DH, 512)
        t2 = first(DH, 512)
        w0t = first(48, EMBED)
        w1t = first(DH, 2 * EMBED)
        w2t = first(DH, 8 * EMBED)
        tb = first(EMBED, 3)
        wft = first(EMBED, 3 * D)
        y0t = first(EMBED, 2 * 512)
        y12t = first(EMBED, IMAGES * (L1 + L2))
        zz = first(L1 + L2 + 1, IMAGES * D)
        BC = 4 * D // P
        bn = first(P, 5 * BC)
        bnf = first(P, 2 * BC)
        bnv = first(P, BC)
        inv = early(P, 4 * D)
        thr = early(P, 4 * D)
        bn_t = first(P, BC)
        wqkv = early(DH, 2 * 3 * D)
        w3 = first(DH, 2 * D)
        w3r = first(DH + 1, 2 * D)
        w3s = early(DH + 1, 3 * D).bitcast(BF16).rearrange("p (s c n) -> p s c n", s=3, c=2)
        spk = early(P, T * 3 * D // 2).bitcast(BF16).rearrange("p (t n) -> p t n", t=T)
        qT16 = early(DH, T * P).bitcast(BF16).rearrange("p (t c n) -> p t c n", t=T, c=2)
        kv16 = early(DH, HALF * DH).bitcast(BF16).rearrange("p (b c n) -> p b c n", b=HALF, c=2)
        s16 = early(DH + 1, 2 * 2 * P).bitcast(BF16).rearrange("p (u h c n) -> p u h c n", u=2, h=2, c=2)

        ws = sb("ws", [DH, 2, E])
        bsr = sb("bsr", [P, E])
        wr = sb("wr", [DH, 2, E])
        lg = sb("lg", [P, T, E])
        pr = sb("pr", [P, T, E])
        rt = sb("rt", [P, 2, T, E])
        tops = sb("tops", [P, 2, T, E])
        oh16 = sb("oh16", [P, T * E], BF16)
        ohs = sb("ohs", [P, T, E])
        sm = sb("sm", [P, 16, T])
        cnt = sb("cnt", [P, 4, E])
        cum = sb("cum", [P, 2, E, E])
        slot = sb("slot", [P, 3, 2 * T], I32)
        cnti = sb("cnti", [P, 2, E], I32)
        texp = sb("texp", [P, NT1])
        texpi = [sb(f"texpi{k}", [P, NT1], I32) for k in range(2)]
        dmp = sb("dmp", [P, 2, NT1])
        gid = [sb(f"gid{k}", [P, NT1], I32) for k in range(2)]
        did = [sb(f"did{k}", [P, NT1], I32) for k in range(2)]
        pmax = sb("pmax", [P, 3, T])

        xg = sb("xg", [P, XB, D])
        xgT = sb("xgT", [DH + 1, 2, 2, P])
        hT = sb("hT", [P, 2, F0 // P, P])
        ys = sb("ys", [P, 2, D])
        AB = hT[:, 0].rearrange("p c n -> p (c n)")[:, 0:2 * T * 3 * NT1 // 2].bitcast(BF16).rearrange("p (i a j) -> p i a j", i=2 * T, a=3)
        jmap = hT[:, 1].rearrange("p c n -> p (c n)")[:, 0:NT1 * (E - 1)].rearrange("p (j e) -> p j e", j=NT1)
        ohr = sb("ohr", [P, 2 * T, P], BF16)

        wqk2 = sb("wqk2", [DH, 2, 3 * D + 16])
        wg2 = sb("wg2", [16, HG * P])
        wo = sb("wo", [P, HG, D])
        lnw = sb("lnw", [P, 2, D])
        ls = sb("ls", [P, HEADS])
        lsT = sb("lsT", [P, HG])
        dk = sb("dk", [P, HEADS])
        silu_table = sb("silu_table", [P, 1])
        qk = w2a[:, :, :, :].rearrange("p e f d -> p (e f d)")

        def over1(n):
            return place("late1", w1_space, P, n)

        def over3(n):
            return place("late3", region, P, n)

        def over2(n):
            return place("late2", qk, P, n)

        qkp = over1(2 * 2 * HEADS * HPAD).rearrange("p (u a h j) -> p u a h j", u=2, a=2, h=HEADS)
        vp = over3(2 * HEADS * HPAD).rearrange("p (u h j) -> p u h j", u=2, h=HEADS)
        qTm = over3(2 * HG * 4 * P).rearrange("p (u g i n) -> p u g i n", u=2, g=HG, i=4)
        kvs = over3(HALF * HG * P).rearrange("p (b g i j) -> p b g i j", b=HALF, g=HG, i=4)
        dec = over3(HEADS * P).rearrange("p (g i n) -> p g i n", g=HG, i=4)
        decT = over3(HG * P)
        kT = over2(2 * HG * P).rearrange("p (u g n) -> p u g n", u=2, g=HG)
        qdT = over2(HG * P).rearrange("p (g n) -> p g n", g=HG)
        kd = over2(HEADS * HPAD).rearrange("p (h j) -> p h j", h=HEADS)
        g1 = over2(2 * 16).rearrange("p (u n) -> p u n", u=2)
        g1T = over2(2 * P).rearrange("p (u n) -> p u n", u=2)
        pt = over2(HEADS * P).rearrange("p (g i n) -> p g i n", g=HG, i=4)
        gate = over2(2 * HG * P).rearrange("p (u n) -> p u n", u=2)
        og = over2(2 * HG * P).rearrange("p (u n) -> p u n", u=2)
        ao = ys

        ps = ctx.enter_context(nc.psum_tensor("ps", [P, 8, 512], F32))

        def bank(i, rows=P, n=512, lo=0):
            return ps[0:rows, i, lo:lo + n]

        ident = cst[:, C_ID:C_ID + P]

        cst_in = sem("cst_in")
        tokw_in = sem("tokw_in")
        idx_in = sem("idx_in")
        g2_in = sem("g2_in")
        g1_in = sem("g1_in")
        g0_in = [sem(f"g0_in{n}") for n in range(2)]
        bn_in = sem("bn_in")
        aw_in = sem("aw_in")
        rw_in = sem("rw_in")
        lw_in = sem("lw_in")
        wa_in = sem("wa_in")
        wb_in = sem("wb_in")
        consts_ready = sem("consts_ready")
        mhalf_ready = sem("mhalf_ready")
        dve_done = sem("dve_done")
        act_done = sem("act_done")
        pe_t = sem("tok_transposed")
        dve_t = sem("tok_copied")
        pe_y = sem("tok_level_done")
        dve_y = sem("tok_level_copied")
        pe_z = sem("z_done")
        dve_z = sem("z_copied")
        pe_h = sem("h_done")
        dve_h = sem("h_copied")
        var_ready = [sem(f"var_ready{k}") for k in range(NORMS)]
        rstd_ready = [sem(f"rstd_ready{k}") for k in range(NORMS)]
        xn_ready = sem("xn_ready")
        xn_last = sem("xn_last")
        pe_xt = sem("xt_done")
        xt_ready = sem("xt_ready")
        pair_copied = sem("pair_copied")
        bnw_ready = sem("bnw_ready")
        bn_root = sem("bn_root")
        bn_var = sem("bn_var")
        qkv_done = sem("qkv_done")
        spk_ready = sem("spk_ready")
        qtr_done = sem("qtr_done")
        qT_ready = sem("qT_ready")
        kv_done = sem("kv_done")
        kv_ready = sem("kv_ready")
        xa_done = sem("xa_done")
        s_ready = sem("s_ready")
        y3_done = sem("y3_done")
        bn_folded = sem("bn_folded")
        bn_out = sem("bn_out")
        bn_back = sem("bn_back")
        fire_done = sem("fire_done")
        logit_done = sem("logit_done")
        shift_ready = sem("shift_ready")
        exp_ready = sem("exp_ready")
        oh_ready = sem("oh_ready")
        rank_done = sem("rank_done")
        imp_ready = sem("imp_ready")
        imp_done = sem("imp_done")
        ohr_ready = sem("ohr_ready")
        inv_done = sem("inv_done")
        texp_ready = sem("texp_ready")
        map_ready = sem("map_ready")
        xrow_out = sem("xrow_out")
        dec_ready = sem("dec_ready")
        proj_done = sem("proj_done")
        silu_ready = sem("silu_ready")
        g1_ready = sem("g1_ready")
        tr2_done = sem("tr2_done")
        qT_masked = sem("qT_masked")
        g1T_ready = sem("g1T_ready")
        batch_done = sem("batch_done")
        batch_copied = sem("batch_copied")
        qdT_ready = sem("qdT_ready")
        wo_halved = sem("wo_halved")
        gate_done = sem("gate_done")
        gate_ready = sem("gate_ready")
        kd_ready = sem("kd_ready")
        kvs_done = sem("kvs_done")
        kvs_ready = sem("kvs_ready")
        sc_done = sem("scores_done")
        pt_ready = sem("pt_ready")
        pv_done = sem("pv_done")
        og_ready = sem("og_ready")
        wo_done = sem("wo_done")
        attn_out = sem("attn_out")
        summed = sem("summed")
        final = sem("final")
        stored = sem("stored")
        stored2 = sem("stored2")
        gates_init = sem("gates_init")
        masks_init = sem("masks_init")
        res_ready = sem("res_ready")
        kT_ready = sem("kT_ready")
        ffn = []
        for k in range(2):
            ffn.append({n: sem(f"m{k}_{n}") for n in (
                "rows0", "rows1", "rows2", "rows3", "w0", "w1", "w2", "w3", "xt", "xgT", "up", "act",
                "down", "y",
                "put0", "put1")})
        back = [[sem(f"back{k}_{t}") for t in range(T)] for k in range(2)]
        back2 = [sem(f"second_back{t}") for t in range(T)]

        block = ctx.enter_context(nc.Block())

        back0 = xn[:, :, :].unsqueeze(1)
        back1 = qk[:, 0:2 * T * D].rearrange("p (k t d) -> p k t d", k=2, t=T)

        def both(ap, b):
            if len(ap.shape) == 2:
                return ap.rearrange("p (h b) -> p h b", b=HALF)[:, :, b]
            return ap.rearrange("p (h b) n -> p h b n", b=HALF)[:, :, b]

        def rows_of(dram_rows, t, choice=0):
            lo = choice * ROWS + (t % HALF) * TOKENS + (t // HALF) * P
            return dram_rows[lo:lo + P, :]

        def rows_of_two(dram_rows, t, choice=0):
            images = dram_rows[choice * ROWS:(choice + 1) * ROWS, :].rearrange("(b h r) d -> r h b d", b=IMAGES, h=2)
            return images[:, t // HALF, t % HALF:t % HALF + 2, :]

        @block.sync
        def _(sp):
            sp.dma_start(idx2[:], a["idx2"]).then_inc(idx_in, 16)
            sp.dma_start(idx1[:], a["idx1"]).then_inc(idx_in, 16)
            sp.dma_start(idx0[:], a["idx0"]).then_inc(idx_in, 16)
            sp.dma_start(cst[:], a["cst"]).then_inc(cst_in, 16)
            sp.dma_start(w0t, a["w0t"]).then_inc(tokw_in, 16)
            sp.dma_start(w1t, a["w1t"]).then_inc(tokw_in, 16)
            sp.dma_start(w2t, a["w2t"]).then_inc(tokw_in, 16)
            sp.dma_start(tb, a["tb"]).then_inc(tokw_in, 16)
            sp.dma_start(wft, a["wft"]).then_inc(tokw_in, 16)
            sp.dma_start(zz[L1 + L2:L1 + L2 + 1, :].rearrange("p (b n) -> p b n", b=IMAGES),
                         spread(a["bf"], 1, [1, IMAGES, D])).then_inc(tokw_in, 16)
            sp.dma_start(wqkv.rearrange("p (c n) -> p c n", c=2), a["wqkv"]).then_inc(aw_in, 16)
            sp.dma_start(w3.rearrange("p (c n) -> p c n", c=2), a["w3"]).then_inc(aw_in, 16)
            sp.dma_start(ws[:], a["ws"]).then_inc(rw_in, 16)
            sp.dma_start(wr[:], a["wr"]).then_inc(rw_in, 16)
            sp.dma_start(bsr[:], a["bs"].partition_broadcast(P)).then_inc(rw_in, 16)
            sp.wait_ge(g0_in[1], 16 * GP)
            for e in range(E):
                sp.dma_start(w2a[:, e, :, :], a["w2a"][:, e, :, :]).then_inc(wa_in, 16)
            for e in range(E):
                sp.dma_start(w2b[:, e, :, :], a["w2b"][:, e, :, :]).then_inc(wb_in, 16)
            sp.dma_start(b2a[:], a["b2a"].partition_broadcast(P)).then_inc(wa_in, 16)
            sp.dma_start(wqk2[:], a["wqk2"]).then_inc(lw_in, 16)
            sp.dma_start(wg2[:], a["wg2"]).then_inc(lw_in, 16)
            sp.dma_start(wo[:], a["wo"]).then_inc(lw_in, 16)
            sp.dma_start(lnw[:, 0, :], a["lnw"].partition_broadcast(P)).then_inc(lw_in, 16)
            sp.dma_start(lnw[:, 1, :], a["lnb"].partition_broadcast(P)).then_inc(lw_in, 16)
            sp.dma_start(ls[:], a["ls"].partition_broadcast(P)).then_inc(lw_in, 16)
            sp.dma_start(lsT[:], a["lsT"]).then_inc(lw_in, 16)

            for k, (ready, before) in enumerate(((xn_ready, T), (xn_last, 0))):
                m = ffn[k]
                for i, t in enumerate((PAIRS, range(T))[k]):
                    sp.wait_ge(ready, before + i + 1)
                    sp.dma_start(rows_of(xn_rows[k], t), xn[:, t, :]).then_inc(xrow_out, 16)
                sp.wait_ge(texp_ready, k + 1)
                n, F = ((NT0, F0), (NT1, F1))[k]
                rows = (DH + 1, DH)[k]

                def weights(s, b, used):
                    e = sp.value_load(texpi[k][0:1, bass.ds(s, 1)], min_val=0, max_val=E - 1)
                    if used is not None:
                        sp.wait_ge(m["up"], used)
                    sp.dma_start(w1buf[0:rows, b, 0:2 * F], a[("w1a", "w1b")[k]][bass.ds(e * rows, rows), :]
                                 ).then_inc(m[f"w{b}"], 16)

                weights(0, 0, None)
                sp.wait_ge(m["rows0"], 16)
                for s in range(1, WB):
                    weights(s, s, None)
                with sp.Fori(0, (n - WB) // WB) as i:
                    for b in range(WB):
                        weights(WB * i + (WB + b), b, WB * i + (b + 1))
                for s in range(n // WB * WB, n):
                    weights(s, s % WB, s - WB + 1)
                sp.wait_ge(m["put0"], 16 * ((n + 1) // 2))
                sp.wait_ge(m["put1"], 16 * (n // 2))
                dst = (back0, back1)[k]
                for t in range(0, T, 2):
                    if k == 0:
                        sp.dma_start(dst[:, 0, t, :], rows_of(y_rows[k], t)).then_inc(back[k][t], 16)
                    else:
                        sp.dma_start(dst[:, 0, t:t + 2, :], rows_of_two(y_rows[k], t)).then_inc(back[k][t], 16)
            for t in (0, 4):
                sp.wait_ge(final, t + 2)
                sp.dma_start(rows_of_two(out, t), H[:, t:t + 2, :]).then_inc(stored, 16)
            sp.wait_ge(final, T - 1)
            sp.dma_start(rows_of(out, T - 2), H[:, T - 2, :]).then_inc(stored, 16)
            sp.wait_ge(stored, 16 * 3)

        @block.gpsimd
        def _(pool):
            nc.gpsimd.memset(mhalf[:], -0.5).then_inc(mhalf_ready, 1)
            pool.wait_ge(idx_in, 48)
            for q in range(2):
                pool.indirect_dma_start(out=g2[:, q * 192:(q + 1) * 192], out_offset=None, in_=a["x2"],
                                        in_offset=bass.IndirectOffsetOnAxis(idx2[:, q:q + 1], 0)
                                        ).then_inc(g2_in, 16)
            for q in range(8):
                pool.indirect_dma_start(out=pg1[:, q * 48:(q + 1) * 48], out_offset=None, in_=a["x1"],
                                        in_offset=bass.IndirectOffsetOnAxis(idx1[:, q:q + 1], 0)
                                        ).then_inc(g1_in, 16)
            def root(norm, first, n, at):
                pool.wait_ge(var_ready[norm], at)
                nc.gpsimd.tensor_tensor(rstd[:, norm, first:first + n], var_eps[:, norm, first:first + n],
                                        mhalf[:, first:first + n], ALU.pow).then_inc(rstd_ready[norm], 1)

            pool.wait_ge(mhalf_ready, 1)
            for q in range(2 * GP):
                if q == 2 * GP - 7:
                    root(0, 0, 2, 1)
                if q == 2 * GP - 4:
                    root(0, 2, 2, 2)
                pool.indirect_dma_start(out=g0[:, q * 12:(q + 1) * 12], out_offset=None, in_=a["x0"],
                                        in_offset=bass.IndirectOffsetOnAxis(idx0[:, q:q + 1], 0)
                                        ).then_inc(g0_in[q // GP], 16)
            def mlp(k):
                m = ffn[k]
                n = (NT0, NT1)[k]
                pool.wait_ge(xrow_out, 16 * T * (k + 1))
                pool.wait_ge(map_ready, 2 * k + 1)
                for s in range(n + AHEAD):
                    if k == 0 and s == XB:
                        nc.gpsimd.memset(qTm.rearrange("p u g i n -> p (u g i n)"), 0.0).then_inc(masks_init, 1)
                    if s < n:
                        if s >= XB:
                            pool.wait_ge(m["xt"], s - XB + 1)
                        pool.indirect_dma_start(out=xg[:, s % XB, :], out_offset=None, in_=xn_rows[k],
                                                in_offset=bass.IndirectOffsetOnAxis(gid[k][:, s:s + 1], 0)
                                                ).then_inc(m[f"rows{s % XB}"], 16)
                    if s >= AHEAD:
                        j = s - AHEAD
                        if j == 0:
                            pool.wait_ge(map_ready, 2 * k + 2)
                        pool.wait_ge(m["y"], j + 1)
                        pool.indirect_dma_start(out=y_rows[k],
                                                out_offset=bass.IndirectOffsetOnAxis(did[k][:, j:j + 1], 0),
                                                in_=ys[:, j % 2, :], in_offset=None
                                                ).then_inc(m[f"put{j % 2}"], 16)

            root(0, 4, 2, 3)
            root(0, 6, 2, 4)
            for b in range(HALF):
                pool.wait_ge(var_ready[1], b + 1)
                nc.gpsimd.tensor_tensor(both(rstd[:, 1, :], b), both(var_eps[:, 1, :], b), mhalf[:, 0:2], ALU.pow
                                        ).then_inc(rstd_ready[1], 1)
            mlp(0)
            for t in range(3):
                root(2, t, 1, t + 1)
            def keys_decayed(t):
                pool.wait_ge(silu_ready, 2 * t + 2)
                if t >= 1:
                    pool.wait_ge(kvs_done, t)
                nc.gpsimd.tensor_tensor(kd[:], qkp[:, t % 2, 1], spread(dk[:], 2, [P, HEADS, HPAD]), ALU.mult
                                        ).then_inc(kd_ready, 1)

            pool.wait_ge(act_done, HEADS + HG + 1)
            keys_decayed(0)
            for t in range(T + 1):
                if t + 3 < T:
                    root(2, t + 3, 1, t + 4)
                if t + 1 < HALF:
                    keys_decayed(t + 1)
                if t >= 1:
                    root(3, t - 1, 1, t)
                if t < T:
                    pool.wait_ge(xn_ready, 2 * T + t + 1)
                    nc.gpsimd.tensor_tensor(H[:, t, :], H[:, t, :], lnw[:, 1, :], ALU.add).then_inc(res_ready, 1)
                if t >= 1:
                    root(4, t - 1, 1, t)
            mlp(1)

        @block.tensor
        def _(pe):
            def mm(o, l, r, start=True, stop=True):
                return nc.tensor.matmul(o, l, r, start=start, stop=stop)

            def tr(o, i, idn):
                return nc.tensor.transpose(o, i, idn)

            pe.wait_ge(cst_in, 16)
            pe.wait_ge(g2_in, 32)
            for b in range(IMAGES):
                last = tr(bank(3, DH, P, b * P), g2.rearrange("p (f b) -> p b f", b=IMAGES)[:, b], ident)
            last.then_inc(pe_t, 1)
            pe.wait_ge(g1_in, 16 * 8)
            for b in range(IMAGES):
                last = tr(bank(2, DH, P, b * P), pg1.rearrange("p (f b) -> p b f", b=IMAGES)[:, b], ident)
            last.then_inc(pe_t, 1)
            pe.wait_ge(tokw_in, 96)
            pe.wait_ge(dve_t, 1)
            for j in range(8):
                last = mm(bank(6, EMBED, IMAGES * L2, IMAGES * L1), w2t[:, j * EMBED:(j + 1) * EMBED],
                          t2.rearrange("p (b j n) -> p j b n", b=IMAGES, j=8)[:, j], j == 0, j == 7)
            pe.wait_ge(dve_t, 2)
            for j in range(2):
                last = mm(bank(6, EMBED, IMAGES * L1), w1t[:, j * EMBED:(j + 1) * EMBED],
                          t1.rearrange("p (b j n) -> p j b n", b=IMAGES, j=2)[:, j], j == 0, j == 1)
            last.then_inc(pe_y, 1)
            pe.wait_ge(dve_y, 2)
            for b in range(IMAGES):
                bk = (7, 2, 3, 6)[b]
                mm(bank(bk, L1, D), y12t[:, b * L1:(b + 1) * L1], wft[:, D:2 * D])
                mm(bank(bk, L2, D, D), y12t[:, IMAGES * L1 + b * L2:IMAGES * L1 + (b + 1) * L2],
                   wft[:, 2 * D:3 * D]).then_inc(pe_z, 1)

            def keep_warm(n, bk):
                for _ in range(n):
                    mm(bank(bk), ident, cst[:, 0:512])

            def level0_transposed(part, bk):
                n, images = PARTS[part]
                pe.wait_ge(g0_in[n], 16 * GP)
                for b in images:
                    last = tr(bank(bk, 48, P, b * P),
                              g0.rearrange("p (n f b) -> p n b f", n=2, b=IMAGES)[:, n, b], ident)
                last.then_inc(pe_t, 1)

            def level0_tokens(part, bk):
                n, images = PARTS[part]
                lo, size = images[0] * P, len(images) * P
                pe.wait_ge(dve_t, 3 + part)
                mm(bank(bk, EMBED, size, lo), w0t, t0[:, n * 512 + lo:n * 512 + lo + size]).then_inc(pe_y, 1)

            def fused(n, b, bk, part):
                pe.wait_ge(dve_y, 3 + part)
                pe.wait_ge(dve_z, 2 * IMAGES)
                for i in (b, b + 1):
                    o = bank(bk, P, D, (i - b) * D)
                    mm(o, y0t[:, n * 512 + i * P:n * 512 + (i + 1) * P], wft[:, 0:D], True, False)
                    last = mm(o, cst[0:L1 + L2 + 1, C_A + n * P:C_A + (n + 1) * P], zz[:, i * D:(i + 1) * D],
                              False, True)
                last.then_inc(pe_h, 1)

            def xtr(t, n, at, ready=xn_ready):
                pe.wait_ge(ready, at + 1)
                if n >= 2:
                    pe.wait_ge(xt_ready, n - 1)
                tr(bank(n % 2, DH, P), xn[:, t, 0:DH], ident)
                tr(bank(n % 2, DH, P, P), xn[:, t, DH:D], ident).then_inc(pe_xt, 1)

            def qkv(t):
                pe.wait_ge(xt_ready, t + 1)
                if t >= 2:
                    pe.wait_ge(spk_ready, t - 1)
                for h in range(2):
                    for c in range(2):
                        last = mm(bank(2 + 2 * (t % 2) + h, P, 288), xT[:, t, c, :],
                                  wqkv[:, c * 3 * D + h * 288:c * 3 * D + (h + 1) * 288], c == 0, c == 1)
                last.then_inc(qkv_done, 1)

            b6 = ps[:, 6, :].bitcast(BF16)

            def qtr(t):
                pe.wait_ge(spk_ready, t + 1)
                if t >= 1:
                    pe.wait_ge(qT_ready, t)
                for c in range(2):
                    last = tr(b6[0:DH, c * P:(c + 1) * P], spk[:, t, c * DH:(c + 1) * DH], ident16[:])
                last.then_inc(qtr_done, 1)

            level0_transposed(0, 0)
            level0_transposed(1, 1)
            level0_tokens(0, 4)
            level0_tokens(1, 2)
            fused(0, 0, 5, 0)
            fused(0, 2, 7, 1)
            pe.wait_ge(consts_ready, 4)
            pe.wait_ge(bnw_ready, 3)
            xtr(0, 0, 0)
            pe.wait_ge(dve_h, 2)
            xtr(1, 1, 1)
            qkv(0)
            xtr(2, 2, 2)
            qkv(1)
            level0_transposed(2, 7)
            qtr(0)
            xtr(3, 3, 3)
            level0_tokens(2, 7)
            qkv(2)
            qtr(1)
            fused(1, 0, 7, 2)
            qkv(3)
            qtr(2)
            pe.wait_ge(dve_h, 3)
            fused(1, 2, 7, 2)
            qtr(3)
            def kv(b):
                pe.wait_ge(spk_ready, b + HALF + 1)
                if b >= 1:
                    pe.wait_ge(kv_ready, b)
                for c in range(2):
                    for t in (b, b + HALF):
                        last = mm(bank(7, DH, DH, c * DH), spk[:, t, D + c * DH:D + (c + 1) * DH],
                                  spk[:, t, 2 * D + c * DH:2 * D + (c + 1) * DH], t == b, t != b)
                last.then_inc(kv_done, 1)

            def xa(b):
                pe.wait_ge(kv_ready, b + 1)
                pe.wait_ge(spk_ready, T - 1 if b < 2 else T)
                for h in range(2):
                    for c in range(2):
                        last = mm(bank(2 + b, DH, P, (h * 2 + c) * P), kv16[:, b, c, :], qT16[:, b + h * HALF, c, :])
                last.then_inc(xa_done, 1)

            pe.wait_ge(dve_h, 4)
            xtr(4, 4, 4)
            xtr(5, 5, 5)
            for t in range(HALF, T):
                qkv(t)
                if t > HALF:
                    qtr(t - 1)
                    kv(t - HALF - 1)
                if t + 2 < T:
                    xtr(t + 2, t + 2, t + 2)
            xa(0)
            xa(1)
            qtr(T - 1)
            kv(HALF - 1)

            def y3(b):
                pe.wait_ge(s_ready, b + 1)
                if b >= 2:
                    pe.wait_ge(fire_done, b - 1)
                for h in range(2):
                    for part in range(3):
                        for c in range(2):
                            r = DH + 1 - c
                            last = mm(bank(7 - b % 2, P, D, h * D), s16[0:r, b % 2, h, c, :], w3s[0:r, part, c, :],
                                      part == 0 and c == 0, part == 2 and c == 1)
                last.then_inc(y3_done, 1)

            def pair_transposed(b):
                pe.wait_ge(xn_ready, T + 2 * (b + 1))
                if b >= 2:
                    pe.wait_ge(pair_copied, b - 1)
                for h in range(2):
                    for c in range(2):
                        last = tr(bank(b % 2, DH, P, (2 * h + c) * P), xn[:, b + h * HALF, c * DH:(c + 1) * DH], ident)
                last.then_inc(pe_xt, 1)

            def pair_logits(b):
                pe.wait_ge(pair_copied, b + 1)
                for t in (b, b + HALF):
                    for c in range(2):
                        last = mm(bank(2, P, E, t * E), xT[:, t, c, :], ws[:, c, :], c == 0, c == 1)
                return last

            pe.wait_ge(rw_in, 48)
            pe.wait_ge(kv_ready, HALF)
            y3(0)
            xa(2)
            pe.wait_ge(qT_ready, T)
            y3(1)
            xa(3)
            pair_transposed(0)
            y3(2)
            pair_transposed(1)
            pair_logits(0)
            y3(3)
            pair_transposed(2)
            pair_logits(1)
            pair_transposed(3)
            pair_logits(2)
            pair_logits(3).then_inc(logit_done, 1)

            def route(k):
                pe.wait_ge(oh_ready, k + 1)
                for s in range(T):
                    last = mm(bank(3, P, (T - s) * E, s * E), tri16[:] if s == 0 else ones16[:],
                              oh16[:, 0:(T - s) * E], s == 0, s == T - 1)
                for t in range(T):
                    last = mm(bank(4, P, E), ones16[:], oh16[:, t * E:(t + 1) * E], t == 0, t == T - 1)
                last.then_inc(rank_done, 1)
                n = T * (k + 1)
                nt = (NT0, NT1)[k]
                for i in range(n):
                    if i % 4 == 0:
                        pe.wait_ge(ohr_ready, (2 * k) + i // 4 + 1)
                    last = mm(bank(6, P, 3 * nt), ohr[:, i, :], AB[:, i, :, 0:nt], i == 0, i == n - 1)
                last.then_inc(inv_done, 1)
                if k == 1:
                    pe.wait_ge(imp_ready, 1)
                    mm(bank(5, P, E), ones[:], rt[:, 0, 0, :]).then_inc(imp_done, 1)

            def mlp(k):
                m = ffn[k]
                n, F = ((NT0, F0), (NT1, F1))[k]
                w2, rows = ((w2a, DH + 1), (w2b, DH))[k]
                C = F // P
                NH = (2, 1)[k]

                def xt(s, b, quarter):
                    pe.wait_ge(m[f"rows{b}"], (quarter + 1) * 16)
                    for c in range(2):
                        last = tr(bank(6 * (b % 2), DH, P, c * P), xg[:, b, c * DH:(c + 1) * DH], ident)
                    last.then_inc(m["xt"], 1)

                def up(s, b, quarter, prior):
                    pe.wait_ge(m["xgT"], s + 1)
                    pe.wait_ge(m[f"w{b}"], (quarter + 1) * 16)
                    if prior:
                        pe.wait_ge(m["act"], s - 1)
                    for f in range(C):
                        for c in range(2):
                            r = rows if c == 0 else DH
                            last = mm(bank(2 + 2 * (b % 2) + f * NH // C, P, P, f % (C // NH) * P),
                                      w1buf[0:r, b, c * F + f * P:c * F + (f + 1) * P], xgT[0:r, b % 2, c, :],
                                      c == 0, c == 1)
                    last.then_inc(m["up"], 1)

                def down(s, b, prior):
                    e = pe.value_load(texpi[k][0:1, bass.ds(s, 1)], min_val=0, max_val=E - 1)
                    pe.wait_ge(m["act"], s + 1)
                    if prior:
                        pe.wait_ge(m["y"], s - 1)
                    flat = w2[:, :, :, :].rearrange("p e f d -> p (e f d)")
                    for c in range(C):
                        last = mm(bank((1, 7)[b % 2], P, D), hT[:, b % 2, c, :],
                                  flat[:, bass.ds(e * (C * D) + c * D, D)], c == 0, c == C - 1)
                    last.then_inc(m["down"], 1)

                keep_warm(2, 3)
                pe.wait_ge(texp_ready, k + 1)
                pe.wait_ge((wa_in, wb_in)[k], (16 * (E + 1), 16 * E)[k])
                xt(0, 0, 0)
                up(0, 0, 0, False)
                xt(1, 1, 0)
                for s in range(1, XB):
                    up(s, s, 0, s >= 2)
                    xt(s + 1, (s + 1) % XB, (s + 1) // XB)
                    down(s - 1, s - 1, s > 2)
                with pe.Fori(0, (n - XB) // XB) as i:
                    for b in range(XB):
                        s = XB * i + (XB + b)
                        up(s, b, i + 1, True)
                        xt(s + 1, (b + 1) % XB, i + (1 + (b + 1) // XB))
                        down(s - 1, (b + XB - 1) % XB, True)
                for s in range(n // XB * XB, n + 1):
                    if s < n:
                        up(s, s % XB, s // XB, True)
                    if s + 1 < n:
                        xt(s + 1, (s + 1) % XB, (s + 1) // XB)
                    down(s - 1, (s - 1) % XB, True)

            route(0)
            mlp(0)

            pe.wait_ge(lw_in, 112)

            def transposed(b):
                if b >= 1:
                    pe.wait_ge(batch_copied, b)
                if b < T:
                    pe.wait_ge(xn_ready, 2 * T + b + 1)
                    for c in range(2):
                        last = tr(bank(0, DH, P, c * P), xn[:, b, c * DH:(c + 1) * DH], ident)
                if b >= 4:
                    pe.wait_ge(xn_last, b - 3)
                    for c in range(2):
                        last = tr(bank(0, DH, P, (2 + c) * P), xn[:, b - 4, c * DH:(c + 1) * DH], ident)
                last.then_inc(batch_done, 1)

            def proj(t):
                pe.wait_ge(batch_copied, t + 1)
                if t >= 1:
                    pe.wait_ge(gate_ready, t)
                    if t <= HALF:
                        pe.wait_ge(kvs_ready, t)
                    else:
                        pe.wait_ge(qdT_ready, t - HALF)
                for bk, lo, hi in ((2, 0, 2 * D), (3, 2 * D, 3 * D + 16)):
                    for c in range(2):
                        last = mm(bank(bk, P, hi - lo), xT[:, t, c, :], wqk2[:, c, lo:hi], c == 0, c == 1)
                    last.then_inc(proj_done, 1)

            def heads_transposed(t):
                u = t % 2
                pe.wait_ge(silu_ready, 2 * (t + 1))
                pe.wait_ge(g1_ready, t + 1)
                tr(bank(2, 16, P, 3 * P), g1[:, u, :], ident)
                for g in range(HG):
                    tr(bank(2, P, P, g * P), qkp[:, u, 0, 4 * g:4 * g + 4, :], ident)
                for g in range(HG):
                    last = tr(bank(3, P, P, g * P), qkp[:, u, 1, 4 * g:4 * g + 4, :], ident)
                last.then_inc(tr2_done, 1)

            def gate_and_state(t):
                u = t % 2
                pe.wait_ge(qT_masked, t + 1)
                pe.wait_ge(g1T_ready, t + 1)
                if t < HALF:
                    pe.wait_ge(kd_ready, t + 1)
                    for g in range(HG):
                        last = mm(bank(2, P, 64, g * 64), kd[:, 4 * g:4 * g + 4, :], vp[:, u, 4 * g:4 * g + 4, 0:HD])
                    last.then_inc(kvs_done, 1)
                pe.wait_ge(kT_ready, t + 1)
                for g in range(HG):
                    last = mm(bank(3, P, P, g * P), wg2[:, g * P:(g + 1) * P], g1T[0:16, u, :])
                last.then_inc(gate_done, 1)

            def attend(t, groups):
                u = t % 2
                for g in groups:
                    if t >= 1:
                        pe.wait_ge(pt_ready, HG * (t - 1) + g + 1)
                    mm(bank(4 + g), kT[:, u, g, :], qTm[:, u, g]).then_inc(sc_done, 1)

            def values(t):
                u = t % 2
                if t >= 1:
                    pe.wait_ge(og_ready, t)
                if t >= HALF:
                    pe.wait_ge(kvs_ready, t - HALF + 1)
                    pe.wait_ge(qdT_ready, t - HALF + 1)
                for g in range(HG):
                    if t >= HALF:
                        mm(bank(1, P, P, g * P), kvs[:, t - HALF, g], qdT[:, g, :], True, False)
                    pe.wait_ge(pt_ready, HG * t + g + 1)
                    for i in range(4):
                        last = mm(ps[i * HPAD:(i + 1) * HPAD, 1, g * P:(g + 1) * P], vp[:, u, 4 * g + i, :],
                                  pt[:, g, i, :], t < HALF, True)
                last.then_inc(pv_done, 1)

            def logits(t):
                pe.wait_ge(batch_copied, t + 5)
                for c in range(2):
                    last = mm(bank(7, P, E, D + t * E), xT[:, t, c, :], wr[:, c, :], c == 0, c == 1)
                return last

            def out_projected(t):
                if t >= 1:
                    pe.wait_ge(attn_out, t)
                if t >= 2:
                    logits(t - 2)
                pe.wait_ge(og_ready, t + 1)
                for g in range(HG):
                    last = mm(bank(7, P, D), og[:, t % 2, g * P:(g + 1) * P], wo[:, g, :], g == 0, g == HG - 1)
                last.then_inc(wo_done, 1)

            keep_warm(11, 3)
            pe.wait_ge(gates_init, 1)
            transposed(0)
            proj(0)
            transposed(1)
            heads_transposed(0)
            gate_and_state(0)
            pe.wait_ge(wo_halved, 1)
            for t in range(T):
                attend(t, (0, 1))
                if t + 1 < T:
                    proj(t + 1)
                transposed(t + 2)
                if t + 1 < T:
                    heads_transposed(t + 1)
                attend(t, (2,))
                if t >= 1:
                    out_projected(t - 1)
                values(t)
                if t + 1 < T:
                    gate_and_state(t + 1)
            out_projected(T - 1)
            transposed(T + 2)
            pe.wait_ge(attn_out, T)
            logits(T - 2)
            transposed(T + 3)
            logits(T - 1).then_inc(logit_done, 1)
            route(1)
            mlp(1)

        @block.scalar
        def _(act):
            act.dma_start(bn, a["bn"]).then_inc(bn_in, 16)
            act.wait_ge(bn_var, 1)
            act.activation(bn_t, bnv, ACT.Sqrt).then_inc(bn_root, 1)
            act.wait_ge(bn_folded, 1)
            act.dma_start(bn_rows.rearrange("i (p n) -> p i n", p=P), bnf.rearrange("p (i n) -> p i n", i=2)
                          ).then_inc(bn_out, 16)
            act.wait_ge(bn_out, 16)
            act.dma_start(inv, bn_rows[0, :].partition_broadcast(P)).then_inc(bn_back, 16)
            act.dma_start(thr, bn_rows[1, :].partition_broadcast(P)).then_inc(bn_back, 16)

            for b in range(HALF):
                act.wait_ge(pe_xt, T + b + 1)
                act.activation(xT[:].rearrange("p (h b) c n -> p h b (c n)", b=HALF)[:, :, b],
                               bank(b % 2, DH).rearrange("p (h n) -> p h n", h=2), ACT.Copy).then_inc(pair_copied, 1)

            def softmax_exp(k):
                act.wait_ge(shift_ready, k + 1)
                act.activation(pr[:], lg[:], ACT.Exp).then_inc(exp_ready, 1)

            def mlp(k, fn):
                m = ffn[k]
                n, F, NH = ((NT0, F0, 2), (NT1, F1, 1))[k]
                W = F // NH

                def one(s, b, prior):
                    act.wait_ge(m["up"], s + 1)
                    if prior:
                        act.wait_ge(m["down"], s - 1)
                    act.activation(hT[:, b, 0:F // P, :].rearrange("p (h c) n -> p h (c n)", h=NH),
                                   ps[:, 2 + 2 * b:2 + 2 * b + NH, 0:W], fn).then_inc(m["act"], 1)

                one(0, 0, False)
                one(1, 1, False)
                with act.Fori(0, (n - 3) // 2) as i:
                    for b in range(2):
                        one(2 * i + (2 + b), b, True)
                one(n - 1, 0, True)

            def outputs_in(k):
                n = (NT0, NT1)[k]
                act.wait_ge(ffn[k]["put0"], 16 * ((n + 1) // 2))
                act.wait_ge(ffn[k]["put1"], 16 * (n // 2))

            softmax_exp(0)
            done = Count(act, act_done)
            act.wait_ge(lw_in, 112)
            act.wait_ge(cst_in, 16)
            for h in range(HEADS):
                done.did(act.activation(dec[:, h // 4, h % 4, :], cst[:, C_DIFF:C_DIFF + P], ACT.Exp, scale=ls[:, h:h + 1]))
            for g in range(HG):
                done.did(act.activation(decT[:, g * P:(g + 1) * P], cst[:, C_IOTA:C_IOTA + P], ACT.Exp,
                                        scale=lsT[:, g:g + 1], bias=lsT[:, g:g + 1]))
            done.did(act.activation(dk[:], ls[:], ACT.Exp, scale=cst[:, C_DK:C_DK + 1]))
            mlp(0, ACT.Gelu)
            act.wait_ge(lw_in, 112)
            act.activation(silu_table[:], ls[:, 0:1], ACT.Silu)
            outputs_in(0)
            for t in range(1, T, 2):
                act.dma_start(back0[:, 0, t, :], rows_of(y_rows[0], t)).then_inc(back[0][t], 16)
            act.wait_ge(masks_init, 1)
            act.wait_ge(gates_init, 1)
            for t in range(T):
                u = t % 2
                act.wait_ge(proj_done, 2 * t + 1)
                act.activation(qkp[:, u, :, :, 0:HD], ps[:, 2, 0:2 * D].rearrange("p (a h j) -> p a h j", a=2, h=HEADS),
                               ACT.Silu).then_inc(silu_ready, 1)
                act.wait_ge(proj_done, 2 * t + 2)
                if t >= 2:
                    act.wait_ge(pv_done, t - 1)
                act.activation(vp[:, u, :, 0:HD], ps[:, 3, 0:D].rearrange("p (h j) -> p h j", h=HEADS), ACT.Silu
                               ).then_inc(silu_ready, 1)
                act.activation(g1[:, u, :], ps[:, 3, D:D + 16], ACT.Copy).then_inc(g1_ready, 1)
                act.wait_ge(tr2_done, t + 1)
                act.activation(g1T[0:16, u, :], bank(2, 16, P, 3 * P), ACT.Copy).then_inc(g1T_ready, 1)
                for i in range(4):
                    rows = slice(i * HPAD, (i + 1) * HPAD)
                    part = act.activation(qTm[rows, u, :, i, :], ps[rows, 2, 0:HG * P].rearrange("p (g n) -> p g n", g=HG),
                                          ACT.Copy)
                part.then_inc(qT_masked, 1)
                act.activation(kT[:, u].rearrange("p g n -> p (g n)"), bank(3, P, HG * P), ACT.Copy).then_inc(kT_ready, 1)
                act.wait_ge(gate_done, t + 1)
                if t >= 2:
                    act.wait_ge(og_ready, t - 1)
                act.activation(gate[:, u, :], bank(3, P, HG * P), ACT.Tanh, scale=0.5).then_inc(gate_ready, 1)
            softmax_exp(1)
            mlp(1, ACT.Silu)
            outputs_in(1)
            for t in range(0, T, 2):
                act.dma_start(back1[:, 1, t:t + 2, :], rows_of_two(y_rows[1], t, 1)).then_inc(back2[t], 16)
            act.wait_ge(final, 4)
            act.dma_start(rows_of_two(out, 2), H[:, 2:4, :]).then_inc(stored2, 16)
            act.wait_ge(final, T)
            act.dma_start(rows_of(out, T - 1), H[:, T - 1, :]).then_inc(stored2, 16)
            act.wait_ge(stored2, 16 * 2)

        @block.vector
        def _(dve):
            v = nc.vector
            own = Count(dve, dve_done)
            did_, settle = own.did, own.settle

            dve.wait_ge(cst_in, 16)
            v.tensor_copy(ident16[:], ident).then_inc(consts_ready, 1)
            v.tensor_copy(tri16[:], cst[:, C_TRI:C_TRI + P]).then_inc(consts_ready, 1)
            v.memset(ones[:], 1.0).then_inc(consts_ready, 1)
            v.memset(ones16[:], 1.0).then_inc(consts_ready, 1)
            did_(v.memset(xgT[DH:DH + 1, :, 0, :], 1.0))
            dve.wait_ge(bn_in, 16)
            gamma, beta, mean, var, bias = (bn[:, i * BC:(i + 1) * BC] for i in range(5))
            cinv, cthr = bnf[:, 0:BC], bnf[:, BC:2 * BC]
            v.tensor_scalar(bnv, var, LN_EPS, None, ALU.add).then_inc(bn_var, 1)
            dve.wait_ge(bn_root, 1)
            did_(v.reciprocal(cinv, bn_t))
            settle()
            did_(v.tensor_tensor(bn_t, bnv, cinv, ALU.mult))
            settle()
            did_(v.tensor_tensor(bn_t, bn_t, cinv, ALU.mult))
            settle()
            did_(v.tensor_scalar(bn_t, bn_t, -0.5, 1.5, ALU.mult, ALU.add))
            settle()
            did_(v.tensor_tensor(cinv, cinv, bn_t, ALU.mult))
            settle()
            did_(v.tensor_tensor(cinv, cinv, gamma, ALU.mult))
            did_(v.tensor_tensor(cthr, mean, bias, ALU.subtract))
            settle()
            did_(v.tensor_tensor(cthr, cthr, cinv, ALU.mult))
            settle()
            did_(v.tensor_tensor(cthr, cthr, beta, ALU.subtract))
            settle()
            v.tensor_scalar(cthr, cthr, 2.0, None, ALU.add).then_inc(bn_folded, 1)

            dve.wait_ge(pe_t, 1)
            v.tensor_copy(t2, bank(3, DH)).then_inc(dve_t, 1)
            dve.wait_ge(pe_t, 2)
            v.tensor_copy(t1, bank(2, DH)).then_inc(dve_t, 1)
            dve.wait_ge(tokw_in, 96)
            dve.wait_ge(pe_y, 1)
            N1 = IMAGES * L1
            v.tensor_scalar(y12t[:, 0:N1], bank(6, EMBED, N1), tb[:, 1:2], None, ALU.add).then_inc(dve_y, 1)
            v.tensor_scalar(y12t[:, N1:], bank(6, EMBED, IMAGES * L2, N1), tb[:, 2:3], None, ALU.add).then_inc(dve_y, 1)
            for b in range(IMAGES):
                bk = (7, 2, 3, 6)[b]
                dve.wait_ge(pe_z, b + 1)
                v.tensor_copy(zz[0:L1, b * D:(b + 1) * D], bank(bk, L1, D)).then_inc(dve_z, 1)
                v.tensor_copy(zz[L1:L1 + L2, b * D:(b + 1) * D], bank(bk, L2, D, D)).then_inc(dve_z, 1)

            dve.wait_ge(aw_in, 32)
            dve.wait_ge(bn_back, 32)
            for c in range(2):
                part = wqkv[:, c * 3 * D:(c + 1) * 3 * D]
                v.tensor_tensor(part, part, inv[0:DH, 0:3 * D], ALU.mult).then_inc(bnw_ready, 1)
            w3v = w3.rearrange("p (c n) -> p c n", c=2)
            w3rv = w3r.rearrange("p (c n) -> p c n", c=2)
            did_(v.memset(w3rv[DH:DH + 1, 1, :], 0.0))
            did_(v.memset(s16[DH:DH + 1].rearrange("p u h c n -> p (u h c n)"), 1.0))
            did_(v.tensor_scalar(w3rv[DH:DH + 1, 0, :], thr[DH:DH + 1, 3 * D:4 * D], -1.0, None, ALU.mult))
            did_(v.tensor_tensor(w3rv[0:DH], w3v, spread(inv[0:DH, 3 * D:4 * D], 1, [DH, 2, D]), ALU.mult))
            settle()
            did_(v.tensor_copy(w3s[:, 0], w3rv))
            settle()
            did_(v.tensor_tensor(w3rv, w3rv, w3s[:, 0], ALU.subtract))
            settle()
            did_(v.tensor_copy(w3s[:, 1], w3rv))
            settle()
            did_(v.tensor_tensor(w3rv, w3rv, w3s[:, 1], ALU.subtract))
            settle()
            v.tensor_copy(w3s[:, 2], w3rv).then_inc(bnw_ready, 1)

            def norm_stats(norm, src, t):
                did_(v.bn_stats(stats[:, t % 2, :], src))
                settle()
                did_(v.bn_aggr(mv[:, norm, t, :], stats[:, t % 2, :]))

            def norm_var(norm, lo, n=1):
                settle()
                v.tensor_scalar(var_eps[:, norm, lo:lo + n], mv[:, norm, lo:lo + n, 1], LN_EPS, None, ALU.add
                                ).then_inc(var_ready[norm], 1)

            def normalise(norm, t, at, dst=None, src=None, sig=None):
                dve.wait_ge(rstd_ready[norm], at)
                v.tensor_scalar(xn[:, t, :] if dst is None else dst, H[:, t, :] if src is None else src,
                                mv[:, norm, t, 0:1], rstd[:, norm, t:t + 1], ALU.subtract, ALU.mult
                                ).then_inc(xn_ready if sig is None else sig, 1)

            def xt_copy(t, n, bk):
                dve.wait_ge(pe_xt, n + 1)
                v.tensor_copy(xT[:, t, :, :], bank(bk, DH, 2 * P).rearrange("p (c n) -> p c n", c=2)
                              ).then_inc(xt_ready, 1)

            def spikes(t):
                dve.wait_ge(qkv_done, t + 1)
                bk = 2 + 2 * (t % 2)
                v.tensor_tensor(spk[:, t, :].rearrange("p (h n) -> p h n", h=2), ps[:, bk:bk + 2, 0:288],
                                thr[:, 0:3 * D].rearrange("p (h n) -> p h n", h=2), ALU.is_ge).then_inc(spk_ready, 1)

            def qT_copy(t):
                dve.wait_ge(qtr_done, t + 1)
                v.tensor_copy(qT16[:, t], ps[0:DH, 6, :].bitcast(BF16)[:, 0:2 * P].rearrange("p (c n) -> p c n", c=2)
                              ).then_inc(qT_ready, 1)

            def level0_copy(part, bk):
                n, images = PARTS[part]
                lo, size = images[0] * P, len(images) * P
                dve.wait_ge(pe_t, 3 + part)
                v.tensor_copy(t0[:, n * 512 + lo:n * 512 + lo + size], bank(bk, 48, size, lo)).then_inc(dve_t, 1)

            def level0_bias(part, bk):
                n, images = PARTS[part]
                lo, size = images[0] * P, len(images) * P
                dve.wait_ge(pe_y, 2 + part)
                v.tensor_scalar(y0t[:, n * 512 + lo:n * 512 + lo + size], bank(bk, EMBED, size, lo), tb[:, 0:1], None,
                                ALU.add).then_inc(dve_y, 1)

            def fused_copy(n, b, bk):
                t = n * HALF + b
                dve.wait_ge(pe_h, t // 2 + 1)
                v.tensor_copy(H[:, t:t + 2, :].rearrange("p t n -> p (t n)"), bank(bk, P, 2 * D)).then_inc(dve_h, 1)
                dve.wait_ge(dve_h, t // 2 + 1)
                for u in range(2):
                    did_(v.bn_stats(stats[:, u, :], H[:, t + u, :]))
                settle()
                for u in range(2):
                    did_(v.bn_aggr(mv[:, 0, t + u, :], stats[:, u, :]))
                norm_var(0, t, 2)

            def norm0(t):
                normalise(0, t, t // 2 + 1)

            def xt0(t):
                xt_copy(t, t, t % 2)

            level0_copy(0, 0)
            level0_copy(1, 1)
            level0_bias(0, 4)
            level0_bias(1, 2)
            fused_copy(0, 0, 5)
            norm0(0)
            norm0(1)
            fused_copy(0, 2, 7)
            xt0(0)
            norm0(2)
            norm0(3)
            xt0(1)
            spikes(0)
            xt0(2)
            spikes(1)
            level0_copy(2, 7)
            qT_copy(0)
            xt0(3)
            level0_bias(2, 7)
            spikes(2)
            qT_copy(1)
            fused_copy(1, 0, 7)
            spikes(3)
            norm0(4)
            norm0(5)
            qT_copy(2)
            fused_copy(1, 2, 7)
            qT_copy(3)
            xt0(4)
            xt0(5)
            norm0(6)
            norm0(7)
            def kv_copy(b):
                dve.wait_ge(kv_done, b + 1)
                v.tensor_tensor(kv16[:, b], bank(7, DH, D).rearrange("p (c n) -> p c n", c=2),
                                spread(cst[0:DH, C_BD:C_BD + DH], 1, [DH, 2, DH]), ALU.mult).then_inc(kv_ready, 1)

            for t in range(HALF, T):
                spikes(t)
                if t > HALF:
                    qT_copy(t - 1)
                    kv_copy(t - HALF - 1)
                if t + 2 < T:
                    xt0(t + 2)

            def spikes_out(b):
                dve.wait_ge(xa_done, b + 1)
                if b >= 2:
                    dve.wait_ge(y3_done, b - 1)
                v.tensor_scalar(s16[0:DH, b % 2].rearrange("p h c n -> p (h c n)"), bank(2 + b, DH),
                                float(HD) ** -0.125, 1.0, ALU.mult, ALU.is_ge).then_inc(s_ready, 1)

            def fire(b):
                dve.wait_ge(y3_done, b + 1)
                v.scalar_tensor_tensor(both(H[:], b), bank(7 - b % 2, P, 2 * D).rearrange("p (h n) -> p h n", h=2),
                                       0.0, both(H[:], b), ALU.is_ge, ALU.add).then_inc(fire_done, 1)
                dve.wait_ge(fire_done, b + 1)
                for h in range(2):
                    did_(v.bn_stats(stats[:, h, :], H[:, b + h * HALF, :]))
                settle()
                for h in range(2):
                    did_(v.bn_aggr(mv[:, 1, b + h * HALF, :], stats[:, h, :]))
                settle()
                v.tensor_scalar(both(var_eps[:, 1, :], b), both(mv[:, 1], b)[:, :, 1], LN_EPS, None, ALU.add
                                ).then_inc(var_ready[1], 1)

            def norm_pair(b):
                for h in range(2):
                    normalise(1, b + h * HALF, b + 1)

            spikes_out(0)
            spikes_out(1)
            qT_copy(T - 1)
            kv_copy(HALF - 1)
            fire(0)
            spikes_out(2)
            norm_pair(0)
            fire(1)
            spikes_out(3)
            norm_pair(1)
            fire(2)
            norm_pair(2)
            fire(3)
            norm_pair(3)

            def argmax_first(src, oh, best):
                did_(v.tensor_tensor(oh, src, best, ALU.is_ge))
                settle()
                did_(v.tensor_tensor(rt[:, 0], oh, spread(cst[:, C_E8:C_E8 + E], 1, [P, T, E]), ALU.mult))
                settle()
                did_(v.tensor_reduce(sm[:, 0, :], rt[:, 0], AX, ALU.min))
                settle()
                did_(v.tensor_tensor(oh, spread(cst[:, C_E8:C_E8 + E], 1, [P, T, E]), spread(sm[:, 0, :], 2, [P, T, E]),
                                     ALU.is_equal))
                settle()

            def route(k):
                nt = (NT0, NT1)[k]
                K = k + 1
                n = K * T
                dve.wait_ge(logit_done, k + 1)
                src = (bank(2, P, T * E), bank(7, P, T * E, D))[k].rearrange("p (t e) -> p t e", t=T)
                if k == 0:
                    dve.wait_ge(rw_in, 48)
                    did_(v.tensor_tensor(lg[:], src, spread(bsr[:], 1, [P, T, E]), ALU.add))
                    settle()
                    src = lg[:]
                did_(v.tensor_reduce(sm[:, 1, :], src, AX, ALU.max))
                settle()
                argmax_first(src, tops[:, 0], spread(sm[:, 1, :], 2, [P, T, E]))
                if k == 0:
                    v.tensor_copy(oh16[:], tops[:, 0].rearrange("p t e -> p (t e)")).then_inc(oh_ready, 1)
                else:
                    did_(v.scalar_tensor_tensor(ohs[:], tops[:, 0], -3.0e38, src, ALU.mult, ALU.add))
                    settle()
                    did_(v.tensor_reduce(sm[:, 4, :], ohs[:], AX, ALU.max))
                    settle()
                    argmax_first(ohs[:], tops[:, 1], spread(sm[:, 4, :], 2, [P, T, E]))
                    v.tensor_tensor(oh16[:].rearrange("p (t e) -> p t e", t=T), tops[:, 0], tops[:, 1], ALU.add
                                    ).then_inc(oh_ready, 1)
                v.tensor_tensor(lg[:], src, spread(sm[:, 1, :], 2, [P, T, E]), ALU.subtract).then_inc(shift_ready, 1)
                dve.wait_ge(rank_done, k + 1)
                did_(v.tensor_scalar(cnti[:, 0, :], bank(4, P, E), float(P - 1), None, ALU.add))
                settle()
                did_(v.tensor_scalar(cnti[:, 1, :], cnti[:, 0, :], -P, None, ALU.bitwise_and))
                settle()
                did_(v.tensor_tensor(cum[:], cnti[:, 1, :].unsqueeze(1).unsqueeze(1).to_broadcast([P, 2, E, E]),
                                     cst[:, C_TRI8:C_TRI8 + 2 * E * E].rearrange("p (k e f) -> p k e f", k=2, e=E), ALU.mult))
                settle()
                did_(v.tensor_reduce(cnt[:, 2:4, :], cum[:], AX, ALU.add))
                settle()
                did_(v.tensor_tensor(ohs[:], bank(3, P, T * E).rearrange("p (t e) -> p t e", t=T),
                                     spread(cnt[:, 3, :], 1, [P, T, E]), ALU.add))
                settle()
                did_(v.tensor_tensor(rt[:, 0:K], spread(ohs[:], 1, [P, K, T, E]), tops[:, 0:K], ALU.mult))
                settle()
                with nc.allow_low_precision(reason="whole numbers, and one of the summands is not zero"):
                    did_(v.tensor_reduce(slot[:, 0, 0:n].rearrange("p (k t) -> p k t", k=K), rt[:, 0:K], AX, ALU.add))
                settle()
                did_(v.tensor_scalar(slot[:, 2, 0:n], slot[:, 0, 0:n], -P, None, ALU.bitwise_and))
                did_(v.tensor_scalar(slot[:, 1, 0:n], slot[:, 0, 0:n], P - 1, None, ALU.bitwise_and))
                settle()
                did_(v.tensor_tensor(AB[:, 0:n, 2, 0:nt], spread(cst[:, C_J:C_J + nt], 1, [P, n, nt]),
                                     spread(slot[:, 2, 0:n], 2, [P, n, nt]), ALU.is_equal))
                settle()
                did_(v.tensor_tensor(AB[:, 0:n, 0, 0:nt], AB[:, 0:n, 2, 0:nt],
                                     spread(cst[:, C_TOK:C_TOK + n], 2, [P, n, nt]), ALU.mult))
                did_(v.tensor_tensor(AB[:, 0:n, 1, 0:nt], AB[:, 0:n, 2, 0:nt],
                                     spread(cst[:, C_TOK + 2 * T:C_TOK + 2 * T + n], 2, [P, n, nt]), ALU.mult))
                settle()
                did_(v.tensor_tensor(jmap[:, 0:nt, :],
                                     cst[:, C_J128:C_J128 + nt * (E - 1)].rearrange("p (j e) -> p j e", j=nt),
                                     spread(cnt[:, 2, 0:E - 1], 1, [P, nt, E - 1]), ALU.is_ge))
                settle()
                did_(v.tensor_reduce(texp[:, 0:nt], jmap[:, 0:nt, :], AX, ALU.add))
                settle()
                v.tensor_copy(texpi[k][:, 0:nt], texp[:, 0:nt]).then_inc(texp_ready, 1)
                for i in range(0, n, 4):
                    v.tensor_tensor(ohr[:, i:i + 4, :], spread(cst[:, C_IOTA:C_IOTA + P], 1, [P, 4, P]),
                                    spread(slot[:, 1, i:i + 4], 2, [P, 4, P]), ALU.is_equal).then_inc(ohr_ready, 1)
                dve.wait_ge(inv_done, k + 1)
                high, low, taken_slot = (bank(6, P, nt, a * nt) for a in range(3))
                did_(v.tensor_copy(dmp[:, 0, 0:nt], low))
                settle()
                number = v.scalar_tensor_tensor(gid[k][:, 0:nt], high, float(P), dmp[:, 0, 0:nt], ALU.mult, ALU.add)
                if k == 0:
                    number.then_inc(map_ready, 1)
                else:
                    did_(number)
                    settle()
                    v.tensor_scalar(gid[k][:, 0:nt], gid[k][:, 0:nt], ROWS - 1, None, ALU.bitwise_and
                                    ).then_inc(map_ready, 1)
                did_(v.scalar_tensor_tensor(dmp[:, 0, 0:nt], high, float(P), dmp[:, 0, 0:nt], ALU.mult, ALU.add))
                did_(v.tensor_scalar(dmp[:, 1, 0:nt], taken_slot, -1.0, 1.0, ALU.mult, ALU.add))
                settle()
                did_(v.tensor_tensor(dmp[:, 1, 0:nt], dmp[:, 1, 0:nt], cst[:, C_ROW:C_ROW + nt], ALU.mult))
                settle()
                v.tensor_tensor(did[k][:, 0:nt], dmp[:, 1, 0:nt], dmp[:, 0, 0:nt], ALU.add).then_inc(map_ready, 1)

            def weights(k):
                K = k + 1
                dve.wait_ge(exp_ready, k + 1)
                did_(v.tensor_reduce(sm[:, 2, :], pr[:], AX, ALU.add))
                settle()
                did_(v.reciprocal(sm[:, 3, :], sm[:, 2, :]))
                settle()
                did_(v.tensor_tensor(pr[:], pr[:], spread(sm[:, 3, :], 2, [P, T, E]), ALU.mult))
                settle()
                if k == 1:
                    v.tensor_reduce(rt[:, 0, 0, :], pr[:].rearrange("p t e -> p e t"), AX, ALU.add).then_inc(imp_ready, 1)
                    dve.wait_ge(imp_done, 1)
                    did_(v.tensor_scalar(cnt[:, 0, :], bank(5, P, E), 1.0, 1.0 - 0.9, ALU.subtract, ALU.mult))
                    settle()
                    did_(v.tensor_scalar(cnt[:, 0, :], cnt[:, 0, :], 1.0, 0.01, ALU.add, ALU.add))
                    settle()
                    did_(v.reciprocal(cnt[:, 0, :], cnt[:, 0, :]))
                    settle()
                    did_(v.tensor_tensor(pr[:], pr[:], spread(cnt[:, 0, :], 1, [P, T, E]), ALU.mult))
                    settle()
                did_(v.tensor_tensor(rt[:, 0:K], tops[:, 0:K], spread(pr[:], 1, [P, K, T, E]), ALU.mult))
                settle()
                did_(v.tensor_reduce(pmax[:, 0:K, :], rt[:, 0:K], AX, ALU.add))
                settle()
                if k == 1:
                    did_(v.tensor_tensor(pmax[:, 2, :], pmax[:, 0, :], pmax[:, 1, :], ALU.add))
                    settle()
                    did_(v.reciprocal(pmax[:, 2, :], pmax[:, 2, :]))
                    settle()
                    did_(v.tensor_tensor(pmax[:, 0:2, :], pmax[:, 0:2, :], spread(pmax[:, 2, :], 1, [P, 2, T]), ALU.mult))
                    settle()

            def mlp(k):
                m = ffn[k]
                n, F = ((NT0, F0), (NT1, F1))[k]
                C = F // P
                if k == 0:
                    dve.wait_ge(wa_in, 16 * (E + 1))

                def xt(s, b, prior):
                    dve.wait_ge(m["xt"], s + 1)
                    if prior:
                        dve.wait_ge(m["up"], s - 1)
                    v.tensor_copy(xgT[0:DH, b, :, :], bank(6 * b, DH, 2 * P).rearrange("p (c n) -> p c n", c=2)
                                  ).then_inc(m["xgT"], 1)

                def y(s, b, half, prior):
                    dve.wait_ge(m["down"], s + 1)
                    if prior:
                        dve.wait_ge(m[f"put{b}"], half * 16)
                    if k == 0:
                        e = dve.value_load(texpi[k][0:1, bass.ds(s, 1)], min_val=0, max_val=E - 1)
                        v.tensor_tensor(ys[:, b, :], bank((1, 7)[b], P, D), b2a[:, bass.ds(e * D, D)], ALU.add
                                        ).then_inc(m["y"], 1)
                    else:
                        v.tensor_copy(ys[:, b, :], bank((1, 7)[b], P, D)).then_inc(m["y"], 1)

                xt(0, 0, False)
                xt(1, 1, False)
                for s in range(1, XB):
                    xt(s + 1, (s + 1) % 2, True)
                    y(s - 1, (s - 1) % 2, (s - 1) // 2, s > 2)
                with dve.Fori(0, (n - XB) // XB) as i:
                    for b in range(XB):
                        s = XB * i + (XB + b)
                        xt(s + 1, (b + 1) % 2, True)
                        y(s - 1, (b + 1) % 2, 2 * i + (XB + b - 1) // 2, True)
                for s in range(n // XB * XB, n + 1):
                    if s + 1 < n:
                        xt(s + 1, (s + 1) % 2, True)
                    y(s - 1, (s - 1) % 2, (s - 1) // 2, True)

            route(0)
            weights(0)
            v.memset(vp.rearrange("p u h j -> p (u h j)"), 0.0)
            v.memset(kvs.rearrange("p b g i j -> p (b g i j)"), 0.0)
            mlp(0)

            v.memset(qkp.rearrange("p u a h j -> p (u a h j)"), 0.0).then_inc(gates_init, 1)
            dve.wait_ge(act_done, HEADS + HG + 1)
            v.tensor_tensor(dec.rearrange("p g i n -> p (g i) n"), dec.rearrange("p g i n -> p (g i) n"),
                            spread(cst[:, C_KEEP:C_KEEP + P], 1, [P, HEADS, P]), ALU.mult).then_inc(dec_ready, 1)
            dve.wait_ge(lw_in, 112)
            v.tensor_scalar(wo[:], wo[:], 0.5, None, ALU.mult).then_inc(wo_halved, 1)

            def input_sum(t):
                dve.wait_ge(back[0][t], 16)
                did_(v.scalar_tensor_tensor(H[:, t, :], xn[:, t, :], pmax[:, 0, t:t + 1], H[:, t, :], ALU.mult, ALU.add))
                settle()
                norm_stats(2, H[:, t, :], t)
                norm_var(2, t)

            def queries_decayed(t):
                dve.wait_ge(qT_masked, t + 1)
                if t > HALF:
                    dve.wait_ge(pv_done, t)
                v.tensor_tensor(qdT.rearrange("p g n -> p (g n)"), bank(2, P, HG * P), decT, ALU.mult
                                ).then_inc(qdT_ready, 1)

            def state_copy(t):
                dve.wait_ge(kvs_done, t + 1)
                v.tensor_tensor(kvs[:, t, :, :, 0:HD], bank(2, P, D).rearrange("p (g i j) -> p g i j", g=HG, i=4),
                                spread(cst[:, C_BDP:C_BDP + 64].rearrange("p (i j) -> p i j", i=4), 1, [P, HG, 4, HD]),
                                ALU.mult).then_inc(kvs_ready, 1)

            def weigh(t, groups):
                for g in groups:
                    dve.wait_ge(sc_done, HG * t + g + 1)
                    if g == 0 and t >= 1:
                        dve.wait_ge(pv_done, t)
                    v.tensor_tensor(pt[:, g].rearrange("p i n -> p (i n)"), bank(4 + g),
                                    dec[:, g].rearrange("p i n -> p (i n)"), ALU.mult).then_inc(pt_ready, 1)

            def gated(t):
                u = t % 2
                dve.wait_ge(gate_ready, t + 1)
                dve.wait_ge(pv_done, t + 1)
                if t >= 2:
                    dve.wait_ge(wo_done, t - 1)
                v.scalar_tensor_tensor(og[:, u, :], gate[:, u, :], 1.0, bank(1, P, HG * P), ALU.add, ALU.mult
                                       ).then_inc(og_ready, 1)

            def batch_copy(b):
                dve.wait_ge(batch_done, b + 1)
                if b < T:
                    last = v.tensor_copy(xT[:, b].rearrange("p c n -> p (c n)"), bank(0, DH, 2 * P))
                if b >= 4:
                    last = v.tensor_copy(xT[:, b - 4].rearrange("p c n -> p (c n)"), bank(0, DH, 2 * P, 2 * P))
                last.then_inc(batch_copied, 1)

            def out_stats(t):
                dve.wait_ge(wo_done, t + 1)
                norm_stats(3, bank(7, P, D), t)
                norm_var(3, t)
                v.scalar_tensor_tensor(ao[:, t % 2, :], bank(7, P, D), mv[:, 3, t, 0:1], lnw[:, 0, :],
                                       ALU.subtract, ALU.mult).then_inc(attn_out, 1)

            def next_stats(t):
                dve.wait_ge(res_ready, t + 1)
                dve.wait_ge(attn_out, t + 1)
                dve.wait_ge(rstd_ready[3], t + 1)
                did_(v.scalar_tensor_tensor(H[:, t, :], ao[:, t % 2, :], rstd[:, 3, t:t + 1], H[:, t, :],
                                            ALU.mult, ALU.add))
                settle()
                norm_stats(4, H[:, t, :], t)
                norm_var(4, t)

            input_sum(0)
            input_sum(1)
            normalise(2, 0, 1)
            input_sum(2)
            batch_copy(0)
            normalise(2, 1, 2)
            normalise(2, 2, 3)
            batch_copy(1)
            state_copy(0)
            dve.wait_ge(dec_ready, 1)
            for t in range(T):
                weigh(t, (0, 1))
                batch_copy(t + 2)
                if t + 3 < T:
                    input_sum(t + 3)
                weigh(t, (2,))
                if t >= 1:
                    out_stats(t - 1)
                if t + 3 < T:
                    normalise(2, t + 3, t + 4)
                gated(t)
                if t >= 1:
                    next_stats(t - 1)
                if HALF <= t + 1 < T:
                    queries_decayed(t + 1)
                if t + 1 < HALF:
                    state_copy(t + 1)
                if t >= 1:
                    normalise(4, t - 1, t, sig=xn_last)
            out_stats(T - 1)
            batch_copy(T + 2)
            next_stats(T - 1)
            normalise(4, T - 1, T, sig=xn_last)
            batch_copy(T + 3)

            route(1)
            weights(1)
            mlp(1)
            for t in range(T + 1):
                if t < T:
                    dve.wait_ge(back[1][t - t % 2], 16)
                    v.scalar_tensor_tensor(H[:, t, :], back1[:, 0, t, :], pmax[:, 0, t:t + 1], H[:, t, :],
                                           ALU.mult, ALU.add).then_inc(summed, 1)
                if t >= 1:
                    u = t - 1
                    dve.wait_ge(summed, t)
                    dve.wait_ge(back2[u - u % 2], 16)
                    v.scalar_tensor_tensor(H[:, u, :], back1[:, 1, u, :], pmax[:, 1, u:u + 1], H[:, u, :],
                                           ALU.mult, ALU.add).then_inc(final, 1)


def layouts(i):
    x = i["x"]
    c = np.ascontiguousarray

    def pixels(p):
        h = IMG // p
        t = x.reshape(IMAGES, CH, h, p, h, p).transpose(2, 4, 3, 5, 1, 0)
        return c(t.reshape(h * h, IMAGES * p * p * CH))

    def halves(w):
        return c(w.reshape(2, DH, -1).transpose(1, 0, 2))

    r = {"cst": constants(), "x0": pixels(1), "x1": pixels(2), "x2": pixels(4)}
    r["idx0"] = c(i["L0_tok_idx0"].reshape(2, P, GP).transpose(1, 0, 2).reshape(P, 2 * GP))
    r["idx1"] = c(i["L0_tok_idx1"].reshape(L1, 2, 8).transpose(1, 0, 2).reshape(P, 8))
    r["idx2"] = c(i["L0_tok_idx2"].reshape(L2, 8, 2).transpose(1, 0, 2).reshape(P, 2))
    r["w0t"] = c(i["L0_tok_W0"].T)
    r["w1t"] = c(i["L0_tok_W1"].T.reshape(2, DH, EMBED).transpose(1, 0, 2).reshape(DH, -1))
    r["w2t"] = c(i["L0_tok_W2"].T.reshape(8, DH, EMBED).transpose(1, 0, 2).reshape(DH, -1))
    r["tb"] = c(np.stack([i[f"L0_tok_b{k}"] for k in range(3)], 1))
    r["wft"] = c(i["L0_tok_Wf"].T.reshape(3, EMBED, D).transpose(1, 0, 2).reshape(EMBED, -1))
    r["bf"] = c(i["L0_tok_bf"].reshape(1, D))
    r["bn"] = c(np.concatenate([i[f"L0_attn_{n}"].reshape(P, -1)
                                for n in ("bn_gamma", "bn_beta", "bn_mean", "bn_var", "b")], 1))
    w = i["L0_attn_W"]
    r["wqkv"] = halves(w[0:3].transpose(2, 0, 1).reshape(D, 3 * D))
    r["w3"] = halves(w[3].T)
    r["ws"] = halves(i["L0_ffn_Ws"])
    r["bs"] = c(i["L0_ffn_bs"])
    r["wr"] = halves(i["L1_ffn_router_w"].T)
    w = np.zeros((E, DH + 1, 2, F0), np.float32)
    w[:, 0:DH] = i["L0_ffn_W1"].reshape(E, 2, DH, F0).transpose(0, 2, 1, 3)
    w[:, DH, 0] = i["L0_ffn_b1"]
    r["w1a"] = w.reshape(E * (DH + 1), 2 * F0)
    r["w2a"] = c(i["L0_ffn_W2"].reshape(E, F0 // P, P, D).transpose(2, 0, 1, 3))
    r["b2a"] = c(i["L0_ffn_b2"].reshape(-1))
    r["w1b"] = c(i["L1_ffn_w1"].transpose(0, 2, 1).reshape(E, 2, DH, F1).transpose(0, 2, 1, 3).reshape(E * DH, 2 * F1))
    r["w2b"] = c(i["L1_ffn_w2"].transpose(0, 2, 1).reshape(E, F1 // P, P, D).transpose(2, 0, 1, 3))
    r["wqk2"] = halves(np.concatenate([i[f"L1_attn_{n}"] for n in ("Wq", "Wk", "Wv", "Wg1")], 1))

    def padded(w):
        z = np.zeros((HG, 4, HPAD, w.shape[1]), w.dtype)
        z[:, :, 0:HD] = w.reshape(HG, 4, HD, -1)
        return z.reshape(HG, P, -1)

    r["wg2"] = c(padded(i["L1_attn_Wg2"].T).transpose(2, 0, 1).reshape(16, HG * P))
    r["wo"] = c(padded(i["L1_attn_Wo"]).transpose(1, 0, 2))
    r["lsT"] = c(np.repeat(i["L1_attn_log_slope"].reshape(HG, 4), HPAD, 1).T)
    r["lnw"] = c(i["L1_attn_ln_w"])
    r["lnb"] = c(i["L1_attn_ln_b"])
    r["ls"] = c(i["L1_attn_log_slope"])
    return r


def kernel(**inputs):
    import concourse.bacc as bacc
    from concourse.bass_utils import run_bass_kernel_spmd

    nc = bacc.Bacc("TRN2", target_bir_lowering=False, num_devices=1)
    arrays = {f"in_{n}": v for n, v in layouts({n: np.asarray(v) for n, v in inputs.items()}).items()}
    aps = {n[3:]: nc.dram_tensor(n, v.shape, mybir.dt.from_np(v.dtype), kind="ExternalInput").ap()
           for n, v in arrays.items()}
    out = nc.dram_tensor("out_rows", (ROWS, D), F32, kind="ExternalOutput").ap()
    build(nc, aps, out)
    r = run_bass_kernel_spmd(nc, [arrays], core_ids=[0])
    return r.results[0]["out_rows"].reshape(IMAGES, TOKENS, D)
```
